# Optimizing a Trainium2 kernel written in Bass

```python
import numpy as np
import jax
import jax.numpy as jnp

def _softmax(x, axis=-1):
    return jax.nn.softmax(x, axis=axis)

def _gelu(x):
    return jax.nn.gelu(x, approximate=True)

def _silu(x):
    return jax.nn.silu(x)

def _sigmoid(x):
    return jax.nn.sigmoid(x)

def _layernorm(x, axis=-1, eps=1e-05):
    m = jnp.mean(x, axis=axis, keepdims=True)
    v = jnp.var(x, axis=axis, keepdims=True)
    return (x - m) / jnp.sqrt(v + eps)

def _scatter_add(tgt, idx, src, axis=0):
    return tgt.at[idx].add(src)

def _segment_sum(src, seg, n):
    return jax.ops.segment_sum(src, seg, n)
kernel_name = 'mk_decoder_postln_d1_seqx_r4_bcb17a'

def setup_inputs(seed: int=0):
    np.random.seed(seed)
    _w = jnp.asarray

    def _rec_inputs():
        import jax
        import jax.numpy as jnp
        _rk = jax.random.key(seed)
        x = -0.0005207 + 1.001 * jax.random.normal(jax.random.fold_in(_rk, 1), (64, 128, 256), jnp.float32)
        _lenS = 128 - jax.random.randint(jax.random.fold_in(_rk, 7), (64,), 0, max(1, 128 // 4) + 1, jnp.int32)
        _lenS2 = 128 - jax.random.randint(jax.random.fold_in(_rk, 8), (64,), 0, max(1, 128 // 4) + 1, jnp.int32)
        _ctx_512P = jax.random.normal(jax.random.fold_in(_rk, 11), (64, 16, 128), jnp.float32)
        _ctx_512c = jax.random.dirichlet(jax.random.fold_in(_rk, 511), 0.3 * jnp.ones((16,), jnp.float32), (64, 128))
        _ctx_512t = jnp.einsum('bsk,bkd->bsd', _ctx_512c, _ctx_512P)
        _ctx_512t = _ctx_512t * jax.lax.rsqrt(jnp.mean(jnp.square(_ctx_512t)) + 1e-12) * 0.953939
        ctx_512 = 0.502058 + 0.29099 * (_ctx_512t + 0.3 * jax.random.normal(jax.random.fold_in(_rk, 611), (64, 128, 128), jnp.float32))
        itok_BxS2xS_0_7 = jax.random.randint(jax.random.fold_in(_rk, 12), (64, 128, 128), 0, 8, jnp.int32)
        return (x, ctx_512, itok_BxS2xS_0_7)
    x, ctx_512, itok_BxS2xS_0_7 = _rec_inputs()

    def _L0_attn_setup():
        import jax, jax.numpy as jnp
        import numpy as np
        B, S, E, H = (2, 512, 256, 16)
        key = jax.random.key(seed)
        k1, k2 = jax.random.split(key)
        inputs = jax.random.normal(k1, (B, S, E), dtype=jnp.float32)
        qkv_kernel = jax.random.normal(k2, (E, 3 * E), dtype=jnp.float32) * (1.0 / np.sqrt(E))
        qkv_bias = jnp.zeros((1, 3 * E), dtype=jnp.float32)
        return {'inputs': inputs, 'qkv_kernel': qkv_kernel, 'qkv_bias': qkv_bias}
    _L0_attn_all = _L0_attn_setup()
    _L0_attn_in = {k: v for k, v in _L0_attn_all.items() if k in ('qkv_kernel', 'qkv_bias')}
    del _L0_attn_all

    def _L0_xattn_setup():
        import jax, jax.numpy as jnp
        import numpy as np
        key = jax.random.key(seed)
        k1, k2, k3, k4, k5 = jax.random.split(key, 5)
        B, K, S, E, I, D = (4, 2, 128, 8, 256, 512)
        x = jax.random.normal(k1, (B, S, I), dtype=jnp.float32)
        weights = jax.random.uniform(k2, (B, K, S), dtype=jnp.float32)
        ensembles = jax.random.randint(k3, (B, K, S), 0, E, dtype=jnp.int64)
        lim1 = float(np.sqrt(6.0 / (D + I)))
        proj_in = jax.random.uniform(k4, (E, D, I), dtype=jnp.float32, minval=-lim1, maxval=lim1)
        proj_out = jax.random.uniform(k5, (E, I, D), dtype=jnp.float32, minval=-lim1, maxval=lim1)
        return {'x': x, 'weights': weights, 'ensembles': ensembles, 'proj_in': proj_in, 'proj_out': proj_out}
    _L0_xattn_all = _L0_xattn_setup()
    _L0_xattn_in = {k: v for k, v in _L0_xattn_all.items() if k in ('proj_in', 'proj_out')}
    del _L0_xattn_all

    def _L0_ffn_setup():
        import jax, jax.numpy as jnp
        import numpy as np
        H = 256
        I = 1024
        E = 4
        LN_EPS = 1e-12

        def _layer_norm(x, gamma, beta, eps=LN_EPS):
            mu = jnp.mean(x, axis=-1, keepdims=True)
            var = jnp.mean(jnp.square(x - mu), axis=-1, keepdims=True)
            return (x - mu) * jax.lax.rsqrt(var + eps) * gamma + beta
        key = jax.random.key(seed)
        ks = jax.random.split(key, 8)
        B, S = (4, 128)
        scale = 0.02
        return {'hidden_states': jax.random.normal(ks[0], (B, S, H), jnp.float32), 'W_router': jax.random.normal(ks[1], (H, E), jnp.float32) * scale, 'W1': jax.random.normal(ks[2], (E, H, I), jnp.float32) * scale, 'b1': jax.random.normal(ks[3], (E, I), jnp.float32) * scale, 'Wo': jax.random.normal(ks[4], (I, H), jnp.float32) * scale, 'bo': jax.random.normal(ks[5], (H,), jnp.float32) * scale, 'ln_gamma': jnp.ones((H,), jnp.float32), 'ln_beta': jnp.zeros((H,), jnp.float32)}
    _L0_ffn_all = _L0_ffn_setup()
    _L0_ffn_in = {k: v for k, v in _L0_ffn_all.items() if k in ('W_router', 'W1', 'b1', 'Wo', 'bo', 'ln_gamma', 'ln_beta')}
    del _L0_ffn_all
    return {'x': x, 'ctx_512': ctx_512, 'itok_BxS2xS_0_7': itok_BxS2xS_0_7, 'L0_attn_qkv_kernel': _L0_attn_in['qkv_kernel'], 'L0_attn_qkv_bias': _L0_attn_in['qkv_bias'], 'L0_xattn_proj_in': _L0_xattn_in['proj_in'], 'L0_xattn_proj_out': _L0_xattn_in['proj_out'], 'L0_ffn_W_router': _L0_ffn_in['W_router'], 'L0_ffn_W1': _L0_ffn_in['W1'], 'L0_ffn_b1': _L0_ffn_in['b1'], 'L0_ffn_Wo': _L0_ffn_in['Wo'], 'L0_ffn_bo': _L0_ffn_in['bo'], 'L0_ffn_ln_gamma': _L0_ffn_in['ln_gamma'], 'L0_ffn_ln_beta': _L0_ffn_in['ln_beta']}

def reference(x, ctx_512, itok_BxS2xS_0_7, L0_attn_qkv_kernel, L0_attn_qkv_bias, L0_xattn_proj_in, L0_xattn_proj_out, L0_ffn_W_router, L0_ffn_W1, L0_ffn_b1, L0_ffn_Wo, L0_ffn_bo, L0_ffn_ln_gamma, L0_ffn_ln_beta):
    import jax
    import jax.numpy as jnp

    def _L0_attn_ref(inputs, qkv_kernel, qkv_bias):
        import jax, jax.numpy as jnp
        import numpy as np
        B, S, E, H = (2, 512, 256, 16)
        b, s, e = inputs.shape
        hidden, heads = (E, H)
        qkv = jnp.einsum('bse,ef->bsf', inputs, qkv_kernel) + qkv_bias
        qkv_heads = qkv.reshape(b, heads, s, -1)
        q, k, v = jnp.split(qkv_heads, 3, axis=-1)
        scale = 1.0 / np.sqrt(2.0 * hidden)
        qk = jnp.einsum('bhse,bhte->bhst', q, k) * scale
        mask = jnp.triu(jnp.full((s, s), -jnp.inf, dtype=jnp.float32), k=1)
        attn = jax.nn.softmax(qk + mask, axis=-1)
        out = jnp.einsum('bhst,bhte->bhse', attn, v).reshape(b, s, e)
        return out

    def _L0_xattn_ref(x, weights, ensembles, proj_in, proj_out):
        import jax, jax.numpy as jnp
        import numpy as np
        E = proj_in.shape[0]
        h = jax.nn.relu(jnp.einsum('edi,bsi->bsed', proj_in, x))
        o = jnp.einsum('eid,bsed->bsei', proj_out, h)
        onehot = jax.nn.one_hot(ensembles, E, dtype=x.dtype)
        gate = jnp.einsum('bks,bkse->bse', weights, onehot)
        return jnp.einsum('bsei,bse->bsi', o, gate)

    def _L0_ffn_ref(hidden_states, W_router, W1, b1, Wo, bo, ln_gamma, ln_beta):
        import jax, jax.numpy as jnp
        import numpy as np
        H = 256
        I = 1024
        E = 4
        LN_EPS = 1e-12

        def _layer_norm(x, gamma, beta, eps=LN_EPS):
            mu = jnp.mean(x, axis=-1, keepdims=True)
            var = jnp.mean(jnp.square(x - mu), axis=-1, keepdims=True)
            return (x - mu) * jax.lax.rsqrt(var + eps) * gamma + beta
        B, S, _ = hidden_states.shape
        x = hidden_states.reshape(-1, H)
        logits = x @ W_router
        expert_idx = jnp.argmax(logits, axis=-1)
        h = jnp.einsum('th,ehi->tei', x, W1) + b1
        h = jax.nn.gelu(h, approximate=False)
        onehot = jax.nn.one_hot(expert_idx, E, dtype=x.dtype)
        intermediate = jnp.einsum('te,tei->ti', onehot, h)
        y = intermediate @ Wo + bo + x
        y = _layer_norm(y, ln_gamma, ln_beta)
        return y.reshape(B, S, H)
    x = _layernorm(x + _L0_attn_ref(x, L0_attn_qkv_kernel, L0_attn_qkv_bias), axis=-1)
    x = _layernorm(x + _L0_xattn_ref(x, ctx_512, itok_BxS2xS_0_7, L0_xattn_proj_in, L0_xattn_proj_out), axis=-1)
    x = _layernorm(x + _L0_ffn_ref(x, L0_ffn_W_router, L0_ffn_W1, L0_ffn_b1, L0_ffn_Wo, L0_ffn_bo, L0_ffn_ln_gamma, L0_ffn_ln_beta), axis=-1)
    return x

_drawn_inputs = setup_inputs


def setup_inputs(seed=0):
    import zlib

    import numpy as np

    out = dict(_drawn_inputs(seed))
    spreads = {'L0_attn_qkv_bias': (0.0, 0.277),
     'L0_ffn_ln_gamma': (1.0, 0.2),
     'L0_ffn_ln_beta': (0.0, 0.1)}
    factors = {'L0_ffn_b1': 8.0, 'L0_ffn_bo': 5.395}
    for name, (base, spread) in spreads.items():
        noise = np.random.default_rng([zlib.crc32(name.encode()), seed]).standard_normal(out[name].shape)
        drawn = base * np.exp(spread * noise) if base else spread * noise
        out[name] = jnp.asarray(drawn.astype(out[name].dtype))
    for name, factor in factors.items():
        out[name] = (out[name] * factor).astype(out[name].dtype)
    return out
```

```python
from contextlib import ExitStack

import concourse.bass as bass
from concourse import mybir

F32 = mybir.dt.float32
F16 = mybir.dt.float16
BF16 = mybir.dt.bfloat16
I32 = mybir.dt.int32
ALU = mybir.AluOpType
ACT = mybir.ActivationFunctionType
AX = mybir.AxisListType

P = 128
D = 256
DK = D // P
HEADS = 16
HD = D // HEADS
QKV = 3 * D
TILES = 4
T = TILES * P
E1 = 8
I1 = 512
C1 = I1 // P
E2 = 4
I2 = 1024
C2 = I2 // P
SCORE_SCALE = (2.0 * D) ** -0.5
MASKED = -1.0e30

LAG = 5
SLOTS = E1 * C1 + LAG
POSITIONS = 2 * SLOTS
EVERY = 14
ATTENTION = [
    (0, "x_T", 0), (1, "qkv", 0), (2, "qkv", 1), (3, "shuffle", 0), (8, "split", 0),
    (12, "qk_T", 0), (13, "qk_T", 1), (15, "scores", 0), (16, "mask", 0), (16, "qk_T", 2),
    (17, "qk_T", 3), (18, "exp", 0), (19, "exp", 1), (19, "scores", 1), (20, "mask", 1),
    (21, "P_T", 0), (22, "P_T", 1), (22, "exp", 2), (23, "exp", 3), (24, "PV", 0),
    (25, "P_T", 2), (26, "P_T", 3), (28, "PV", 1), (29, "gather", 0),
]
TIMETABLE = {}
for _j in range(TILES):
    for _p, _name, _n in ATTENTION:
        TIMETABLE.setdefault(_p + EVERY * _j, []).append((_name, _j, _n))
assert max(TIMETABLE) < POSITIONS

USE = {}
for _p in sorted(TIMETABLE):
    for _name, _j, _n in TIMETABLE[_p]:
        if _name in ("x_T", "qkv", "qk_T", "P_T", "PV"):
            USE[_name, _j, _n] = len(USE)
for _key in (("ctx_T", 0, 0), ("tok_T", 0, 0), ("x1_T", 0, 0), ("x1_T", 0, 1)):
    USE[_key] = len(USE)
SMALL_USES = len(USE) // 2
assert len(USE) % 2 == 0

HID_XM = E1 * C1
HID_F = HID_XM + E2 * DK
HID_USES = (HID_F + C2) // 2
OUT_OH = E1 * TILES
OUT_Y = OUT_OH + 1
OUT_USES = [len([u for u in range(OUT_Y + TILES) if u % 2 == b]) for b in range(2)]

TAIL = {2: ("stats", 0), 4: ("stats", 1), 6: ("stats", 2), 8: ("stats", 3), 9: ("aggregate", 0),
        11: ("normal", 0), 16: ("stats2", 0), 17: ("stats2", 1), 19: ("stats2", 2),
        21: ("stats2", 3), 22: ("aggregate2", 0), 25: ("finish", 0), 26: ("store", 0)}
GATES_AT = 66

WCHUNK = 2048
WCHUNKS = ([("pin", n) for n in range(4)] + [("pout", n) for n in range(4)]
           + [("w1", n) for n in range(4)] + [("wo", 0)])
WNAMES = ["pin", "pout", "w1", "wo"]


def wait(eng, sem, value):
    if not (isinstance(value, int) and value <= 0):
        eng.wait_ge(sem, value)


def decoder_layer(nc, x, ctx, itok, w_qkv, b_qkv, p_in, p_out, w_router, w_1, b_1, w_o, b_o,
                  gamma, beta, out):
    B = x.shape[0]
    STEPS = B // TILES
    es = ExitStack()
    with es:
        def sb(name, shape, dt=F32):
            return es.enter_context(nc.sbuf_tensor(name, shape, dt))

        def ps(name, shape, dt=F32):
            return es.enter_context(nc.psum_tensor(name, shape, dt))

        def sem(name):
            return es.enter_context(nc.semaphore(name))

        qkv_dram = nc.dram_tensor("qkv_scratch", [TILES, P, QKV], F32, kind="Internal").ap()
        attn_dram = nc.dram_tensor("attn_scratch", [TILES, P, D], F32, kind="Internal").ap()

        pin = [sb(f"pin{k}", [P, DK, E1 * I1], F16) for k in "hl"]
        pout = [sb(f"pout{k}", [P, E1 * C1, D], F16) for k in "hl"]
        w1 = [sb(f"w1{k}", [P, E2 * DK, I2], F16) for k in "hl"]
        wo = [sb(f"wo{k}", [P, C2, D], F16) for k in "hl"]
        wqkv = sb("wqkv", [P, DK, QKV])
        b1p = sb("b1p", [P, I2], BF16)
        bqkv = sb("bqkv", [P, QKV])
        bo_r = sb("bo_r", [P, D])
        gamma_r = sb("gamma_r", [P, D])
        beta_r = sb("beta_r", [P, D])
        router_r = sb("router_r", [P, E2, D])
        ident = sb("ident", [P, P])
        ident16 = sb("ident16", [P, P], BF16)
        mask = sb("mask", [P, P])
        minus_half = sb("minus_half", [P, TILES])
        choice = sb("choice", [P, E2])
        tops = sb("tops", [P, len(WCHUNKS) + 1])
        top5 = sb("top5", [P, 8])
        top5a = sb("top5a", [P, 8])
        pow2 = sb("pow2", [P, 8])
        inv2 = sb("inv2", [P, 8])
        up = sb("up", [P, 8])
        down = sb("down", [P, 8])

        x_sb = sb("x_sb", [P, TILES, D])
        x1 = sb("x1", [P, TILES, D])
        x1T = [sb(f"x1T{k}", [P, DK, T], F16) for k in "hl"]
        acc = sb("acc", [P, TILES, D])
        hT = [sb(f"hT{k}", [P, 2, C1, T], F16) for k in "hl"]
        gT = [h[:, :, :, :].rearrange("p a c t -> p (a c) t") for h in hT]
        gate = sb("gate", [P, TILES, E1])
        yy = sb("yy", [P, TILES, D])
        x2b = sb("x2b", [P, TILES, D])
        attn = yy
        split_all = sb("split_all", [P, QKV + D])
        rest = split_all[:, 0:QKV].rearrange("p (h s e) -> p h s e", h=HEADS, s=3)
        xT = split_all[:, QKV:QKV + D].rearrange("p (k s) -> p k s", k=DK)
        g32 = split_all[:, :].rearrange("p (a t) -> p a t", a=2)
        oh12 = sb("oh12", [P, TILES, P], BF16)
        ohT = sb("ohT", [P, T], BF16)
        logit = sb("logit", [P, TILES, E2])
        logit_top = sb("logit_top", [P, TILES])
        is_top = sb("is_top", [P, TILES, E2])
        index = sb("index", [P, TILES, E2])
        index_min = sb("index_min", [P, TILES])
        onehot = sb("onehot", [P, TILES, E2])
        qk6_all = sb("qk6_all", [P, 2, 4096], BF16)
        qk6 = [qk6_all[:, b, 0:HEADS * 240].rearrange("p (h s e) -> p h s e", h=HEADS, e=HD) for b in range(2)]
        xmT = [qk6_all[:, b, :].bitcast(F16).rearrange("p (e k t) -> p e k t", e=E2, k=DK) for b in range(2)]
        prob = sb("prob", [P, 2, 8, P])
        xm = [prob[:, b, :, :].rearrange("p h t -> p (h t)").rearrange("p (j d) -> p j d", j=TILES) for b in range(2)]
        qkT = sb("qkT", [P, 2, 8, P], BF16)
        ctx_sb = qkT[:, 0, :, :].rearrange("p h t -> p (h t)").bitcast(F32).rearrange("p (j k) -> p j k", j=TILES)
        tok_sb = qkT[:, 1, :, :].rearrange("p h t -> p (h t)").bitcast(I32).rearrange("p (j k) -> p j k", j=TILES)
        tokf = qkT[:, 1, :, :].rearrange("p h t -> p (h t)").bitcast(F32).rearrange("p (j k) -> p j k", j=TILES)
        PT = [sb(f"PT{k}", [P, 2, 4, P], F16) for k in "hl"]
        qkv_tok = sb("qkv_tok", [P, QKV])
        qkv_h = sb("qkv_h", [P, HEADS, 3, HD])
        ctxT = qkv_tok[:, 0:T].rearrange("p (j k) -> p j k", j=TILES)
        tokT = qkv_h[:, :, :, :].rearrange("p h s e -> p (h s e)")[:, 0:T].rearrange("p (j k) -> p j k", j=TILES)
        neg_max = sb("neg_max", [P, 2, 8])
        row_sum = sb("row_sum", [P, 2, 8])
        row_inv = sb("row_inv", [P, 2, 8])
        pv = sb("pv", [P, 8, HD])
        attn_h = sb("attn_h", [P, HEADS, HD])
        junk = sb("junk", [P, 2, D])
        stats = {k: sb(f"stats_{k}", [P, TILES, 6]) for k in ("n1", "n2", "n3", "n4")}
        mv = {k: sb(f"mv_{k}", [P, TILES, 2]) for k in ("n1", "n2", "n3", "n4")}
        vare = {k: sb(f"vare_{k}", [P, TILES]) for k in ("n1", "n2", "n3", "n4")}
        rstd = {k: sb(f"rstd_{k}", [P, TILES]) for k in ("n1", "n2", "n3", "n4")}
        stage = [qk6_all[:, b, :].bitcast(F32) for b in range(2)]
        b1_sb = g32[0:E2, :, :].rearrange("p a t -> p (a t)")
        b1_all = hT[0][0:E2, :, :, :].rearrange("p a c t -> p (a c t)").bitcast(BF16)
        b1_h = [b1_all[:, n * I2:(n + 1) * I2] for n in range(3)]

        hid = [ps(f"hid{b}", [P, T]) for b in range(2)]
        outp = [ps(f"outp{b}", [P, T]) for b in range(2)]
        score = ps("score", [P, 8, P])
        small = [ps(f"small{b}", [P, T]) for b in range(2)]

        const_pool = sem("const_pool")
        consts_loaded = sem("consts_loaded")
        stage_loaded = [sem(f"stage_loaded{b}") for b in range(2)]
        tops_found = sem("tops_found")
        stage_hi = sem("stage_hi")
        stage_lo = sem("stage_lo")
        top_reduced = sem("top_reduced")
        scales = sem("scales")
        b1_steps = sem("b1_steps")
        b1_placed = sem("b1_placed")
        settled = sem("settled")
        x_loaded = sem("x_loaded")
        gates_loaded = sem("gates_loaded")
        small_ready = [sem(f"small_ready{b}") for b in range(2)]
        xT_copied = sem("xT_copied")
        qkv_biased = sem("qkv_biased")
        qkv_stored = sem("qkv_stored")
        qkv_reloaded = sem("qkv_reloaded")
        hi_written = sem("hi_written")
        rest_found = sem("rest_found")
        mid_written = sem("mid_written")
        lo_written = sem("lo_written")
        qkT_copied = sem("qkT_copied")
        scores_done = sem("scores_done")
        scores_masked = sem("scores_masked")
        max_found = sem("max_found")
        exps_done = sem("exps_done")
        sums_inverted = sem("sums_inverted")
        PT_hi = sem("PT_hi")
        PT_lo = sem("PT_lo")
        pv_summed = sem("pv_summed")
        attn_scaled = sem("attn_scaled")
        attn_stored = sem("attn_stored")
        attn_loaded = sem("attn_loaded")
        tok_cast = sem("tok_cast")
        gatesT = sem("gatesT")
        gate_summed = sem("gate_summed")
        gate_scaled = sem("gate_scaled")
        x1_sum = sem("x1_sum")
        x1_ready = sem("x1_ready")
        x1T_hi = sem("x1T_hi")
        x1T_lo = sem("x1T_lo")
        n_stats = {k: sem(f"n_stats_{k}") for k in ("n1", "n2", "n3", "n4")}
        n_aggr = {k: sem(f"n_aggr_{k}") for k in ("n1", "n2", "n3", "n4")}
        n_eps = {k: sem(f"n_eps_{k}") for k in ("n1", "n2", "n3", "n4")}
        n_rstd = {k: sem(f"n_rstd_{k}") for k in ("n1", "n2", "n3", "n4")}
        hid_ready = [sem(f"hid_ready{b}") for b in range(2)]
        out_ready = [sem(f"out_ready{b}") for b in range(2)]
        h_hi = sem("h_hi")
        h_lo = sem("h_lo")
        o_summed = sem("o_summed")
        x2_sum = sem("x2_sum")
        x2_ready = sem("x2_ready")
        x2_biased = sem("x2_biased")
        logit_done = sem("logit_done")
        choice_steps = sem("choice_steps")
        masked = [sem(f"masked{b}") for b in range(2)]
        xm_hi = sem("xm_hi")
        xm_lo = sem("xm_lo")
        ohT_copied = sem("ohT_copied")
        gelu_done = sem("gelu_done")
        g_hi = sem("g_hi")
        g_lo = sem("g_lo")
        y_summed = sem("y_summed")
        z_ready = sem("z_ready")
        z_gamma = sem("z_gamma")
        z_beta = sem("z_beta")
        out_ready_sb = sem("out_ready_sb")
        out_stored = sem("out_stored")

        def chunk_dram(name, n):
            if name == "pin":
                return p_in.rearrange("(k p) n -> p k n", p=P)[:, n // 2, (n % 2) * WCHUNK:(n % 2 + 1) * WCHUNK]
            if name == "pout":
                return p_out.rearrange("(c p) n -> p c n", p=P)[:, 8 * n:8 * n + 8, :]
            if name == "w1":
                return w_1.rearrange("(c p) n -> p c n", p=P)[:, 2 * n:2 * n + 2, :]
            return w_o.rearrange("(c p) n -> p c n", p=P)

        def chunk_sb(name, n, part):
            whole = {"pin": pin, "pout": pout, "w1": w1, "wo": wo}[name][part]
            return whole[:, :, :].rearrange("p c n -> p (c n)")[:, n * WCHUNK:(n + 1) * WCHUNK]

        def small_wait_ready(eng, a, key):
            wait(eng, small_ready[USE[key] % 2], a * SMALL_USES + USE[key] // 2 + 1)

        def small_read(a, key):
            name, j, n = key
            if name == "x_T":
                return xT_copied, a * TILES + j + 1
            if name == "qkv":
                return qkv_biased, a * 8 + 2 * j + n + 1
            if name == "qk_T":
                return qkT_copied, a * 16 + 4 * j + n + 1
            if name == "P_T":
                return PT_lo, a * 16 + 4 * j + n + 1
            if name == "PV":
                return pv_summed, a * 8 + 2 * j + n + 1
            if name == "x1_T":
                return x1T_lo, a * DK + n + 1
            return gatesT, a * 2 + (1 if name == "ctx_T" else 2)

        BY_USE = {u: k for k, u in USE.items()}

        def small_wait_free(pe, a, key):
            u = USE[key] - 2
            if u >= 0:
                wait(pe, *small_read(a, BY_USE[u]))
            elif not isinstance(a, int) or a > 0:
                wait(pe, *small_read(a - 1, BY_USE[u + len(USE)]))

        def hid_read(i, u):
            if u < HID_XM:
                return h_lo, i * E1 * C1 + u + 1
            if u < HID_F:
                return xm_lo, i * E2 * DK + u - HID_XM + 1
            return gelu_done, i * C2 + u - HID_F + 1

        def out_read(i, u):
            if u < OUT_OH:
                return o_summed, i * E1 * TILES + u + 1
            if u == OUT_OH:
                return ohT_copied, i + 1
            return y_summed, i * TILES + u - OUT_Y + 1

        def small_of(key):
            return small[USE[key] % 2]

        block = es.enter_context(nc.Block())

        @block.sync
        def _(sp):
            loads = [(wqkv[:, :, :], w_qkv.rearrange("(k p) n -> p k n", p=P)),
                     (bqkv[:, :], b_qkv[0, :].partition_broadcast(P)),
                     (bo_r[:, :], b_o.partition_broadcast(P)),
                     (gamma_r[:, :], gamma.partition_broadcast(P)),
                     (beta_r[:, :], beta.partition_broadcast(P)),
                     (router_r[:, :, :], w_router.partition_broadcast(P)),
                     (b1_sb, b_1)]
            for to, of in loads:
                sp.dma_start(to, of).then_inc(consts_loaded, 16)
            for again in range(2):
                for n, (name, q) in enumerate(WCHUNKS):
                    m = again * len(WCHUNKS) + n
                    if m >= 2:
                        if m - 2 < len(WCHUNKS):
                            sp.wait_ge(tops_found, m - 1)
                        else:
                            sp.wait_ge(stage_lo, m - 1 - len(WCHUNKS))
                    src = chunk_dram(name, q)
                    to = stage[m % 2] if name == "pin" else stage[m % 2].rearrange("p (c n) -> p c n", n=src.shape[-1])
                    sp.dma_start(to, src).then_inc(stage_loaded[m % 2], 16)
            for part in range(3):
                sp.wait_ge(b1_steps, 2 + 2 * part)
                sp.dma_start(b1p[E2 * part:E2 * part + E2, :], b1_h[part]).then_inc(b1_placed, 16)

            def load_step(a):
                wait(sp, x1_sum, a * TILES)
                sp.dma_start(x_sb[:, :, :], x_of(a)).then_inc(x_loaded, 16)

            def load_gates(a):
                wait(sp, scores_done, (a + 1) * 8)
                sp.dma_start(ctx_sb, rows_of(ctx, a)).then_inc(gates_loaded, 16)
                sp.dma_start(tok_sb, rows_of(itok, a)).then_inc(gates_loaded, 16)

            def rows_of(t, a):
                return t.rearrange("(i j) s d -> i s j d", j=TILES)[a]

            def x_of(a):
                return rows_of(x, a)

            def attention(a, pos):
                for name, j, n in TIMETABLE.get(pos, []):
                    if name == "shuffle":
                        wait(sp, qkv_biased, a * 8 + 2 * j + 2)
                        sp.dma_start(qkv_dram[j], qkv_tok[:, :]).then_inc(qkv_stored, 16)
                        wait(sp, lo_written, a * 8 + 2 * j)
                        settle(sp)
                        wait(sp, qkv_stored, (a * TILES + j + 1) * 16)
                        sp.dma_start(qkv_h[:, :, :, :].rearrange("p h s e -> p h (s e)"),
                                     qkv_dram[j].rearrange("s (c f) -> (s c) f", c=HEADS)
                                     .rearrange("(h p) f -> p h f", h=HEADS)).then_inc(qkv_reloaded, 16)
                    if name == "gather":
                        wait(sp, attn_scaled, a * 8 + 2 * j + 2)
                        sp.dma_start(attn_dram[j].rearrange("s (c f) -> (s c) f", c=HEADS)
                                     .rearrange("(h p) f -> p h f", h=HEADS),
                                     attn_h[:, :, :]).then_inc(attn_stored, 16)
                        if j == 0:
                            wait(sp, out_stored, (a - 1) * 16)
                            settle(sp)
                        wait(sp, attn_stored, (a * TILES + j + 1) * 16)
                        sp.dma_start(attn[:, j, :], attn_dram[j]).then_inc(attn_loaded, 16)

            def settle(eng):
                eng.sem_inc(settled, 1)

            def tail(i):
                wait(sp, out_ready_sb, (i + 1) * TILES)
                sp.dma_start(rows_of(out, i), yy[:, :, :]).then_inc(out_stored, 16)

            def step(i, a, t):
                if a is not None:
                    load_step(a)
                for pos in range(POSITIONS):
                    if t is not None and TAIL.get(pos, ("",))[0] == "store":
                        tail(t)
                    if a is not None:
                        attention(a, pos)
                    if a is not None and pos == GATES_AT:
                        load_gates(a)

            step(None, 0, None)
            step(0, 1, None)
            with sp.Fori(1, STEPS - 1) as i:
                step(i, i + 1, i - 1)
            step(STEPS - 1, None, STEPS - 2)
            tail(STEPS - 1)
            sp.wait_ge(out_stored, 16 * STEPS)

        @block.gpsimd
        def _(pool):
            pool.memset(ident[:, :], 0.0).then_inc(const_pool, 1)
            pool.memset(ident16[:, :], 0.0).then_inc(const_pool, 1)
            pool.memset(mask[:, :], 0.0).then_inc(const_pool, 1)
            pool.memset(minus_half[:, :], -0.5).then_inc(const_pool, 1)
            pool.memset(oh12[:, :, :], 0.0).then_inc(const_pool, 1)
            pool.memset(b1p[:, :], 0.0).then_inc(const_pool, 1)
            for e in range(E2):
                pool.memset(choice[:, e:e + 1], float(E2 + e)).then_inc(const_pool, 1)
            pool.memset(tops[:, :], 0.0).then_inc(const_pool, 1)
            pool.wait_ge(const_pool, 11)
            for m in (ident, ident16):
                pool.affine_select(out=m[:, :], in_=m[:, :], compare_op=ALU.not_equal, fill=1.0, base=0,
                                   pattern=[[-1, P]], channel_multiplier=1).then_inc(const_pool, 1)
            pool.affine_select(out=mask[:, :], in_=mask[:, :], compare_op=ALU.is_ge, fill=MASKED, base=0,
                               pattern=[[-1, P]], channel_multiplier=1).then_inc(const_pool, 1)
            pool.wait_ge(top_reduced, 1)
            pool.partition_all_reduce(top5a[:, 0:5], top5[:, 0:5], P, bass.bass_isa.ReduceOp.max).then_inc(scales, 1)

            def rsqrt(k, i):
                wait(pool, n_eps[k], i + 1)
                pool.tensor_tensor(rstd[k][:, :], vare[k][:, :], minus_half[:, :], ALU.pow).then_inc(n_rstd[k], 1)

            def late(a):
                wait(pool, gates_loaded, (a + 1) * 32)
                pool.sem_inc(settled, 1)
                pool.tensor_copy(tokf, tok_sb).then_inc(tok_cast, 1)
                rsqrt("n1", a)

            def mixed(i, a):
                rsqrt("n2", i)
                wait(pool, x2_ready, (i + 1) * TILES)
                pool.tensor_tensor(x2b[:, :, :], acc[:, :, :], beta_r[:, None, :].to_broadcast([P, TILES, D]),
                                   ALU.add).then_inc(x2_biased, 1)
                if a is not None:
                    wait(pool, x1_sum, (a + 1) * TILES)
                else:
                    wait(pool, out_stored, i * 16)
                pool.tensor_tensor(yy[:, :, :], acc[:, :, :], bo_r[:, None, :].to_broadcast([P, TILES, D]),
                                   ALU.add).then_inc(x2_biased, 1)

            def tail(i, what):
                if what == "aggregate":
                    rsqrt("n3", i)
                if what == "normal":
                    wait(pool, z_ready, (i + 1) * TILES)
                    pool.tensor_tensor(yy[:, :, :], yy[:, :, :], gamma_r[:, None, :].to_broadcast([P, TILES, D]),
                                       ALU.mult).then_inc(z_gamma, 1)
                    wait(pool, z_gamma, i + 1)
                    pool.tensor_tensor(yy[:, :, :], yy[:, :, :], x2b[:, :, :], ALU.add).then_inc(z_beta, 1)
                if what == "aggregate2":
                    rsqrt("n4", i)

            def step(i, a, t):
                for pos in range(POSITIONS):
                    if t is not None and pos in TAIL:
                        tail(t, TAIL[pos][0])
                if i is not None:
                    mixed(i, a)
                if a is not None:
                    late(a)

            pool.wait_ge(consts_loaded, 16 * 7)
            step(None, 0, None)
            step(0, 1, None)
            with pool.Fori(1, STEPS - 1) as i:
                step(i, i + 1, i - 1)
            step(STEPS - 1, None, STEPS - 2)
            for pos in sorted(TAIL):
                tail(STEPS - 1, TAIL[pos][0])

        @block.scalar
        def _(act):
            act.wait_ge(scales, 6)
            for n, (name, q) in enumerate(WCHUNKS):
                m = len(WCHUNKS) + n
                w = WNAMES.index(name)
                act.wait_ge(stage_loaded[m % 2], 16 * (m // 2 + 1))
                act.activation(chunk_sb(name, q, 0), stage[m % 2], ACT.Copy,
                               scale=up[:, w:w + 1]).then_inc(stage_hi, 1)

            def attention(a, pos):
                for name, j, n in TIMETABLE.get(pos, []):
                    key = (name, j, n)
                    b = j % 2
                    if name == "x_T":
                        small_wait_ready(act, a, key)
                        if (j > 0) or not isinstance(a, int) or a > 0:
                            before = (a, j - 1) if j else (a - 1, TILES - 1)
                            small_wait_ready(act, before[0], ("qkv", before[1], 1))
                        act.activation(split_all[:, QKV:QKV + D], small_of(key)[:, 0:D],
                                       ACT.Copy).then_inc(xT_copied, 1)
                    if name == "split":
                        wait(act, qkv_reloaded, (a * TILES + j + 1) * 16)
                        if j >= 2:
                            small_wait_ready(act, a, ("PV", j - 2, 1))
                        elif not isinstance(a, int) or a > 0:
                            wait(act, hid_ready[(HID_F + C2 - 1) % 2], (a - 1) * HID_USES)
                            small_wait_ready(act, a - 1, ("PV", j + 2, 1))
                        q, k, v = (qkv_h[:, :, s, :] for s in range(3))
                        act.activation(qk6[b][:, :, 3:6, :], q[:, :, None, :].to_broadcast([P, HEADS, 3, HD]),
                                       ACT.Copy).then_inc(hi_written, 1)
                        act.activation(qk6[b][:, :, 6:11:2, :], k[:, :, None, :].to_broadcast([P, HEADS, 3, HD]),
                                       ACT.Copy).then_inc(hi_written, 1)
                        act.activation(qk6[b][:, :, 12, :], v, ACT.Copy).then_inc(hi_written, 1)
                        wait(act, rest_found, a * TILES + j + 1)
                        q, k, v = (rest[:, :, s, :] for s in range(3))
                        act.activation(qk6[b][:, :, 0:2, :], q[:, :, None, :].to_broadcast([P, HEADS, 2, HD]),
                                       ACT.Copy).then_inc(mid_written, 1)
                        act.activation(qk6[b][:, :, 7:10:2, :], k[:, :, None, :].to_broadcast([P, HEADS, 2, HD]),
                                       ACT.Copy).then_inc(mid_written, 1)
                        act.activation(qk6[b][:, :, 14, :], v, ACT.Copy).then_inc(mid_written, 1)
                    if name == "qk_T":
                        small_wait_ready(act, a, key)
                        wait(act, scores_done, a * 8 + 2 * j + n // 2)
                        act.activation(qkT[0:96, n % 2, :, :].rearrange("p h t -> p (h t)"),
                                       small_of(key)[0:96, :].bitcast(BF16), ACT.Copy).then_inc(qkT_copied, 1)
                    if name == "exp":
                        h = n // 2
                        wait(act, max_found, a * 8 + 2 * j + h + 1)
                        wait(act, sums_inverted, a * 8 + 2 * (j - 1) + h + 1)
                        for g in range(4 * (n % 2), 4 * (n % 2) + 4):
                            act.activation(prob[:, h, g, :], prob[:, h, g, :], ACT.Exp, bias=neg_max[:, h, g:g + 1],
                                           scale=1.0, accum_out=row_sum[:, h, g:g + 1]).then_inc(exps_done, 1)
                    if name == "P_T":
                        small_wait_ready(act, a, key)
                        act.activation(PT[0][:, n % 2, :, :].rearrange("p h t -> p (h t)"), small_of(key)[:, :],
                                       ACT.Copy).then_inc(PT_hi, 1)

            def copy_gates(a):
                small_wait_ready(act, a, ("ctx_T", 0, 0))
                wait(act, qkv_stored, (a + 1) * TILES * 16)
                act.activation(ctxT.rearrange("p j k -> p (j k)"), small_of(("ctx_T", 0, 0))[:, :],
                               ACT.Copy).then_inc(gatesT, 1)
                small_wait_ready(act, a, ("tok_T", 0, 0))
                wait(act, lo_written, (a + 1) * TILES * 2)
                act.activation(tokT.rearrange("p j k -> p (j k)"), small_of(("tok_T", 0, 0))[:, :],
                               ACT.Copy).then_inc(gatesT, 1)

            def copy_x1(a):
                for k in range(DK):
                    key = ("x1_T", 0, k)
                    small_wait_ready(act, a, key)
                    act.activation(x1T[0][:, k, :], small_of(key)[:, :], ACT.Copy).then_inc(x1T_hi, 1)

            def hidden(i, n):
                e, c = n // C1, n % C1
                wait(act, hid_ready[n % 2], i * HID_USES + n // 2 + 1)
                if e >= 2:
                    u = (e - 1) * TILES - 1
                    wait(act, out_ready[u % 2], i * OUT_USES[u % 2] + u // 2 + 1)
                elif not isinstance(i, int) or i > 0:
                    u = OUT_Y + TILES - 1
                    wait(act, out_ready[u % 2], i * OUT_USES[u % 2])
                if n == 0 and isinstance(i, int) and i == 0:
                    act.wait_ge(b1_placed, 48)
                act.activation(hT[0][:, e % 2, c, :], hid[n % 2][:, :], ACT.Relu).then_inc(h_hi, 1)

            def ffn_in(i, a):
                if a is not None:
                    for j in (TILES - 2, TILES - 1):
                        small_wait_ready(act, a, ("PV", j, 1))
                for n in range(E2 * DK):
                    u = HID_XM + n
                    wait(act, hid_ready[u % 2], i * HID_USES + u // 2 + 1)
                    act.activation(xmT[0][:, n // DK, n % DK, :], hid[u % 2][:, :], ACT.Copy).then_inc(xm_hi, 1)
                wait(act, out_ready[OUT_OH % 2], i * OUT_USES[OUT_OH % 2] + OUT_OH // 2 + 1)
                act.activation(ohT[:, :], outp[OUT_OH % 2][:, 0:T // 2].bitcast(BF16), ACT.Copy).then_inc(ohT_copied, 1)

            def gelus(i):
                for c in range(C2):
                    u = HID_F + c
                    wait(act, hid_ready[u % 2], i * HID_USES + u // 2 + 1)
                    wait(act, g_lo, i * C2 + c - 1)
                    act.activation(g32[:, c % 2, :], hid[u % 2][:, :], ACT.Gelu,
                                   scale=down[:, 2:3]).then_inc(gelu_done, 1)
                    wait(act, gelu_done, i * C2 + c + 1)
                    act.activation(gT[0][:, c, :], g32[:, c % 2, :], ACT.Copy, scale=up[:, 4:5]).then_inc(g_hi, 1)

            def step(i, a, t):
                for pos in range(POSITIONS):
                    if i is not None and pos % 2 == 0 and pos // 2 < E1 * C1:
                        hidden(i, pos // 2)
                    if a is not None:
                        attention(a, pos)
                if i is not None:
                    ffn_in(i, a)
                if a is not None:
                    copy_gates(a)
                if i is not None:
                    gelus(i)
                if a is not None:
                    copy_x1(a)

            step(None, 0, None)
            step(0, 1, None)
            with act.Fori(1, STEPS - 1) as i:
                step(i, i + 1, i - 1)
            step(STEPS - 1, None, STEPS - 2)

        @block.tensor
        def _(pe):
            pe.wait_ge(const_pool, 14)

            def attention(a, pos):
                for name, j, n in TIMETABLE.get(pos, []):
                    key = (name, j, n)
                    b = j % 2
                    if key in USE:
                        small_wait_free(pe, a, key)
                        bank, ready = small_of(key), small_ready[USE[key] % 2]
                    if name == "x_T":
                        wait(pe, x_loaded, (a + 1) * 16)
                        for k in range(DK):
                            mm = pe.transpose(bank[:, k * P:(k + 1) * P], x_sb[:, j, k * P:(k + 1) * P], ident[:, :])
                        mm.then_inc(ready, 1)
                    if name == "qkv":
                        wait(pe, xT_copied, a * TILES + j + 1)
                        c0, c1 = (0, T) if n == 0 else (T, QKV)
                        for k in range(DK):
                            mm = pe.matmul(bank[:, 0:c1 - c0], xT[:, k, :], wqkv[:, k, c0:c1], start=(k == 0), stop=(k == DK - 1))
                        mm.then_inc(ready, 1)
                    if name == "qk_T":
                        wait(pe, lo_written, a * 8 + 2 * j + 2)
                        wait(pe, mid_written, a * 12 + 3 * j + 3)
                        turned = bank[:, :].bitcast(BF16)
                        for g in range(4):
                            flat = qk6[b][:, 4 * n + g, :, :].rearrange("p s e -> p (s e)")
                            for half in range(2):
                                s = 2 * g + half
                                mm = pe.transpose(turned[0:96, s * P:(s + 1) * P], flat[:, 96 * half:96 * half + 96], ident16[:, :])
                        mm.then_inc(ready, 1)
                    if name == "scores":
                        wait(pe, qkT_copied, a * 16 + 4 * j + 2 * n + 2)
                        wait(pe, scores_masked, a * 8 + 2 * j + n)
                        for g in range(8):
                            mm = pe.matmul(score[:, g, :], qkT[0:96, g // 4, 2 * (g % 4), :], qkT[0:96, g // 4, 2 * (g % 4) + 1, :],
                                           start=True, stop=True)
                        mm.then_inc(scores_done, 1)
                    if name == "P_T":
                        wait(pe, exps_done, a * 64 + 16 * j + 4 * n + 4)
                        for g in range(4):
                            mm = pe.transpose(bank[:, g * P:(g + 1) * P], prob[:, n // 2, 4 * (n % 2) + g, :], ident[:, :])
                        mm.then_inc(ready, 1)
                    if name == "PV":
                        wait(pe, PT_lo, a * 16 + 4 * j + 2 * n + 2)
                        for g in range(8):
                            v3 = qk6[b][:, 8 * n + g, 12:15, :].rearrange("p s e -> p (s e)")
                            for part in range(2):
                                mm = pe.matmul(bank[:, 48 * g:48 * g + 48], PT[part][:, g // 4, g % 4, :], v3,
                                               start=(part == 0), stop=(part == 1))
                        mm.then_inc(ready, 1)

            def turn_gates(a):
                for key, src, sem_, val in ((("ctx_T", 0, 0), ctx_sb, gates_loaded, (a + 1) * 32),
                                            (("tok_T", 0, 0), tokf, tok_cast, a + 1)):
                    small_wait_free(pe, a, key)
                    wait(pe, sem_, val)
                    for j in range(TILES):
                        mm = pe.transpose(small_of(key)[:, j * P:(j + 1) * P], src[:, j, :], ident[:, :])
                    mm.then_inc(small_ready[USE[key] % 2], 1)

            def turn_x1(a):
                wait(pe, x1_ready, (a + 1) * TILES)
                for k in range(DK):
                    key = ("x1_T", 0, k)
                    small_wait_free(pe, a, key)
                    for j in range(TILES):
                        mm = pe.transpose(small_of(key)[:, j * P:(j + 1) * P], x1[:, j, k * P:(k + 1) * P], ident[:, :])
                    mm.then_inc(small_ready[USE[key] % 2], 1)

            def hid_wait_free(i, u):
                if u >= 2:
                    wait(pe, *hid_read(i, u - 2))
                else:
                    wait(pe, gelu_done, i * C2 - 1 + u)

            def out_wait_free(i, u):
                if u >= 2:
                    wait(pe, *out_read(i, u - 2))
                else:
                    wait(pe, y_summed, i * TILES - u)

            PAIRS = ((0, 0), (1, 0), (0, 1))

            def hidden(i, n):
                e, c = n // C1, n % C1
                if n == 0:
                    wait(pe, x1T_lo, (i + 1) * DK)
                    if isinstance(i, int) and i == 0:
                        pe.wait_ge(stage_lo, 4)
                hid_wait_free(i, n)
                terms = [(k, w, v) for k in range(DK) for w, v in PAIRS]
                for m, (k, w, v) in enumerate(terms):
                    mm = pe.matmul(hid[n % 2][:, :], pin[w][:, k, e * I1 + c * P:e * I1 + (c + 1) * P], x1T[v][:, k, :],
                                   start=(m == 0), stop=(m == len(terms) - 1))
                mm.then_inc(hid_ready[n % 2], 1)

            def output(i, n):
                e, j = n // TILES, n % TILES
                if n == 0 and isinstance(i, int) and i == 0:
                    pe.wait_ge(stage_lo, 8)
                if j == 0:
                    wait(pe, h_lo, i * E1 * C1 + (e + 1) * C1)
                out_wait_free(i, n)
                terms = [(c, v, w) for c in range(C1) for w, v in PAIRS]
                for m, (c, v, w) in enumerate(terms):
                    mm = pe.matmul(outp[n % 2][:, 0:D], hT[w][:, e % 2, c, j * P:(j + 1) * P], pout[v][:, e * C1 + c, :],
                                   start=(m == 0), stop=(m == len(terms) - 1))
                mm.then_inc(out_ready[n % 2], 1)

            def ffn_in(i):
                for n in range(E2 * DK):
                    e, k = n // DK, n % DK
                    u = HID_XM + n
                    if k == 0:
                        wait(pe, masked[e % 2], i * 2 + e // 2 + 1)
                    hid_wait_free(i, u)
                    for j in range(TILES):
                        mm = pe.transpose(hid[u % 2][:, j * P:(j + 1) * P], xm[e % 2][:, j, k * P:(k + 1) * P], ident[:, :])
                    mm.then_inc(hid_ready[u % 2], 1)
                wait(pe, choice_steps, (i + 1) * 6)
                out_wait_free(i, OUT_OH)
                turned = outp[OUT_OH % 2][:, 0:T // 2].bitcast(BF16)
                for j in range(TILES):
                    mm = pe.transpose(turned[:, j * P:(j + 1) * P], oh12[:, j, :], ident16[:, :])
                mm.then_inc(out_ready[OUT_OH % 2], 1)

            def ffn_hidden(i):
                if isinstance(i, int) and i == 0:
                    pe.wait_ge(stage_lo, len(WCHUNKS))
                    pe.wait_ge(b1_placed, 48)
                wait(pe, ohT_copied, i + 1)
                wait(pe, xm_lo, (i + 1) * E2 * DK)
                for c in range(C2):
                    u = HID_F + c
                    hid_wait_free(i, u)
                    pe.matmul(hid[u % 2][:, :], b1p[:, c * P:(c + 1) * P], ohT[:, :], start=True, stop=False)
                    terms = [(e, k, w, v) for e in range(E2) for k in range(DK) for w, v in PAIRS]
                    for m, (e, k, w, v) in enumerate(terms):
                        mm = pe.matmul(hid[u % 2][:, :], w1[w][:, e * DK + k, c * P:(c + 1) * P], xmT[v][:, e, k, :],
                                       start=False, stop=(m == len(terms) - 1))
                    mm.then_inc(hid_ready[u % 2], 1)

            def ffn_out(i):
                wait(pe, g_lo, (i + 1) * C2)
                for j in range(TILES):
                    u = OUT_Y + j
                    out_wait_free(i, u)
                    terms = [(c, v, w) for c in range(C2) for w, v in PAIRS]
                    for m, (c, v, w) in enumerate(terms):
                        mm = pe.matmul(outp[u % 2][:, 0:D], gT[w][:, c, j * P:(j + 1) * P], wo[v][:, c, :],
                                       start=(m == 0), stop=(m == len(terms) - 1))
                    mm.then_inc(out_ready[u % 2], 1)

            def step(i, a, t):
                for pos in range(POSITIONS):
                    n = pos // 2
                    if i is not None and pos % 2 == 0 and n < E1 * C1:
                        hidden(i, n)
                    if i is not None and pos % 2 == 1 and n >= LAG:
                        output(i, n - LAG)
                    if a is not None:
                        attention(a, pos)
                if i is not None:
                    ffn_in(i)
                if a is not None:
                    turn_gates(a)
                if i is not None:
                    ffn_hidden(i)
                if a is not None:
                    turn_x1(a)
                if i is not None:
                    ffn_out(i)

            pe.wait_ge(consts_loaded, 16 * 7)
            step(None, 0, None)
            step(0, 1, None)
            with pe.Fori(1, STEPS - 1) as i:
                step(i, i + 1, i - 1)
            step(STEPS - 1, None, STEPS - 2)

        @block.vector
        def _(dve):
            dve.wait_ge(const_pool, 14)
            for m, (name, q) in enumerate(WCHUNKS):
                dve.wait_ge(stage_loaded[m % 2], 16 * (m // 2 + 1))
                dve.tensor_reduce(tops[:, m:m + 1], stage[m % 2], AX.X, ALU.max,
                                  apply_absolute_value=True).then_inc(tops_found, 1)
            dve.wait_ge(consts_loaded, 16 * 7)
            K = len(WCHUNKS)
            dve.tensor_reduce(tops[0:E2, K:K + 1], b1_sb, AX.X, ALU.max, apply_absolute_value=True).then_inc(tops_found, 1)
            dve.wait_ge(tops_found, K + 1)
            dve.tensor_reduce(top5[:, 0:3], tops[:, 0:12].rearrange("p (w n) -> p w n", n=4), AX.X, ALU.max)
            dve.tensor_copy(top5[:, 3:5], tops[:, 12:14]).then_inc(top_reduced, 1)
            dve.wait_ge(scales, 1)
            dve.scalar_tensor_tensor(out=top5a[:, 4:5], in0=top5a[:, 2:3], scalar=float(D), in1=top5a[:, 4:5],
                                     op0=ALU.mult, op1=ALU.add).then_inc(scales, 1)
            dve.wait_ge(scales, 2)
            dve.tensor_scalar(pow2[:, 0:5], top5a[:, 0:5], 2.0 ** -40, None, ALU.max).then_inc(scales, 1)
            dve.wait_ge(scales, 3)
            bits = pow2[:, 0:5].bitcast(I32)
            dve.tensor_scalar(bits, bits, 0x7F800000, None, ALU.bitwise_and).then_inc(scales, 1)
            dve.wait_ge(scales, 4)
            dve.reciprocal(inv2[:, 0:5], pow2[:, 0:5]).then_inc(scales, 1)
            dve.wait_ge(scales, 5)
            for c0, c1, f in ((0, 4, 2.0 ** 6), (4, 5, 2.0 ** 14)):
                dve.tensor_scalar(down[:, c0:c1], pow2[:, c0:c1], 1.0 / f, None, ALU.mult)
                last = dve.tensor_scalar(up[:, c0:c1], inv2[:, c0:c1], f, None, ALU.mult)
            last.then_inc(scales, 1)
            dve.wait_ge(scales, 6)
            dve.tensor_tensor(down[:, 5:6], down[:, 3:4], down[:, 4:5], ALU.mult)
            dve.tensor_scalar(b1_sb, b1_sb, up[0:E2, 2:3], None, ALU.mult).then_inc(b1_steps, 1)
            for part in range(3):
                dve.wait_ge(b1_steps, 1 + 2 * part)
                dve.tensor_copy(b1_h[part], b1_sb).then_inc(b1_steps, 1)
                dve.wait_ge(b1_steps, 2 + 2 * part)
                dve.tensor_tensor(b1_sb, b1_sb, b1_h[part], ALU.subtract).then_inc(b1_steps, 1)
            for n, (name, q) in enumerate(WCHUNKS):
                m = len(WCHUNKS) + n
                w = WNAMES.index(name)
                dve.wait_ge(stage_hi, n + 1)
                dve.wait_ge(stage_loaded[m % 2], 16 * (m // 2 + 1))
                dve.scalar_tensor_tensor(out=chunk_sb(name, q, 1), in0=stage[m % 2], scalar=up[:, w:w + 1],
                                         in1=chunk_sb(name, q, 0), op0=ALU.mult, op1=ALU.subtract).then_inc(stage_lo, 1)
            dve.wait_ge(stage_lo, len(WCHUNKS))

            def attention(a, pos):
                for name, j, n in TIMETABLE.get(pos, []):
                    key = (name, j, n)
                    b = j % 2
                    if name == "qkv":
                        small_wait_ready(dve, a, key)
                        wait(dve, qkv_stored, (a * TILES + j) * 16)
                        wait(dve, gate_summed, a * TILES * E1)
                        c0, c1 = (0, T) if n == 0 else (T, QKV)
                        dve.tensor_tensor(qkv_tok[:, c0:c1], small_of(key)[:, 0:c1 - c0], bqkv[:, c0:c1],
                                          ALU.add).then_inc(qkv_biased, 1)
                    if name == "split":
                        wait(dve, hi_written, a * 12 + 3 * j + 3)
                        wait(dve, mid_written, a * 12 + 3 * j)
                        wait(dve, lo_written, a * 8 + 2 * j)
                        for_h = qk6[b][:, :, 4:13:4, :]
                        dve.tensor_tensor(rest, qkv_h[:, :, :, :], for_h, ALU.subtract).then_inc(rest_found, 1)
                        wait(dve, rest_found, a * TILES + j + 1)
                        wait(dve, mid_written, a * 12 + 3 * j + 3)
                        dve.tensor_tensor(qk6[b][:, :, 2:12:9, :], rest[:, :, 0:2, :], qk6[b][:, :, 0:8:7, :],
                                          ALU.subtract).then_inc(lo_written, 1)
                        dve.tensor_tensor(qk6[b][:, :, 13, :], rest[:, :, 2, :], qk6[b][:, :, 14, :],
                                          ALU.subtract).then_inc(lo_written, 1)
                    if name == "mask":
                        wait(dve, scores_done, a * 8 + 2 * j + n + 1)
                        if j:
                            small_wait_ready(dve, a, ("P_T", j - 1, 2 * n + 1))
                        elif not isinstance(a, int) or a > 0:
                            small_wait_ready(dve, a - 1, ("P_T", TILES - 1, 2 * n + 1))
                            u = HID_XM + E2 * DK - 1 - DK * (1 - n)
                            wait(dve, hid_ready[u % 2], (a - 2) * HID_USES + u // 2 + 1)
                        dve.scalar_tensor_tensor(out=prob[:, n, :, :], in0=score[:, :, :], scalar=SCORE_SCALE,
                                                 in1=mask[:, None, :].to_broadcast([P, 8, P]),
                                                 op0=ALU.mult, op1=ALU.add).then_inc(scores_masked, 1)
                        wait(dve, scores_masked, a * 8 + 2 * j + n + 1)
                        wait(dve, exps_done, a * 64 + 16 * (j - 1) + 8 * n + 8)
                        dve.tensor_reduce(neg_max[:, n, :], prob[:, n, :, :], AX.X, ALU.max,
                                          negate=True).then_inc(max_found, 1)
                    if name == "P_T":
                        wait(dve, PT_hi, a * 16 + 4 * j + n + 1)
                        dve.tensor_tensor(PT[1][:, n % 2, :, :].rearrange("p h t -> p (h t)"), small_of(key)[:, :],
                                          PT[0][:, n % 2, :, :].rearrange("p h t -> p (h t)"),
                                          ALU.subtract).then_inc(PT_lo, 1)
                    if name == "PV":
                        wait(dve, exps_done, a * 64 + 16 * j + 8 * n + 8)
                        dve.reciprocal(row_inv[:, n, :], row_sum[:, n, :]).then_inc(sums_inverted, 1)
                        small_wait_ready(dve, a, key)
                        wait(dve, attn_scaled, a * 8 + 2 * j + n)
                        dve.tensor_reduce(pv[:, :, :], small_of(key)[:, 0:384].rearrange("p (h c e) -> p h e c", h=8, c=3),
                                          AX.X, ALU.add).then_inc(pv_summed, 1)
                        wait(dve, pv_summed, a * 8 + 2 * j + n + 1)
                        wait(dve, sums_inverted, a * 8 + 2 * j + n + 1)
                        wait(dve, attn_stored, (a * TILES + j) * 16)
                        dve.tensor_tensor(attn_h[:, 8 * n:8 * n + 8, :], pv[:, :, :],
                                          row_inv[:, n, :, None].to_broadcast([P, 8, HD]),
                                          ALU.mult).then_inc(attn_scaled, 1)

            def norm_stats(k, i, src, j):
                dve.bn_stats(stats[k][:, j, :], src[:, j, :]).then_inc(n_stats[k], 1)

            def norm_aggregate(k, i, eps):
                wait(dve, n_stats[k], (i + 1) * TILES)
                dve.sem_inc(settled, 1)
                for j in range(TILES):
                    last = dve.bn_aggr(mv[k][:, j, :], stats[k][:, j, :])
                last.then_inc(n_aggr[k], 1)
                wait(dve, n_aggr[k], i + 1)
                dve.tensor_scalar(vare[k][:, :], mv[k][:, :, 1], eps, None, ALU.add).then_inc(n_eps[k], 1)

            def norm_apply(k, i, t, done):
                wait(dve, n_rstd[k], i + 1)
                for j in range(TILES):
                    dve.tensor_scalar(t[:, j, :], t[:, j, :], mv[k][:, j, 0:1], rstd[k][:, j:j + 1],
                                      ALU.subtract, ALU.mult).then_inc(done, 1)

            def first_sum(a):
                wait(dve, attn_loaded, (a + 1) * TILES * 16)
                for j in range(TILES):
                    dve.tensor_tensor(x1[:, j, :], x_sb[:, j, :], attn[:, j, :], ALU.add).then_inc(x1_sum, 1)

            def gates(a):
                wait(dve, x1_sum, (a + 1) * TILES)
                for j in range(TILES):
                    norm_stats("n1", a, x1, j)
                norm_aggregate("n1", a, 1e-5)
                wait(dve, gatesT, (a + 1) * 2)
                wait(dve, o_summed, a * E1 * TILES)
                for j in range(TILES):
                    for e in range(E1):
                        wait(dve, gate_summed, a * TILES * E1 + j * E1 + e - 1)
                        dve.scalar_tensor_tensor(out=junk[:, e % 2, 0:P], in0=tokT[:, j, :], scalar=float(e),
                                                 in1=ctxT[:, j, :], op0=ALU.is_equal, op1=ALU.mult,
                                                 accum_out=gate[:, j, e:e + 1]).then_inc(gate_summed, 1)
                wait(dve, gate_summed, (a + 1) * TILES * E1)
                dve.tensor_scalar(gate[:, :, :], gate[:, :, :], down[:, 0:1], None, ALU.mult).then_inc(gate_scaled, 1)
                norm_apply("n1", a, x1, x1_ready)

            def x1_lo(a):
                for k in range(DK):
                    key = ("x1_T", 0, k)
                    wait(dve, x1T_hi, a * DK + k + 1)
                    dve.tensor_tensor(x1T[1][:, k, :], small_of(key)[:, :], x1T[0][:, k, :],
                                      ALU.subtract).then_inc(x1T_lo, 1)

            def hidden(i, n):
                e, c = n // C1, n % C1
                wait(dve, h_hi, i * E1 * C1 + n + 1)
                dve.scalar_tensor_tensor(out=hT[1][:, e % 2, c, :], in0=hid[n % 2][:, :], scalar=0.0,
                                         in1=hT[0][:, e % 2, c, :], op0=ALU.max, op1=ALU.subtract).then_inc(h_lo, 1)

            def output(i, n):
                e, j = n // TILES, n % TILES
                if n == 0:
                    wait(dve, gate_scaled, i + 1)
                    wait(dve, x2_biased, 2 * i)
                wait(dve, out_ready[n % 2], i * OUT_USES[n % 2] + n // 2 + 1)
                if e == 0:
                    dve.tensor_scalar(acc[:, j, :], outp[n % 2][:, 0:D], gate[:, j, e:e + 1], None,
                                      ALU.mult).then_inc(o_summed, 1)
                else:
                    wait(dve, o_summed, i * E1 * TILES + n - TILES + 1)
                    dve.scalar_tensor_tensor(out=acc[:, j, :], in0=outp[n % 2][:, 0:D], scalar=gate[:, j, e:e + 1],
                                             in1=acc[:, j, :], op0=ALU.mult, op1=ALU.add).then_inc(o_summed, 1)

            def second_norm(i):
                wait(dve, o_summed, (i + 1) * E1 * TILES)
                for j in range(TILES):
                    dve.scalar_tensor_tensor(out=acc[:, j, :], in0=acc[:, j, :], scalar=down[:, 1:2], in1=x1[:, j, :],
                                             op0=ALU.mult, op1=ALU.add).then_inc(x2_sum, 1)
                wait(dve, x2_sum, (i + 1) * TILES)
                for j in range(TILES):
                    norm_stats("n2", i, acc, j)
                norm_aggregate("n2", i, 1e-5)
                norm_apply("n2", i, acc, x2_ready)

            def route(i, a):
                wait(dve, x2_ready, (i + 1) * TILES)
                for j in range(TILES):
                    for e in range(E2):
                        wait(dve, logit_done, i * TILES * E2 + j * E2 + e - 1)
                        dve.tensor_tensor_reduce(junk[:, e % 2, :], acc[:, j, :], router_r[:, e, :], 1.0, 0.0,
                                                 ALU.mult, ALU.add, logit[:, j, e:e + 1]).then_inc(logit_done, 1)
                wait(dve, logit_done, (i + 1) * TILES * E2)
                s = i * 6
                dve.tensor_reduce(logit_top[:, :], logit[:, :, :], AX.X, ALU.max).then_inc(choice_steps, 1)
                wait(dve, choice_steps, s + 1)
                dve.tensor_tensor(is_top[:, :, :], logit[:, :, :], logit_top[:, :, None].to_broadcast([P, TILES, E2]),
                                  ALU.is_ge).then_inc(choice_steps, 1)
                wait(dve, choice_steps, s + 2)
                dve.scalar_tensor_tensor(out=index[:, :, :], in0=is_top[:, :, :], scalar=-float(E2),
                                         in1=choice[:, None, :].to_broadcast([P, TILES, E2]),
                                         op0=ALU.mult, op1=ALU.add).then_inc(choice_steps, 1)
                wait(dve, choice_steps, s + 3)
                dve.tensor_reduce(index_min[:, :], index[:, :, :], AX.X, ALU.min).then_inc(choice_steps, 1)
                wait(dve, choice_steps, s + 4)
                dve.tensor_tensor(onehot[:, :, :], index[:, :, :], index_min[:, :, None].to_broadcast([P, TILES, E2]),
                                  ALU.is_equal).then_inc(choice_steps, 1)
                wait(dve, choice_steps, s + 5)
                dve.tensor_copy(oh12[:, :, 0:3 * E2].rearrange("p j (c e) -> p j c e", c=3),
                                onehot[:, :, None, :].to_broadcast([P, TILES, 3, E2])).then_inc(choice_steps, 1)
                if a is not None:
                    small_wait_ready(dve, a, ("P_T", TILES - 1, 1))
                    small_wait_ready(dve, a, ("P_T", TILES - 1, 3))
                for e in range(E2):
                    if e >= 2:
                        u = HID_XM + DK * (e - 1) - 1
                        wait(dve, hid_ready[u % 2], i * HID_USES + u // 2 + 1)
                    dve.tensor_tensor(xm[e % 2], acc[:, :, :], onehot[:, :, e:e + 1].to_broadcast([P, TILES, D]),
                                      ALU.mult).then_inc(masked[e % 2], 1)
                    if e:
                        turned_lo(i, 2 * (e - 1))
                        turned_lo(i, 2 * (e - 1) + 1)
                turned_lo(i, 2 * (E2 - 1))
                turned_lo(i, 2 * (E2 - 1) + 1)

            def turned_lo(i, n):
                u = HID_XM + n
                wait(dve, xm_hi, i * E2 * DK + n + 1)
                dve.tensor_tensor(xmT[1][:, n // DK, n % DK, :], hid[u % 2][:, :], xmT[0][:, n // DK, n % DK, :],
                                  ALU.subtract).then_inc(xm_lo, 1)

            def ffn(i):
                for c in range(C2):
                    wait(dve, g_hi, i * C2 + c + 1)
                    dve.scalar_tensor_tensor(out=gT[1][:, c, :], in0=g32[:, c % 2, :], scalar=up[:, 4:5],
                                             in1=gT[0][:, c, :], op0=ALU.mult, op1=ALU.subtract).then_inc(g_lo, 1)

            def ffn_out(i):
                wait(dve, x2_biased, 2 * i + 2)
                for j in range(TILES):
                    u = OUT_Y + j
                    wait(dve, out_ready[u % 2], i * OUT_USES[u % 2] + u // 2 + 1)
                    dve.scalar_tensor_tensor(out=yy[:, j, :], in0=outp[u % 2][:, 0:D], scalar=down[:, 5:6],
                                             in1=yy[:, j, :], op0=ALU.mult, op1=ALU.add).then_inc(y_summed, 1)

            def tail(i, what, j):
                if what == "stats":
                    wait(dve, y_summed, (i + 1) * TILES)
                    norm_stats("n3", i, yy, j)
                if what == "aggregate":
                    norm_aggregate("n3", i, 1e-12)
                if what == "normal":
                    norm_apply("n3", i, yy, z_ready)
                if what == "stats2":
                    wait(dve, z_beta, i + 1)
                    norm_stats("n4", i, yy, j)
                if what == "aggregate2":
                    norm_aggregate("n4", i, 1e-5)
                if what == "finish":
                    norm_apply("n4", i, yy, out_ready_sb)

            def step(i, a, t):
                for pos in range(POSITIONS):
                    n = pos // 2
                    if i is not None and pos % 2 == 0 and n < E1 * C1:
                        hidden(i, n)
                    if i is not None and pos % 2 == 1 and n >= LAG:
                        output(i, n - LAG)
                    if a is not None:
                        attention(a, pos)
                    if t is not None and pos in TAIL:
                        tail(t, *TAIL[pos])
                if i is not None:
                    second_norm(i)
                    route(i, a)
                if a is not None:
                    first_sum(a)
                    gates(a)
                if i is not None:
                    ffn(i)
                if a is not None:
                    x1_lo(a)
                if i is not None:
                    ffn_out(i)

            step(None, 0, None)
            step(0, 1, None)
            with dve.Fori(1, STEPS - 1) as i:
                step(i, i + 1, i - 1)
            step(STEPS - 1, None, STEPS - 2)
            for pos in sorted(TAIL):
                tail(STEPS - 1, *TAIL[pos])


def kernel(x, ctx_512, itok_BxS2xS_0_7, L0_attn_qkv_kernel, L0_attn_qkv_bias, L0_xattn_proj_in, L0_xattn_proj_out,
           L0_ffn_W_router, L0_ffn_W1, L0_ffn_b1, L0_ffn_Wo, L0_ffn_bo, L0_ffn_ln_gamma, L0_ffn_ln_beta):
    import numpy as np
    import concourse.bacc as bacc
    from concourse.bass_utils import run_bass_kernel_spmd

    ins = {
        "x": x, "ctx": ctx_512, "itok": itok_BxS2xS_0_7, "w_qkv": L0_attn_qkv_kernel, "b_qkv": L0_attn_qkv_bias,
        "p_in": np.transpose(np.asarray(L0_xattn_proj_in), (2, 0, 1)).reshape(D, E1 * I1),
        "p_out": np.transpose(np.asarray(L0_xattn_proj_out), (0, 2, 1)).reshape(E1 * I1, D),
        "w_router": np.transpose(np.asarray(L0_ffn_W_router)),
        "w_1": np.asarray(L0_ffn_W1).reshape(E2 * D, I2), "b_1": L0_ffn_b1, "w_o": L0_ffn_Wo, "b_o": L0_ffn_bo,
        "gamma": L0_ffn_ln_gamma, "beta": L0_ffn_ln_beta,
    }
    nc = bacc.Bacc("TRN2", target_bir_lowering=False, num_devices=1, dynamic_dma_scratch_size=1024)
    arrays, args = {}, {}
    for name, a in ins.items():
        a = np.ascontiguousarray(a)
        arrays[f"in_{name}"] = a
        args[name] = nc.dram_tensor(f"in_{name}", a.shape, mybir.dt.from_np(a.dtype), kind="ExternalInput").ap()
    out = nc.dram_tensor("out", tuple(np.shape(x)), F32, kind="ExternalOutput").ap()
    decoder_layer(nc, *[args[n] for n in ins], out)
    r = run_bass_kernel_spmd(nc, [arrays], core_ids=[0])
    return r.results[0]["out"]
```

```python
from contextlib import ExitStack

import concourse.bass as bass
from concourse import mybir

F32 = mybir.dt.float32
F16 = mybir.dt.float16
BF16 = mybir.dt.bfloat16
I32 = mybir.dt.int32
ALU = mybir.AluOpType
ACT = mybir.ActivationFunctionType
AX = mybir.AxisListType

P = 128
D = 256
DK = D // P
HEADS = 16
HD = D // HEADS
QKV = 3 * D
TILES = 2
T = TILES * P
E1 = 8
I1 = 512
C1 = I1 // P
E2 = 4
I2 = 1024
C2 = I2 // P
BANK = 512
SCORE_SCALE = (2.0 * D) ** -0.5
MASKED = -1.0e30

HIDDEN = E1 * C1 // 2
OUTPUTS = E1 * TILES
LAG = 3
LARGE = []
for _n in range(HIDDEN + LAG):
    if _n < HIDDEN:
        LARGE.append(("hidden", _n))
    if _n >= LAG:
        LARGE.append(("output", _n - LAG))
LARGE += [("ffn", _n) for _n in range(2 * C2)] + [("ffn_out", _n) for _n in range(2 * TILES)]
FFN_AT = HIDDEN + OUTPUTS
POSITIONS = len(LARGE)

TIMETABLE, AHEAD = {}, {}
for _l in LARGE:
    AHEAD[_l[0], 0, _l[1]] = -1 if _l[0] in ("ffn", "ffn_out") else 0


def _at(ahead, pos, name, j=0, n=0):
    TIMETABLE.setdefault(pos, []).append((name, j, n))
    AHEAD[name, j, n] = ahead


for _p, _name, _n in ((29, "x_T", 0), (30, "qkv", 0), (31, "qkv", 1), (31, "shuffle_out", 0), (32, "shuffle_in", 0),
                      (36, "hi", 0), (38, "rest", 0), (39, "mid", 0), (40, "lo", 0),
                      (42, "qk_T", 0), (44, "qk_T", 1), (47, "scores", 0), (48, "mask", 0), (48, "qk_T", 2),
                      (49, "qk_T", 3), (50, "exp", 0), (51, "exp", 1), (51, "scores", 1)):
    _at(2, _p, _name, 0, _n)
_at(2, 12, "x_load")
for _p, _name, _n in ((0, "mask", 1), (1, "P_T", 0), (2, "P_T", 1), (3, "exp", 2), (4, "PV", 0), (5, "exp", 3),
                      (5, "P_T", 2), (7, "P_T", 3), (9, "PV", 1), (9, "gather", 0)):
    _at(1, _p, _name, 0, _n)
for _p, _name, _n in ((9, "x_T", 0), (10, "qkv", 0), (11, "qkv", 1), (11, "shuffle_out", 0), (11, "shuffle_in", 0),
                      (16, "hi", 0), (17, "rest", 0), (18, "mid", 0), (19, "lo", 0),
                      (21, "qk_T", 0), (22, "qk_T", 1), (24, "scores", 0), (25, "mask", 0), (24, "qk_T", 2),
                      (25, "qk_T", 3), (26, "exp", 0), (27, "exp", 1), (27, "scores", 1), (28, "mask", 1),
                      (28, "P_T", 0), (29, "P_T", 1), (30, "exp", 2), (31, "exp", 3), (31, "PV", 0), (32, "P_T", 2),
                      (33, "P_T", 3), (34, "PV", 1), (35, "gather", 0)):
    _at(1, _p, _name, 1, _n)
_at(1, 28, "gate_load")
_at(1, 34, "gate_T", 0, 0)
_at(1, 35, "gate_T", 0, 1)
_at(1, 37, "gates", 0)
_at(1, 38, "gates", 1)
_at(1, 33, "residual")
_at(1, 41, "x1_sum")
_at(1, 42, "x1_norm")
_at(1, 45, "x1_T")
_at(0, 32, "x2_sum")
_at(0, 33, "x2_norm")
_at(0, 35, "logits")
_at(0, 36, "choose")
for _e, (_p, _q) in enumerate(((0, 10), (2, 13), (10, 15), (13, 20))):
    _at(-1, _p, "xm", 0, _e)
    _at(-1, _q, "xm_T", 0, _e)
_at(-1, 20, "oh_T")
_at(-1, 18, "x2_bias")
_at(-2, 1, "z_stats")
_at(-2, 3, "z_norm")
_at(-2, 7, "z_out_stats")
_at(-2, 9, "z_out_norm")
_at(-2, 10, "store")
assert max(TIMETABLE) < POSITIONS

TIMETABLE = {0: [('P_T', 0, 1), ('xm', 0, 0)], 1: [('exp', 0, 2), ('z_stats', 0, 0)], 2: [('xm', 0, 1)], 3: [('exp', 0, 3), ('PV', 0, 0), ('P_T', 0, 2), ('z_norm', 0, 0)], 5: [('P_T', 0, 3)], 7: [('PV', 0, 1), ('z_out_stats', 0, 0)], 9: [('x_T', 1, 0), ('z_out_norm', 0, 0), ('gather', 0, 0)], 10: [('qkv', 1, 0), ('qkv', 1, 1), ('xm', 0, 2), ('store', 0, 0)], 11: [('shuffle_out', 1, 0), ('shuffle_in', 1, 0)], 12: [('x_load', 0, 0), ('xm_T', 0, 0)], 13: [('xm', 0, 3)], 14: [('xm_T', 0, 1)], 16: [('xm_T', 0, 2), ('hi', 1, 0)], 18: [('x2_bias', 0, 0)], 19: [('rest', 1, 0)], 20: [('mid', 1, 0), ('oh_T', 0, 0), ('lo', 1, 0)], 21: [('xm_T', 0, 3)], 24: [('qk_T', 1, 1), ('qk_T', 1, 0)], 26: [('scores', 1, 0), ('qk_T', 1, 2), ('x_T', 0, 0)], 27: [('mask', 1, 0), ('qk_T', 1, 3)], 28: [('exp', 1, 0), ('mask', 1, 1), ('gate_load', 0, 0)], 29: [('scores', 1, 1), ('exp', 1, 1)], 30: [('qkv', 0, 0), ('P_T', 1, 0)], 31: [('P_T', 1, 1), ('shuffle_out', 0, 0), ('gate_T', 0, 0)], 32: [('shuffle_in', 0, 0), ('exp', 1, 2), ('x2_sum', 0, 0)], 33: [('residual', 0, 0), ('exp', 1, 3), ('x2_norm', 0, 0), ('PV', 1, 0)], 34: [('P_T', 1, 2), ('qkv', 0, 1), ('logits', 0, 0)], 35: [('P_T', 1, 3), ('gate_T', 0, 1)], 36: [('PV', 1, 1), ('hi', 0, 0), ('choose', 0, 0)], 37: [('gather', 1, 0), ('gates', 0, 0)], 38: [('rest', 0, 0), ('gates', 1, 0)], 39: [('mid', 0, 0)], 40: [('lo', 0, 0)], 41: [('x1_sum', 0, 0)], 42: [('qk_T', 0, 0), ('x1_norm', 0, 0)], 44: [('qk_T', 0, 1)], 45: [('x1_T', 0, 0), ('scores', 0, 0)], 46: [('mask', 0, 0), ('qk_T', 0, 2)], 47: [('qk_T', 0, 3), ('scores', 0, 1)], 48: [('exp', 0, 0)], 49: [('exp', 0, 1)], 50: [('mask', 0, 1)], 51: [('P_T', 0, 0)]}
AHEAD.update({('P_T', 0, 1): 1, ('xm', 0, 0): -1, ('exp', 0, 2): 1, ('z_stats', 0, 0): -2, ('xm', 0, 1): -1, ('exp', 0, 3): 1, ('PV', 0, 0): 1, ('P_T', 0, 2): 1, ('z_norm', 0, 0): -2, ('P_T', 0, 3): 1, ('PV', 0, 1): 1, ('z_out_stats', 0, 0): -2, ('x_T', 1, 0): 1, ('z_out_norm', 0, 0): -2, ('gather', 0, 0): 1, ('qkv', 1, 0): 1, ('qkv', 1, 1): 1, ('xm', 0, 2): -1, ('store', 0, 0): -2, ('shuffle_out', 1, 0): 1, ('shuffle_in', 1, 0): 1, ('x_load', 0, 0): 2, ('xm_T', 0, 0): -1, ('xm', 0, 3): -1, ('xm_T', 0, 1): -1, ('xm_T', 0, 2): -1, ('hi', 1, 0): 1, ('x2_bias', 0, 0): -1, ('rest', 1, 0): 1, ('mid', 1, 0): 1, ('oh_T', 0, 0): -1, ('lo', 1, 0): 1, ('xm_T', 0, 3): -1, ('qk_T', 1, 1): 1, ('qk_T', 1, 0): 1, ('scores', 1, 0): 1, ('qk_T', 1, 2): 1, ('x_T', 0, 0): 2, ('mask', 1, 0): 1, ('qk_T', 1, 3): 1, ('exp', 1, 0): 1, ('mask', 1, 1): 1, ('gate_load', 0, 0): 1, ('scores', 1, 1): 1, ('exp', 1, 1): 1, ('qkv', 0, 0): 2, ('P_T', 1, 0): 1, ('P_T', 1, 1): 1, ('shuffle_out', 0, 0): 2, ('gate_T', 0, 0): 1, ('shuffle_in', 0, 0): 2, ('exp', 1, 2): 1, ('x2_sum', 0, 0): 0, ('residual', 0, 0): 1, ('exp', 1, 3): 1, ('x2_norm', 0, 0): 0, ('PV', 1, 0): 1, ('P_T', 1, 2): 1, ('qkv', 0, 1): 2, ('logits', 0, 0): 0, ('P_T', 1, 3): 1, ('gate_T', 0, 1): 1, ('PV', 1, 1): 1, ('hi', 0, 0): 2, ('choose', 0, 0): 0, ('gather', 1, 0): 1, ('gates', 0, 0): 1, ('rest', 0, 0): 2, ('gates', 1, 0): 1, ('mid', 0, 0): 2, ('lo', 0, 0): 2, ('x1_sum', 0, 0): 1, ('qk_T', 0, 0): 2, ('x1_norm', 0, 0): 1, ('qk_T', 0, 1): 2, ('x1_T', 0, 0): 1, ('scores', 0, 0): 2, ('mask', 0, 0): 2, ('qk_T', 0, 2): 2, ('qk_T', 0, 3): 2, ('scores', 0, 1): 2, ('exp', 0, 0): 2, ('exp', 0, 1): 2, ('mask', 0, 1): 2, ('P_T', 0, 0): 2})

SMALL_USERS = ("x_T", "qkv", "qk_T", "P_T", "PV", "gate_T", "x1_T", "xm_T", "oh_T")
SMALL_ORDER = [k for _p in sorted(TIMETABLE) for k in TIMETABLE[_p] if k[0] in SMALL_USERS]
USE = {k: u for u, k in enumerate(SMALL_ORDER)}
HID_ORDER = [("hidden", 0, n) for n in range(HIDDEN)] + [("ffn", 0, n) for n in range(C2 // 2)]
OUT_ORDER = [("output", 0, n) for n in range(OUTPUTS)] + [("ffn_out", 0, n) for n in range(TILES)]
assert all(len(o) % 2 == 0 for o in (SMALL_ORDER, HID_ORDER, OUT_ORDER))

WCHUNK = 1024
WNAMES = ["pin", "pout", "w1", "wo"]
WPARTS = {"pin": 8, "pout": 8, "w1": 8, "wo": 2}
WCHUNKS = [c for _g in range(4) for c in (("pin", _g), ("pin", 4 + _g), ("pout", 2 * _g), ("pout", 2 * _g + 1))]
WCHUNKS += [("w1", _n) for _n in range(8)] + [("wo", _n) for _n in range(2)]
PLACE = {c: m for m, c in enumerate(WCHUNKS)}
TOP_COLUMN = {c: m for m, c in enumerate((_w, _n) for _w in WNAMES for _n in range(WPARTS[_w]))}
LOADS = 8


MAXIMA_AT = {(-2, 32 + 2 * _m): _m for _m in range(10)}
MAXIMA_AT.update({(-1, 2 * _m): 10 + _m for _m in range(16)})
SCALES_AT = (-1, 33)
B1_AT = {(-1, 41 + 3 * _n): _n for _n in range(3)}
PAIRS_AT = {(-1, 34 + _m): _m for _m in range(18)}
PAIRS_AT.update({(0, 3 + 5 * _m): 18 + _m for _m in range(8)})


def at(table, it, pos):
    return [table[it, pos]] if isinstance(it, int) and (it, pos) in table else []


def wait(eng, sem, value):
    if not (isinstance(value, int) and value <= 0):
        eng.wait_ge(sem, value)


def decoder_layer(nc, x, ctx, itok, w_qkv, b_qkv, p_in, p_out, w_router, w_1, b_1, w_o, b_o,
                  gamma, beta, out):
    STEPS = x.shape[0] // TILES

    def step_of(it, key):
        return it + AHEAD[key]

    def active(it, key):
        return not isinstance(it, int) or 0 <= step_of(it, key) < STEPS

    def pieces(it, pos):
        return [(*key, step_of(it, key)) for key in TIMETABLE.get(pos, []) if active(it, key)]

    def run_pipeline(eng, iteration):
        for it in (-2, -1, 0, 1):
            iteration(it)
        with eng.Fori(2, STEPS - 2) as it:
            iteration(it)
        for it in (STEPS - 2, STEPS - 1, STEPS, STEPS + 1):
            iteration(it)

    es = ExitStack()
    with es:
        def sb(name, shape, dt=F32):
            return es.enter_context(nc.sbuf_tensor(name, shape, dt))

        def ps(name, shape, dt=F32):
            return es.enter_context(nc.psum_tensor(name, shape, dt))

        def sem(name):
            return es.enter_context(nc.semaphore(name))

        qkv_dram = nc.dram_tensor("qkv_scratch", [TILES, P, QKV], F32, kind="Internal").ap()
        attn_dram = nc.dram_tensor("attn_scratch", [TILES, P, D], F32, kind="Internal").ap()

        weights = sb("weights", [P, len(WCHUNKS), 2, WCHUNK], F16)
        wqkv = sb("wqkv", [P, DK, QKV])
        b1p = sb("b1p", [P, I2], BF16)
        bqkv = sb("bqkv", [P, QKV])
        bo_r = sb("bo_r", [P, D])
        gamma_r = sb("gamma_r", [P, D])
        beta_r = sb("beta_r", [P, D])
        router_r = sb("router_r", [P, E2, D])
        ident = sb("ident", [P, P])
        ident16 = sb("ident16", [P, P], BF16)
        mask = sb("mask", [P, P])
        minus_half = sb("minus_half", [P, TILES])
        choice = sb("choice", [P, E2])
        tops = sb("tops", [P, len(WCHUNKS) + 1])
        top5 = sb("top5", [P, 8])
        top5a = sb("top5a", [P, 8])
        pow2 = sb("pow2", [P, 8])
        inv2 = sb("inv2", [P, 8])
        up = sb("up", [P, 8])
        down = sb("down", [P, 8])

        x_sb = sb("x_sb", [P, TILES, D])
        x1 = sb("x1", [P, TILES, D])
        x1T = [sb(f"x1T{k}", [P, DK, T], F16) for k in "hl"]
        acc_x2 = sb("acc_x2", [P, 2, TILES, D])
        acc, x2 = acc_x2[:, 0, :, :], acc_x2[:, 1, :, :]
        hT = [sb(f"hT{k}", [P, 2, C1, T], F16) for k in "hl"]
        gT = [h[:, :, :, :].rearrange("p a c t -> p (a c) t") for h in hT]
        xm = [sb(f"xm{b}", [P, TILES, D]) for b in range(2)]
        xmT = [sb(f"xmT{k}", [P, E2, DK, T], F16) for k in "hl"]
        gate = sb("gate", [P, TILES, E1])
        yy = sb("yy", [P, TILES, D])
        x2b = sb("x2b", [P, TILES, D])
        attn = sb("attn", [P, TILES, D])
        oh12 = sb("oh12", [P, TILES, P], BF16)
        ohT = sb("ohT", [P, T], BF16)
        logit = sb("logit", [P, TILES, E2])
        logit_top = sb("logit_top", [P, TILES])
        is_top = sb("is_top", [P, TILES, E2])
        index = sb("index", [P, TILES, E2])
        index_min = sb("index_min", [P, TILES])
        onehot = sb("onehot", [P, TILES, E2])
        qk6 = [sb(f"qk6{b}", [P, HEADS, 15, HD], BF16) for b in range(2)]
        prob = sb("prob", [P, 2, 8, P])
        qkT = sb("qkT", [P, 2, 8, P], BF16)
        ctx_sb = qkT[:, 0, :, :].rearrange("p h t -> p (h t)").bitcast(F32)[:, 0:T].rearrange("p (j k) -> p j k", j=TILES)
        tok_sb = qkT[:, 1, :, :].rearrange("p h t -> p (h t)").bitcast(I32)[:, 0:T].rearrange("p (j k) -> p j k", j=TILES)
        tokf = qkT[:, 1, :, :].rearrange("p h t -> p (h t)").bitcast(F32)[:, 0:T].rearrange("p (j k) -> p j k", j=TILES)
        PT = [sb(f"PT{k}", [P, 2, 4, P], F16) for k in "hl"]
        qkv_tok = sb("qkv_tok", [P, QKV])
        qkv_h = sb("qkv_h", [P, HEADS, 3, HD])
        ctxT = sb("ctxT", [P, TILES, P])
        tokT = sb("tokT", [P, TILES, P])
        rest = sb("rest", [P, HEADS, 3, HD])
        xT = sb("xT", [P, DK, P])
        g32 = sb("g32", [P, 2, T])
        neg_max = sb("neg_max", [P, 2, 8])
        row_sum = sb("row_sum", [P, 2, 8])
        row_inv = sb("row_inv", [P, 2, 8])
        pv = sb("pv", [P, 8, HD])
        attn_h = sb("attn_h", [P, HEADS, HD])
        junk = sb("junk", [P, 2, D])
        NORMS = ("n1", "n2", "n3", "n4")
        stats = {k: sb(f"stats_{k}", [P, TILES, 6]) for k in NORMS}
        mv = {k: sb(f"mv_{k}", [P, TILES, 2]) for k in NORMS}
        vare = {k: sb(f"vare_{k}", [P, TILES]) for k in NORMS}
        rstd = {k: sb(f"rstd_{k}", [P, TILES]) for k in NORMS}
        last_values = [h[:, :, :, :].rearrange("p a c t -> p (a c t)").bitcast(F32) for h in xmT]
        b1_sb = acc_x2[0:E2, :, :, :].rearrange("p a j d -> p (a j d)")
        b1_h = [t[0:E2, :, :].rearrange("p j d -> p (j d)").bitcast(BF16) for t in (xm[0], xm[1], yy)]

        hid = [ps(f"hid{b}", [P, BANK]) for b in range(2)]
        outp = [ps(f"outp{b}", [P, BANK]) for b in range(2)]
        score = ps("score", [P, 8, P])
        small = [ps(f"small{b}", [P, BANK]) for b in range(2)]

        const_pool = sem("const_pool")
        consts_loaded = sem("consts_loaded")
        chunk_loaded = [sem(f"chunk_loaded{b}") for b in range(LOADS)]
        tops_found = sem("tops_found")
        chunk_hi = sem("chunk_hi")
        chunk_lo = sem("chunk_lo")
        top_reduced = sem("top_reduced")
        scales = sem("scales")
        b1_steps = sem("b1_steps")
        b1_placed = sem("b1_placed")
        settled = sem("settled")
        x_loaded = sem("x_loaded")
        gates_loaded = sem("gates_loaded")
        turned = {k: sem(f"{k}_done") for k in SMALL_USERS}
        xT_copied = sem("xT_copied")
        qkv_biased = sem("qkv_biased")
        qkv_stored = sem("qkv_stored")
        qkv_reloaded = sem("qkv_reloaded")
        hi_written = sem("hi_written")
        rest_found = sem("rest_found")
        mid_written = sem("mid_written")
        lo_written = sem("lo_written")
        qkT_copied = sem("qkT_copied")
        scores_done = sem("scores_done")
        scores_masked = sem("scores_masked")
        max_found = sem("max_found")
        exps_done = sem("exps_done")
        sums_inverted = sem("sums_inverted")
        PT_hi = sem("PT_hi")
        PT_lo = sem("PT_lo")
        pv_summed = sem("pv_summed")
        attn_scaled = sem("attn_scaled")
        attn_stored = sem("attn_stored")
        attn_loaded = sem("attn_loaded")
        tok_cast = sem("tok_cast")
        gatesT = sem("gatesT")
        gate_summed = sem("gate_summed")
        gate_scaled = sem("gate_scaled")
        residual_loaded = sem("residual_loaded")
        x1_sum = sem("x1_sum")
        x1_ready = sem("x1_ready")
        x1T_hi = sem("x1T_hi")
        x1T_lo = sem("x1T_lo")
        n_stats = {k: sem(f"n_stats_{k}") for k in NORMS}
        n_aggr = {k: sem(f"n_aggr_{k}") for k in NORMS}
        n_eps = {k: sem(f"n_eps_{k}") for k in NORMS}
        n_rstd = {k: sem(f"n_rstd_{k}") for k in NORMS}
        hidden_done = sem("hidden_done")
        output_done = sem("output_done")
        ffn_done = sem("ffn_done")
        ffn_out_done = sem("ffn_out_done")
        h_hi = sem("h_hi")
        h_lo = sem("h_lo")
        o_summed = sem("o_summed")
        x2_sum = sem("x2_sum")
        x2_ready = sem("x2_ready")
        x2_biased = sem("x2_biased")
        logit_done = sem("logit_done")
        choice_steps = sem("choice_steps")
        masked = sem("masked")
        xm_hi = sem("xm_hi")
        xm_lo = sem("xm_lo")
        ohT_copied = sem("ohT_copied")
        gelu_done = sem("gelu_done")
        g_hi = sem("g_hi")
        g_lo = sem("g_lo")
        y_summed = sem("y_summed")
        z_ready = sem("z_ready")
        z_gamma = sem("z_gamma")
        z_beta = sem("z_beta")
        z_done = sem("z_done")
        out_stored = sem("out_stored")

        def chunk_dram(name, n):
            if name == "pin":
                return p_in.rearrange("(k p) n -> p k n", p=P)[:, n // 4, (n % 4) * WCHUNK:(n % 4 + 1) * WCHUNK]
            if name == "w1":
                return w_1.rearrange("(c p) n -> p c n", p=P)[:, n, :]
            return (p_out if name == "pout" else w_o).rearrange("(c p) n -> p c n", p=P)[:, 4 * n:4 * n + 4, :]

        def chunk_pair(m, part):
            return weights[:, m, part, :]

        def chunk_values(m):
            if m + 2 < len(WCHUNKS):
                return weights[:, m + 2, :, :].rearrange("p a n -> p (a n)").bitcast(F32)
            return last_values[m + 2 - len(WCHUNKS)]

        def pin(part, k, c0):
            c0 = k * E1 * I1 + c0
            return weights[:, PLACE["pin", c0 // WCHUNK], part, c0 % WCHUNK:c0 % WCHUNK + P]

        def w1(part, chunk, c0):
            return weights[:, PLACE["w1", chunk], part, c0:c0 + P]

        def second(name, part, c):
            return weights[:, PLACE[name, c // 4], part, (c % 4) * D:(c % 4 + 1) * D]

        def turned_value(s, key):
            name, j, n = key
            per = {"x_T": 1, "qkv": 2, "qk_T": 4, "P_T": 4, "PV": 2}
            if name in per:
                return s * TILES * per[name] + j * per[name] + n + 1
            return s * {"gate_T": 2, "x1_T": 1, "xm_T": E2, "oh_T": 1}[name] + n + 1

        def wait_turned(eng, s, key):
            wait(eng, turned[key[0]], turned_value(s, key))

        def read_of(s, key):
            name, j, n = key
            if name in turned:
                reader = {"x_T": xT_copied, "qkv": qkv_biased, "qk_T": qkT_copied, "P_T": PT_lo, "PV": pv_summed,
                          "gate_T": gatesT, "x1_T": x1T_lo, "xm_T": xm_lo, "oh_T": ohT_copied}[name]
                return reader, turned_value(s, key)
            return {"hidden": (h_lo, s * HIDDEN + n + 1), "ffn": (gelu_done, s * (C2 // 2) + n + 1),
                    "output": (o_summed, s * OUTPUTS + n + 1), "ffn_out": (y_summed, s * TILES + n + 1)}[name]

        def wait_bank(pe, it, order, key):
            u, back = order.index(key) - 2, 0
            while back < 3:
                if u < 0:
                    u, back = u + len(order), back + 1
                before = order[u]
                if active(it - back, before):
                    wait(pe, *read_of(step_of(it - back, before), before))
                    return
                u -= 2

        def small_of(key):
            return small[USE[key] % 2]

        def rows_of(t, s):
            return t.rearrange("(i j) s d -> i s j d", j=TILES)[s]

        def it_is(it, n):
            return isinstance(it, int) and it == n

        block = es.enter_context(nc.Block())

        @block.sync
        def _(sp):
            loads = [(wqkv[:, :, :], w_qkv.rearrange("(k p) n -> p k n", p=P)),
                     (bqkv[:, :], b_qkv[0, :].partition_broadcast(P)),
                     (b1_sb, b_1),
                     (router_r[:, :, :], w_router.partition_broadcast(P)),
                     (bo_r[:, :], b_o.partition_broadcast(P)),
                     (gamma_r[:, :], gamma.partition_broadcast(P)),
                     (beta_r[:, :], beta.partition_broadcast(P))]

            def load_weights(m):
                if m >= LOADS:
                    sp.wait_ge(tops_found, m - LOADS + 1)
                src = chunk_dram(*WCHUNKS[m])
                to = chunk_values(m)
                to = to if len(src.shape) == 2 else to.rearrange("p (c n) -> p c n", n=src.shape[-1])
                sp.dma_start(to, src).then_inc(chunk_loaded[m % LOADS], 16)

            def place_b1():
                for part in range(3):
                    sp.wait_ge(b1_steps, 2 + 2 * part)
                    sp.dma_start(b1p[E2 * part:E2 * part + E2, :], b1_h[part]).then_inc(b1_placed, 16)

            def iteration(it):
                for pos in range(POSITIONS):
                    if it_is(it, -2) and pos == 0:
                        for to, of in loads:
                            sp.dma_start(to, of).then_inc(consts_loaded, 16)
                        for m in range(LOADS):
                            load_weights(m)
                    for m in at(MAXIMA_AT, it, pos):
                        if m + LOADS < len(WCHUNKS):
                            load_weights(m + LOADS)
                    if it_is(it, 0) and pos == 30:
                        place_b1()
                    for name, j, n, s in pieces(it, pos):
                        if name == "x_load":
                            wait(sp, turned["x_T"], s * TILES)
                            sp.dma_start(x_sb[:, :, :], rows_of(x, s)).then_inc(x_loaded, 16)
                        if name == "residual":
                            wait(sp, x2_sum, s * TILES)
                            sp.dma_start(x1[:, :, :], rows_of(x, s)).then_inc(residual_loaded, 16)
                        if name == "shuffle_out":
                            wait(sp, qkv_biased, s * 2 * TILES + 2 * j + 2)
                            sp.dma_start(qkv_dram[j], qkv_tok[:, :]).then_inc(qkv_stored, 16)
                        if name == "shuffle_in":
                            wait(sp, rest_found, s * TILES + j)
                            sp.sem_inc(settled, 1)
                            wait(sp, qkv_stored, (s * TILES + j + 1) * 16)
                            sp.dma_start(qkv_h[:, :, :, :].rearrange("p h s e -> p h (s e)"),
                                         qkv_dram[j].rearrange("s (c f) -> (s c) f", c=HEADS)
                                         .rearrange("(h p) f -> p h f", h=HEADS)).then_inc(qkv_reloaded, 16)
                        if name == "gather":
                            wait(sp, attn_scaled, s * 2 * TILES + 2 * j + 2)
                            sp.dma_start(attn_dram[j].rearrange("s (c f) -> (s c) f", c=HEADS)
                                         .rearrange("(h p) f -> p h f", h=HEADS),
                                         attn_h[:, :, :]).then_inc(attn_stored, 16)
                            wait(sp, x1_sum, s * TILES)
                            sp.sem_inc(settled, 1)
                            wait(sp, attn_stored, (s * TILES + j + 1) * 16)
                            sp.dma_start(attn[:, j, :], attn_dram[j]).then_inc(attn_loaded, 16)
                        if name == "gate_load":
                            wait(sp, scores_done, (s + 1) * 2 * TILES)
                            sp.dma_start(ctx_sb, rows_of(ctx, s)).then_inc(gates_loaded, 16)
                            sp.dma_start(tok_sb, rows_of(itok, s)).then_inc(gates_loaded, 16)
                        if name == "store":
                            wait(sp, z_done, (s + 1) * TILES)
                            sp.dma_start(rows_of(out, s), yy[:, :, :]).then_inc(out_stored, 16)

            run_pipeline(sp, iteration)
            sp.wait_ge(out_stored, 16 * STEPS)

        @block.gpsimd
        def _(pool):
            pool.memset(ident[:, :], 0.0).then_inc(const_pool, 1)
            pool.memset(ident16[:, :], 0.0).then_inc(const_pool, 1)
            pool.memset(mask[:, :], 0.0).then_inc(const_pool, 1)
            pool.memset(minus_half[:, :], -0.5).then_inc(const_pool, 1)
            pool.memset(oh12[:, :, :], 0.0).then_inc(const_pool, 1)
            pool.memset(b1p[:, :], 0.0).then_inc(const_pool, 1)
            for e in range(E2):
                pool.memset(choice[:, e:e + 1], float(E2 + e)).then_inc(const_pool, 1)
            pool.memset(tops[:, :], 0.0).then_inc(const_pool, 1)
            pool.wait_ge(const_pool, 11)
            for m in (ident, ident16):
                pool.affine_select(out=m[:, :], in_=m[:, :], compare_op=ALU.not_equal, fill=1.0, base=0,
                                   pattern=[[-1, P]], channel_multiplier=1).then_inc(const_pool, 1)
            pool.affine_select(out=mask[:, :], in_=mask[:, :], compare_op=ALU.is_ge, fill=MASKED, base=0,
                               pattern=[[-1, P]], channel_multiplier=1).then_inc(const_pool, 1)
            pool.wait_ge(top_reduced, 1)
            pool.partition_all_reduce(top5a[:, 0:5], top5[:, 0:5], P, bass.bass_isa.ReduceOp.max).then_inc(scales, 1)
            pool.wait_ge(consts_loaded, 16 * 7)

            def rsqrt(k, s):
                wait(pool, n_eps[k], s + 1)
                pool.tensor_tensor(rstd[k][:, :], vare[k][:, :], minus_half[:, :], ALU.pow).then_inc(n_rstd[k], 1)

            def iteration(it):
                for pos in range(POSITIONS):
                    for name, j, n, s in pieces(it, pos):
                        if name == "gate_T" and n == 0:
                            wait(pool, gates_loaded, (s + 1) * 32)
                            pool.sem_inc(settled, 1)
                            pool.tensor_copy(tokf, tok_sb).then_inc(tok_cast, 1)
                        if name == "x1_norm":
                            rsqrt("n1", s)
                        if name == "x2_norm":
                            rsqrt("n2", s)
                        if name == "xm":
                            if n == 0:
                                wait(pool, choice_steps, (s + 1) * 6 - 1)
                            if n == 0 and it_is(it, 1):
                                pool.wait_ge(b1_placed, 48)
                            wait(pool, turned["xm_T"], s * E2 + n - 1)
                            pool.tensor_tensor(xm[n % 2][:, :, :], x2, onehot[:, :, n:n + 1].to_broadcast([P, TILES, D]),
                                               ALU.mult).then_inc(masked, 1)
                        if name == "x2_bias":
                            wait(pool, x2_ready, (s + 1) * TILES)
                            wait(pool, z_beta, s)
                            pool.tensor_tensor(x2b[:, :, :], x2, beta_r[:, None, :].to_broadcast([P, TILES, D]),
                                               ALU.add).then_inc(x2_biased, 1)
                            wait(pool, out_stored, s * 16)
                            if it_is(it, 1):
                                pool.wait_ge(b1_placed, 48)
                            pool.tensor_tensor(yy[:, :, :], x2, bo_r[:, None, :].to_broadcast([P, TILES, D]),
                                               ALU.add).then_inc(x2_biased, 1)
                        if name == "z_norm":
                            rsqrt("n3", s)
                            wait(pool, z_ready, (s + 1) * TILES)
                            pool.tensor_tensor(yy[:, :, :], yy[:, :, :], gamma_r[:, None, :].to_broadcast([P, TILES, D]),
                                               ALU.mult).then_inc(z_gamma, 1)
                            wait(pool, z_gamma, s + 1)
                            pool.tensor_tensor(yy[:, :, :], yy[:, :, :], x2b[:, :, :], ALU.add).then_inc(z_beta, 1)
                        if name == "z_out_norm":
                            rsqrt("n4", s)

            run_pipeline(pool, iteration)

        @block.scalar
        def _(act):
            def weight_hi(m):
                name = WCHUNKS[m][0]
                if m == 0:
                    act.wait_ge(scales, 6)
                wait(act, chunk_lo, m - 1)
                act.activation(chunk_pair(m, 0), chunk_values(m), ACT.Copy,
                               scale=up[:, WNAMES.index(name):WNAMES.index(name) + 1]).then_inc(chunk_hi, 1)

            def piece(name, j, n, s):
                key = (name, j, n)
                b = j % 2
                if name == "x_T":
                    wait_turned(act, s, key)
                    wait(act, turned["qkv"], s * 2 * TILES + 2 * j)
                    act.activation(xT[:, :, :].rearrange("p k s -> p (k s)"), small_of(key)[:, 0:D],
                                   ACT.Copy).then_inc(xT_copied, 1)
                if name == "hi":
                    wait(act, qkv_reloaded, (s * TILES + j + 1) * 16)
                    wait(act, turned["PV"], (s - 1) * 2 * TILES + 2 * j + 2)
                    q, k, v = (qkv_h[:, :, m, :] for m in range(3))
                    act.activation(qk6[b][:, :, 3:6, :], q[:, :, None, :].to_broadcast([P, HEADS, 3, HD]),
                                   ACT.Copy).then_inc(hi_written, 1)
                    act.activation(qk6[b][:, :, 6:11:2, :], k[:, :, None, :].to_broadcast([P, HEADS, 3, HD]),
                                   ACT.Copy).then_inc(hi_written, 1)
                    act.activation(qk6[b][:, :, 12, :], v, ACT.Copy).then_inc(hi_written, 1)
                if name == "mid":
                    wait(act, rest_found, s * TILES + j + 1)
                    q, k, v = (rest[:, :, m, :] for m in range(3))
                    act.activation(qk6[b][:, :, 0:2, :], q[:, :, None, :].to_broadcast([P, HEADS, 2, HD]),
                                   ACT.Copy).then_inc(mid_written, 1)
                    act.activation(qk6[b][:, :, 7:10:2, :], k[:, :, None, :].to_broadcast([P, HEADS, 2, HD]),
                                   ACT.Copy).then_inc(mid_written, 1)
                    act.activation(qk6[b][:, :, 14, :], v, ACT.Copy).then_inc(mid_written, 1)
                if name == "qk_T":
                    wait_turned(act, s, key)
                    wait(act, scores_done, s * 2 * TILES + 2 * j + n // 2)
                    if j == 0 and n < 2:
                        wait(act, turned["gate_T"], 2 * s)
                    act.activation(qkT[0:96, n % 2, :, :].rearrange("p h t -> p (h t)"),
                                   small_of(key)[0:96, :].bitcast(BF16), ACT.Copy).then_inc(qkT_copied, 1)
                if name == "exp":
                    h = n // 2
                    wait(act, max_found, s * 2 * TILES + 2 * j + h + 1)
                    wait(act, sums_inverted, s * 2 * TILES + 2 * (j - 1) + h + 1)
                    for g in range(4 * (n % 2), 4 * (n % 2) + 4):
                        act.activation(prob[:, h, g, :], prob[:, h, g, :], ACT.Exp, bias=neg_max[:, h, g:g + 1],
                                       scale=1.0, accum_out=row_sum[:, h, g:g + 1]).then_inc(exps_done, 1)
                if name == "P_T":
                    wait_turned(act, s, key)
                    act.activation(PT[0][:, n % 2, :, :].rearrange("p h t -> p (h t)"), small_of(key)[:, :],
                                   ACT.Copy).then_inc(PT_hi, 1)
                if name == "gate_T":
                    wait_turned(act, s, key)
                    wait(act, gate_summed, s * TILES * E1)
                    act.activation((ctxT, tokT)[n][:, :, :].rearrange("p j k -> p (j k)"), small_of(key)[:, 0:T],
                                   ACT.Copy).then_inc(gatesT, 1)
                if name == "x1_T":
                    wait_turned(act, s, key)
                    wait(act, hidden_done, s * HIDDEN)
                    act.activation(x1T[0][:, :, :].rearrange("p k t -> p (k t)"), small_of(key)[:, :],
                                   ACT.Copy).then_inc(x1T_hi, 1)
                if name == "xm_T":
                    wait_turned(act, s, key)
                    if it_is(s, 0) and n == 0:
                        act.wait_ge(chunk_lo, len(WCHUNKS))
                    wait(act, ffn_done, s * (C2 // 2))
                    act.activation(xmT[0][:, n, :, :].rearrange("p k t -> p (k t)"), small_of(key)[:, :],
                                   ACT.Copy).then_inc(xm_hi, 1)
                if name == "oh_T":
                    wait_turned(act, s, key)
                    act.activation(ohT[:, :], small_of(key)[:, 0:T // 2].bitcast(BF16), ACT.Copy).then_inc(ohT_copied, 1)

            def large(name, n, s):
                if name == "hidden":
                    e, half = n // 2, n % 2
                    wait(act, hidden_done, s * HIDDEN + n + 1)
                    if e >= 2:
                        wait(act, output_done, s * OUTPUTS + (e - 1) * TILES)
                    else:
                        wait(act, ffn_out_done, (s - 1) * TILES)
                    act.activation(hT[0][:, e % 2, 2 * half:2 * half + 2, :].rearrange("p c t -> p (c t)"),
                                   hid[n % 2][:, :], ACT.Relu).then_inc(h_hi, 1)
                if name == "ffn" and n % 4 == 3:
                    q = n // 4
                    wait(act, ffn_done, s * (C2 // 2) + q + 1)
                    wait(act, g_lo, s * (C2 // 2) + q)
                    act.activation(g32[:, :, :].rearrange("p c t -> p (c t)"), hid[q % 2][:, :], ACT.Gelu,
                                   scale=down[:, 2:3]).then_inc(gelu_done, 1)
                    wait(act, gelu_done, s * (C2 // 2) + q + 1)
                    act.activation(gT[0][:, 2 * q:2 * q + 2, :], g32[:, :, :], ACT.Copy, scale=up[:, 4:5]).then_inc(g_hi, 1)

            def iteration(it):
                for pos in range(POSITIONS):
                    for m in at(PAIRS_AT, it, pos):
                        weight_hi(m)
                    name, n = LARGE[pos]
                    if active(it, (name, 0, n)):
                        large(name, n, step_of(it, (name, 0, n)))
                    for p in pieces(it, pos):
                        piece(*p)

            run_pipeline(act, iteration)

        @block.tensor
        def _(pe):
            pe.wait_ge(const_pool, 14)
            pe.wait_ge(consts_loaded, 16 * 7)

            def piece(it, name, j, n, s):
                key = (name, j, n)
                b = j % 2
                if name == "scores":
                    wait(pe, qkT_copied, s * 4 * TILES + 4 * j + 2 * n + 2)
                    wait(pe, scores_masked, s * 2 * TILES + 2 * j + n)
                    for g in range(8):
                        mm = pe.matmul(score[:, g, :], qkT[0:96, g // 4, 2 * (g % 4), :], qkT[0:96, g // 4, 2 * (g % 4) + 1, :],
                                       start=True, stop=True)
                    mm.then_inc(scores_done, 1)
                if key not in USE:
                    return
                bank = small_of(key)
                if name == "x_T":
                    wait(pe, x_loaded, (s + 1) * 16)
                if name == "qkv":
                    wait(pe, xT_copied, s * TILES + j + 1)
                if name == "qk_T":
                    wait(pe, lo_written, s * 2 * TILES + 2 * j + 2)
                if name == "P_T":
                    wait(pe, exps_done, s * 16 * TILES + 16 * j + 4 * n + 4)
                if name == "PV":
                    wait(pe, PT_lo, s * 4 * TILES + 4 * j + 2 * n + 2)
                if name == "gate_T":
                    wait(pe, *((gates_loaded, (s + 1) * 32), (tok_cast, s + 1))[n])
                if name == "x1_T":
                    wait(pe, x1_ready, (s + 1) * TILES)
                if name == "xm_T":
                    wait(pe, masked, s * E2 + n + 1)
                if name == "oh_T":
                    wait(pe, choice_steps, (s + 1) * 6)
                wait_bank(pe, it, SMALL_ORDER, key)
                if name == "x_T":
                    for k in range(DK):
                        mm = pe.transpose(bank[:, k * P:(k + 1) * P], x_sb[:, j, k * P:(k + 1) * P], ident[:, :])
                if name == "qkv":
                    c0, c1 = (0, BANK) if n == 0 else (BANK, QKV)
                    for k in range(DK):
                        mm = pe.matmul(bank[:, 0:c1 - c0], xT[:, k, :], wqkv[:, k, c0:c1], start=(k == 0), stop=(k == DK - 1))
                if name == "qk_T":
                    for g in range(4):
                        flat = qk6[b][:, 4 * n + g, :, :].rearrange("p s e -> p (s e)")
                        for half in range(2):
                            m = 2 * g + half
                            mm = pe.transpose(bank[:, :].bitcast(BF16)[0:96, m * P:(m + 1) * P],
                                              flat[:, 96 * half:96 * half + 96], ident16[:, :])
                if name == "P_T":
                    for g in range(4):
                        mm = pe.transpose(bank[:, g * P:(g + 1) * P], prob[:, n // 2, 4 * (n % 2) + g, :], ident[:, :])
                if name == "PV":
                    for g in range(8):
                        v3 = qk6[b][:, 8 * n + g, 12:15, :].rearrange("p s e -> p (s e)")
                        for part in range(2):
                            mm = pe.matmul(bank[:, 48 * g:48 * g + 48], PT[part][:, g // 4, g % 4, :], v3,
                                           start=(part == 0), stop=(part == 1))
                if name == "gate_T":
                    for t in range(TILES):
                        mm = pe.transpose(bank[:, t * P:(t + 1) * P], (ctx_sb, tokf)[n][:, t, :], ident[:, :])
                if name == "x1_T" or name == "xm_T":
                    src = x1 if name == "x1_T" else xm[n % 2]
                    for k in range(DK):
                        for t in range(TILES):
                            c = k * T + t * P
                            mm = pe.transpose(bank[:, c:c + P], src[:, t, k * P:(k + 1) * P], ident[:, :])
                if name == "oh_T":
                    for t in range(TILES):
                        mm = pe.transpose(bank[:, 0:T // 2].bitcast(BF16)[:, t * P:(t + 1) * P], oh12[:, t, :], ident16[:, :])
                mm.then_inc(turned[name], 1)

            PAIRS = ((0, 0), (1, 0), (0, 1))

            def hidden(it, n, s):
                e, half = n // 2, n % 2
                if n == 0:
                    wait(pe, x1T_lo, s + 1)
                if n % 4 == 0 and it_is(it, 0):
                    pe.wait_ge(chunk_lo, PLACE["pin", 4 + n // 4] + 1)
                wait_bank(pe, it, HID_ORDER, ("hidden", 0, n))
                terms = [(k, w, v) for k in range(DK) for w, v in PAIRS]
                for c in range(2):
                    first = e * I1 + (2 * half + c) * P
                    for m, (k, w, v) in enumerate(terms):
                        mm = pe.matmul(hid[n % 2][:, c * T:(c + 1) * T], pin(w, k, first), x1T[v][:, k, :],
                                       start=(m == 0), stop=(m == len(terms) - 1))
                mm.then_inc(hidden_done, 1)

            def output(it, n, s):
                e, j = n // TILES, n % TILES
                if j == 0 and it_is(it, 0):
                    pe.wait_ge(chunk_lo, PLACE["pout", e] + 1)
                if j == 0:
                    wait(pe, h_lo, s * HIDDEN + 2 * (e + 1))
                wait_bank(pe, it, OUT_ORDER, ("output", 0, n))
                terms = [(c, v, w) for c in range(C1) for w, v in PAIRS]
                for m, (c, v, w) in enumerate(terms):
                    mm = pe.matmul(outp[n % 2][:, 0:D], hT[w][:, e % 2, c, j * P:(j + 1) * P], second("pout", v, e * C1 + c),
                                   start=(m == 0), stop=(m == len(terms) - 1))
                mm.then_inc(output_done, 1)

            def ffn(it, n, s):
                c, second = n // 2, n % 2
                if n == 0:
                    if it_is(it, 1):
                        pe.wait_ge(chunk_lo, len(WCHUNKS))
                        pe.wait_ge(b1_placed, 48)
                    wait(pe, ohT_copied, s + 1)
                    wait(pe, xm_lo, (s + 1) * E2)
                if n % 4 == 0:
                    wait_bank(pe, it, HID_ORDER, ("ffn", 0, n // 4))
                to = hid[(c // 2) % 2][:, (c % 2) * T:(c % 2 + 1) * T]
                if not second:
                    pe.matmul(to, b1p[:, c * P:(c + 1) * P], ohT[:, :], start=True, stop=False)
                terms = [(e, k, w, v) for e in (range(2, E2) if second else range(2)) for k in range(DK) for w, v in PAIRS]
                for m, (e, k, w, v) in enumerate(terms):
                    mm = pe.matmul(to, w1(w, e * DK + k, c * P), xmT[v][:, e, k, :],
                                   start=False, stop=(second == 1 and m == len(terms) - 1))
                if n % 4 == 3:
                    mm.then_inc(ffn_done, 1)

            def ffn_out(it, n, s):
                j, half = n // 2, n % 2
                if half == 0:
                    wait_bank(pe, it, OUT_ORDER, ("ffn_out", 0, j))
                for c in range(half * C2 // 2, (half + 1) * C2 // 2):
                    if j == 0 and c % 2 == 0:
                        wait(pe, g_lo, s * (C2 // 2) + c // 2 + 1)
                    for p, (w, v) in enumerate(PAIRS):
                        mm = pe.matmul(outp[j % 2][:, 0:D], gT[w][:, c, j * P:(j + 1) * P], second("wo", v, c),
                                       start=(c == 0 and p == 0), stop=(c == C2 - 1 and p == 2))
                if half == 1:
                    mm.then_inc(ffn_out_done, 1)

            def iteration(it):
                for pos in range(POSITIONS):
                    name, n = LARGE[pos]
                    if active(it, (name, 0, n)):
                        {"hidden": hidden, "output": output, "ffn": ffn, "ffn_out": ffn_out}[name](
                            it, n, step_of(it, (name, 0, n)))
                    for p in pieces(it, pos):
                        piece(it, *p)

            run_pipeline(pe, iteration)

        @block.vector
        def _(dve):
            dve.wait_ge(const_pool, 14)
            dve.wait_ge(consts_loaded, 16 * 7)

            def weight_top(m):
                dve.wait_ge(chunk_loaded[m % LOADS], 16 * (m // LOADS + 1))
                to = TOP_COLUMN[WCHUNKS[m]]
                dve.tensor_reduce(tops[:, to:to + 1], chunk_values(m), AX.X, ALU.max,
                                  apply_absolute_value=True).then_inc(tops_found, 1)

            def weight_lo(m):
                name = WCHUNKS[m][0]
                dve.wait_ge(chunk_hi, m + 1)
                dve.scalar_tensor_tensor(out=chunk_pair(m, 1), in0=chunk_values(m),
                                         scalar=up[:, WNAMES.index(name):WNAMES.index(name) + 1],
                                         in1=chunk_pair(m, 0), op0=ALU.mult, op1=ALU.subtract).then_inc(chunk_lo, 1)

            def find_scales():
                K = len(WCHUNKS)
                dve.tensor_reduce(tops[0:E2, K:K + 1], b1_sb, AX.X, ALU.max, apply_absolute_value=True).then_inc(tops_found, 1)
                dve.wait_ge(tops_found, K + 1)
                dve.tensor_reduce(top5[:, 0:3], tops[:, 0:24].rearrange("p (w n) -> p w n", n=8), AX.X, ALU.max)
                dve.tensor_reduce(top5[:, 3:4], tops[:, 24:26], AX.X, ALU.max)
                dve.tensor_copy(top5[:, 4:5], tops[:, K:K + 1]).then_inc(top_reduced, 1)
                dve.wait_ge(scales, 1)
                dve.scalar_tensor_tensor(out=top5a[:, 4:5], in0=top5a[:, 2:3], scalar=float(D), in1=top5a[:, 4:5],
                                         op0=ALU.mult, op1=ALU.add).then_inc(scales, 1)
                dve.wait_ge(scales, 2)
                dve.tensor_scalar(pow2[:, 0:5], top5a[:, 0:5], 2.0 ** -40, None, ALU.max).then_inc(scales, 1)
                dve.wait_ge(scales, 3)
                bits = pow2[:, 0:5].bitcast(I32)
                dve.tensor_scalar(bits, bits, 0x7F800000, None, ALU.bitwise_and).then_inc(scales, 1)
                dve.wait_ge(scales, 4)
                dve.reciprocal(inv2[:, 0:5], pow2[:, 0:5]).then_inc(scales, 1)
                dve.wait_ge(scales, 5)
                for c0, c1, f in ((0, 4, 2.0 ** 6), (4, 5, 2.0 ** 14)):
                    dve.tensor_scalar(down[:, c0:c1], pow2[:, c0:c1], 1.0 / f, None, ALU.mult)
                    last = dve.tensor_scalar(up[:, c0:c1], inv2[:, c0:c1], f, None, ALU.mult)
                last.then_inc(scales, 1)
                dve.wait_ge(scales, 6)
                dve.tensor_tensor(down[:, 5:6], down[:, 3:4], down[:, 4:5], ALU.mult)
                dve.tensor_scalar(b1_sb, b1_sb, up[0:E2, 2:3], None, ALU.mult).then_inc(b1_steps, 1)

            def b1_part(part):
                dve.wait_ge(b1_steps, 1 + 2 * part)
                dve.tensor_copy(b1_h[part], b1_sb).then_inc(b1_steps, 1)
                if part < 2:
                    dve.wait_ge(b1_steps, 2 + 2 * part)
                    dve.tensor_tensor(b1_sb, b1_sb, b1_h[part], ALU.subtract).then_inc(b1_steps, 1)
                else:
                    dve.wait_ge(b1_steps, 6)

            def norm_stats(k, s, src):
                for j in range(TILES):
                    dve.bn_stats(stats[k][:, j, :], src[:, j, :]).then_inc(n_stats[k], 1)

            def norm_aggregate(k, s, eps):
                wait(dve, n_stats[k], (s + 1) * TILES)
                dve.sem_inc(settled, 1)
                for j in range(TILES):
                    last = dve.bn_aggr(mv[k][:, j, :], stats[k][:, j, :])
                last.then_inc(n_aggr[k], 1)
                wait(dve, n_aggr[k], s + 1)
                dve.tensor_scalar(vare[k][:, :], mv[k][:, :, 1], eps, None, ALU.add).then_inc(n_eps[k], 1)

            def norm_apply(k, s, to, of, done):
                wait(dve, n_rstd[k], s + 1)
                for j in range(TILES):
                    dve.tensor_scalar(to[:, j, :], of[:, j, :], mv[k][:, j, 0:1], rstd[k][:, j:j + 1],
                                      ALU.subtract, ALU.mult).then_inc(done, 1)

            def piece(name, j, n, s):
                key = (name, j, n)
                b = j % 2
                if name == "qkv":
                    wait_turned(dve, s, key)
                    wait(dve, qkv_stored, (s * TILES + j) * 16)
                    c0, c1 = (0, BANK) if n == 0 else (BANK, QKV)
                    dve.tensor_tensor(qkv_tok[:, c0:c1], small_of(key)[:, 0:c1 - c0], bqkv[:, c0:c1],
                                      ALU.add).then_inc(qkv_biased, 1)
                if name == "rest":
                    wait(dve, hi_written, s * 3 * TILES + 3 * j + 3)
                    wait(dve, mid_written, s * 3 * TILES + 3 * j)
                    wait(dve, lo_written, s * 2 * TILES + 2 * j)
                    dve.tensor_tensor(rest[:, :, :, :], qkv_h[:, :, :, :], qk6[b][:, :, 4:13:4, :],
                                      ALU.subtract).then_inc(rest_found, 1)
                if name == "lo":
                    wait(dve, mid_written, s * 3 * TILES + 3 * j + 3)
                    dve.tensor_tensor(qk6[b][:, :, 2:12:9, :], rest[:, :, 0:2, :], qk6[b][:, :, 0:8:7, :],
                                      ALU.subtract).then_inc(lo_written, 1)
                    dve.tensor_tensor(qk6[b][:, :, 13, :], rest[:, :, 2, :], qk6[b][:, :, 14, :],
                                      ALU.subtract).then_inc(lo_written, 1)
                if name == "mask":
                    wait(dve, scores_done, s * 2 * TILES + 2 * j + n + 1)
                    wait(dve, turned["P_T"], s * 4 * TILES + 4 * (j - 1) + 2 * n + 2)
                    dve.scalar_tensor_tensor(out=prob[:, n, :, :], in0=score[:, :, :], scalar=SCORE_SCALE,
                                             in1=mask[:, None, :].to_broadcast([P, 8, P]),
                                             op0=ALU.mult, op1=ALU.add).then_inc(scores_masked, 1)
                    wait(dve, scores_masked, s * 2 * TILES + 2 * j + n + 1)
                    wait(dve, exps_done, s * 16 * TILES + 16 * (j - 1) + 8 * n + 8)
                    dve.tensor_reduce(neg_max[:, n, :], prob[:, n, :, :], AX.X, ALU.max,
                                      negate=True).then_inc(max_found, 1)
                if name == "P_T":
                    wait(dve, PT_hi, s * 4 * TILES + 4 * j + n + 1)
                    dve.tensor_tensor(PT[1][:, n % 2, :, :].rearrange("p h t -> p (h t)"), small_of(key)[:, :],
                                      PT[0][:, n % 2, :, :].rearrange("p h t -> p (h t)"),
                                      ALU.subtract).then_inc(PT_lo, 1)
                if name == "PV":
                    wait(dve, exps_done, s * 16 * TILES + 16 * j + 8 * n + 8)
                    dve.reciprocal(row_inv[:, n, :], row_sum[:, n, :]).then_inc(sums_inverted, 1)
                    wait_turned(dve, s, key)
                    wait(dve, attn_scaled, s * 2 * TILES + 2 * j + n)
                    dve.tensor_reduce(pv[:, :, :], small_of(key)[:, 0:384].rearrange("p (h c e) -> p h e c", h=8, c=3),
                                      AX.X, ALU.add).then_inc(pv_summed, 1)
                    wait(dve, pv_summed, s * 2 * TILES + 2 * j + n + 1)
                    wait(dve, attn_stored, (s * TILES + j) * 16)
                    dve.tensor_tensor(attn_h[:, 8 * n:8 * n + 8, :], pv[:, :, :],
                                      row_inv[:, n, :, None].to_broadcast([P, 8, HD]),
                                      ALU.mult).then_inc(attn_scaled, 1)
                if name == "gates":
                    wait(dve, gatesT, (s + 1) * 2)
                    wait(dve, o_summed, s * OUTPUTS)
                    wait(dve, gate_scaled, s * TILES + j)
                    for e in range(E1):
                        wait(dve, gate_summed, s * TILES * E1 + j * E1 + e - 1)
                        dve.scalar_tensor_tensor(out=junk[:, e % 2, 0:P], in0=tokT[:, j, :], scalar=float(e),
                                                 in1=ctxT[:, j, :], op0=ALU.is_equal, op1=ALU.mult,
                                                 accum_out=gate[:, j, e:e + 1]).then_inc(gate_summed, 1)
                    wait(dve, gate_summed, s * TILES * E1 + (j + 1) * E1)
                    dve.tensor_scalar(gate[:, j, :], gate[:, j, :], down[:, 0:1], None, ALU.mult).then_inc(gate_scaled, 1)
                if name == "x1_sum":
                    wait(dve, attn_loaded, (s + 1) * TILES * 16)
                    wait(dve, residual_loaded, (s + 1) * 16)
                    for t in range(TILES):
                        dve.tensor_tensor(x1[:, t, :], x1[:, t, :], attn[:, t, :], ALU.add).then_inc(x1_sum, 1)
                    wait(dve, x1_sum, (s + 1) * TILES)
                    norm_stats("n1", s, x1)
                if name == "x1_norm":
                    norm_aggregate("n1", s, 1e-5)
                    norm_apply("n1", s, x1, x1, x1_ready)
                if name == "x1_T":
                    wait(dve, x1T_hi, s + 1)
                    dve.tensor_tensor(x1T[1][:, :, :].rearrange("p k t -> p (k t)"), small_of(key)[:, :],
                                      x1T[0][:, :, :].rearrange("p k t -> p (k t)"), ALU.subtract).then_inc(x1T_lo, 1)
                if name == "x2_sum":
                    wait(dve, o_summed, (s + 1) * OUTPUTS)
                    for t in range(TILES):
                        dve.scalar_tensor_tensor(out=acc[:, t, :], in0=acc[:, t, :], scalar=down[:, 1:2], in1=x1[:, t, :],
                                                 op0=ALU.mult, op1=ALU.add).then_inc(x2_sum, 1)
                    wait(dve, x2_sum, (s + 1) * TILES)
                    norm_stats("n2", s, acc)
                if name == "x2_norm":
                    norm_aggregate("n2", s, 1e-5)
                    wait(dve, x2_biased, 2 * s)
                    wait(dve, masked, s * E2)
                    norm_apply("n2", s, x2, acc, x2_ready)
                if name == "logits":
                    wait(dve, x2_ready, (s + 1) * TILES)
                    for t in range(TILES):
                        for e in range(E2):
                            wait(dve, logit_done, s * TILES * E2 + t * E2 + e - 1)
                            dve.tensor_tensor_reduce(junk[:, e % 2, :], x2[:, t, :], router_r[:, e, :], 1.0, 0.0,
                                                     ALU.mult, ALU.add, logit[:, t, e:e + 1]).then_inc(logit_done, 1)
                if name == "choose":
                    choose(s)
                if name == "xm_T":
                    wait(dve, xm_hi, s * E2 + n + 1)
                    dve.tensor_tensor(xmT[1][:, n, :, :].rearrange("p k t -> p (k t)"), small_of(key)[:, :],
                                      xmT[0][:, n, :, :].rearrange("p k t -> p (k t)"), ALU.subtract).then_inc(xm_lo, 1)
                if name == "z_stats":
                    wait(dve, y_summed, (s + 1) * TILES)
                    norm_stats("n3", s, yy)
                    norm_aggregate("n3", s, 1e-12)
                if name == "z_norm":
                    norm_apply("n3", s, yy, yy, z_ready)
                if name == "z_out_stats":
                    wait(dve, z_beta, s + 1)
                    norm_stats("n4", s, yy)
                    norm_aggregate("n4", s, 1e-5)
                if name == "z_out_norm":
                    norm_apply("n4", s, yy, yy, z_done)

            def choose(s):
                wait(dve, logit_done, (s + 1) * TILES * E2)
                dve.tensor_reduce(logit_top[:, :], logit[:, :, :], AX.X, ALU.max).then_inc(choice_steps, 1)
                wait(dve, choice_steps, s * 6 + 1)
                dve.tensor_tensor(is_top[:, :, :], logit[:, :, :], logit_top[:, :, None].to_broadcast([P, TILES, E2]),
                                  ALU.is_ge).then_inc(choice_steps, 1)
                wait(dve, choice_steps, s * 6 + 2)
                dve.scalar_tensor_tensor(out=index[:, :, :], in0=is_top[:, :, :], scalar=-float(E2),
                                         in1=choice[:, None, :].to_broadcast([P, TILES, E2]),
                                         op0=ALU.mult, op1=ALU.add).then_inc(choice_steps, 1)
                wait(dve, choice_steps, s * 6 + 3)
                dve.tensor_reduce(index_min[:, :], index[:, :, :], AX.X, ALU.min).then_inc(choice_steps, 1)
                wait(dve, choice_steps, s * 6 + 4)
                dve.tensor_tensor(onehot[:, :, :], index[:, :, :], index_min[:, :, None].to_broadcast([P, TILES, E2]),
                                  ALU.is_equal).then_inc(choice_steps, 1)
                wait(dve, choice_steps, s * 6 + 5)
                wait(dve, turned["oh_T"], s)
                dve.tensor_copy(oh12[:, :, 0:3 * E2].rearrange("p j (c e) -> p j c e", c=3),
                                onehot[:, :, None, :].to_broadcast([P, TILES, 3, E2])).then_inc(choice_steps, 1)

            def large(name, n, s):
                if name == "hidden":
                    e, half = n // 2, n % 2
                    wait(dve, h_hi, s * HIDDEN + n + 1)
                    chunk = (slice(None), e % 2, slice(2 * half, 2 * half + 2), slice(None))
                    dve.scalar_tensor_tensor(out=hT[1][chunk].rearrange("p c t -> p (c t)"), in0=hid[n % 2][:, :], scalar=0.0,
                                             in1=hT[0][chunk].rearrange("p c t -> p (c t)"),
                                             op0=ALU.max, op1=ALU.subtract).then_inc(h_lo, 1)
                if name == "output":
                    e, j = n // TILES, n % TILES
                    if n == 0:
                        wait(dve, gate_scaled, (s + 1) * TILES)
                        wait(dve, x2_ready, s * TILES)
                    wait(dve, output_done, s * OUTPUTS + n + 1)
                    if e == 0:
                        dve.tensor_scalar(acc[:, j, :], outp[n % 2][:, 0:D], gate[:, j, e:e + 1], None,
                                          ALU.mult).then_inc(o_summed, 1)
                    else:
                        wait(dve, o_summed, s * OUTPUTS + n - TILES + 1)
                        dve.scalar_tensor_tensor(out=acc[:, j, :], in0=outp[n % 2][:, 0:D], scalar=gate[:, j, e:e + 1],
                                                 in1=acc[:, j, :], op0=ALU.mult, op1=ALU.add).then_inc(o_summed, 1)
                if name == "ffn" and n % 4 == 3:
                    q = n // 4
                    wait(dve, g_hi, s * (C2 // 2) + q + 1)
                    dve.scalar_tensor_tensor(out=gT[1][:, 2 * q:2 * q + 2, :], in0=g32[:, :, :], scalar=up[:, 4:5],
                                             in1=gT[0][:, 2 * q:2 * q + 2, :], op0=ALU.mult, op1=ALU.subtract).then_inc(g_lo, 1)
                if name == "ffn_out" and n % 2:
                    j = n // 2
                    if j == 0:
                        wait(dve, x2_biased, 2 * s + 2)
                    wait(dve, ffn_out_done, s * TILES + j + 1)
                    dve.scalar_tensor_tensor(out=yy[:, j, :], in0=outp[j % 2][:, 0:D], scalar=down[:, 5:6],
                                             in1=yy[:, j, :], op0=ALU.mult, op1=ALU.add).then_inc(y_summed, 1)

            def iteration(it):
                for pos in range(POSITIONS):
                    for m in at(MAXIMA_AT, it, pos):
                        weight_top(m)
                    for m in at(PAIRS_AT, it, pos):
                        weight_lo(m)
                    if it_is(it, SCALES_AT[0]) and pos == SCALES_AT[1]:
                        find_scales()
                    for part in at(B1_AT, it, pos):
                        b1_part(part)
                    name, n = LARGE[pos]
                    if active(it, (name, 0, n)):
                        large(name, n, step_of(it, (name, 0, n)))
                    for p in pieces(it, pos):
                        piece(*p)

            run_pipeline(dve, iteration)


def kernel(x, ctx_512, itok_BxS2xS_0_7, L0_attn_qkv_kernel, L0_attn_qkv_bias, L0_xattn_proj_in, L0_xattn_proj_out,
           L0_ffn_W_router, L0_ffn_W1, L0_ffn_b1, L0_ffn_Wo, L0_ffn_bo, L0_ffn_ln_gamma, L0_ffn_ln_beta):
    import numpy as np
    import concourse.bacc as bacc
    from concourse.bass_utils import run_bass_kernel_spmd

    ins = {
        "x": x, "ctx": ctx_512, "itok": itok_BxS2xS_0_7, "w_qkv": L0_attn_qkv_kernel, "b_qkv": L0_attn_qkv_bias,
        "p_in": np.transpose(np.asarray(L0_xattn_proj_in), (2, 0, 1)).reshape(D, E1 * I1),
        "p_out": np.transpose(np.asarray(L0_xattn_proj_out), (0, 2, 1)).reshape(E1 * I1, D),
        "w_router": np.transpose(np.asarray(L0_ffn_W_router)),
        "w_1": np.asarray(L0_ffn_W1).reshape(E2 * D, I2), "b_1": L0_ffn_b1, "w_o": L0_ffn_Wo, "b_o": L0_ffn_bo,
        "gamma": L0_ffn_ln_gamma, "beta": L0_ffn_ln_beta,
    }
    nc = bacc.Bacc("TRN2", target_bir_lowering=False, num_devices=1, dynamic_dma_scratch_size=1024)
    arrays, args = {}, {}
    for name, a in ins.items():
        a = np.ascontiguousarray(a)
        arrays[f"in_{name}"] = a
        args[name] = nc.dram_tensor(f"in_{name}", a.shape, mybir.dt.from_np(a.dtype), kind="ExternalInput").ap()
    out = nc.dram_tensor("out", tuple(np.shape(x)), F32, kind="ExternalOutput").ap()
    decoder_layer(nc, *[args[n] for n in ins], out)
    r = run_bass_kernel_spmd(nc, [arrays], core_ids=[0])
    return r.results[0]["out"]
```

```python
from contextlib import ExitStack

import concourse.bass as bass
from concourse import mybir

F32 = mybir.dt.float32
F16 = mybir.dt.float16
BF16 = mybir.dt.bfloat16
I32 = mybir.dt.int32
ALU = mybir.AluOpType
ACT = mybir.ActivationFunctionType
AX = mybir.AxisListType

P = 128
D = 256
DK = D // P
HEADS = 16
HD = D // HEADS
QKV = 3 * D
TILES = 2
T = TILES * P
E1 = 8
I1 = 512
C1 = I1 // P
E2 = 4
I2 = 1024
C2 = I2 // P
BANK = 512
SCORE_SCALE = (2.0 * D) ** -0.5
MASKED = -1.0e30
X_SCALE = 2.0 ** 6
PAIRS = ((0, 0), (1, 0), (0, 1))

HIDDEN = E1 * C1 // 2
OUTPUTS = E1 * TILES
LAG = 3
LARGE = []
for _n in range(HIDDEN + LAG):
    if _n < HIDDEN:
        LARGE.append(("hidden", _n))
    if _n >= LAG:
        LARGE.append(("output", _n - LAG))
LARGE += [("ffn", _n) for _n in range(2 * C2)] + [("ffn_out", _n) for _n in range(2 * TILES)]
FFN_AT = HIDDEN + OUTPUTS
POSITIONS = len(LARGE)

TIMETABLE = {
    0: [("xm", 0, 0, -1)],
    1: [("P_T", 0, 0, 1), ("P_T", 0, 1, 1), ("z_stats", 0, 0, -2)],
    2: [("exp", 0, 2, 1), ("xm", 0, 1, -1)],
    3: [("PV", 0, 0, 1), ("z_norm", 0, 0, -2)],
    4: [("exp", 0, 3, 1), ("P_T", 0, 2, 1)],
    6: [("P_T", 0, 3, 1), ("x_T", 1, 0, 1)],
    7: [("z_out_stats", 0, 0, -2)],
    8: [("PV", 0, 1, 1)],
    9: [("z_out_norm", 0, 0, -2), ("gather", 0, 0, 1)],
    10: [("qkv", 1, 0, 1), ("qkv", 1, 1, 1), ("xm", 0, 2, -1), ("store", 0, 0, -2)],
    11: [("shuffle_out", 1, 0, 1), ("shuffle_in", 1, 0, 1)],
    12: [("x_load", 0, 0, 2)],
    13: [("xm", 0, 3, -1)],
    14: [("xm_T", 0, 0, -1)],
    16: [("xm_T", 0, 1, -1), ("hi", 1, 0, 1)],
    17: [("x2_bias", 0, 0, -1)],
    18: [("oh_T", 0, 0, -1)],
    19: [("rest", 1, 0, 1), ("xm_T", 0, 2, -1), ("x_scale", 0, 0, 2)],
    20: [("mid", 1, 0, 1), ("lo", 1, 0, 1)],
    22: [("xm_T", 0, 3, -1)],
    23: [("qk_T", 1, 0, 1)],
    24: [("qk_T", 1, 1, 1)],
    25: [("qk_T", 1, 2, 1)],
    26: [("scores", 1, 0, 1), ("mask", 1, 0, 1)],
    27: [("qk_T", 1, 3, 1), ("x_T", 0, 0, 2)],
    28: [("exp", 1, 0, 1), ("gate_load", 0, 0, 1)],
    29: [("mask", 1, 1, 1), ("scores", 1, 1, 1), ("exp", 1, 1, 1)],
    30: [("qkv", 0, 0, 2), ("P_T", 1, 0, 1)],
    31: [("P_T", 1, 1, 1), ("shuffle_out", 0, 0, 2), ("gate_T", 0, 0, 1)],
    32: [("shuffle_in", 0, 0, 2), ("exp", 1, 2, 1), ("x2_sum", 0, 0, 0)],
    33: [("residual", 0, 0, 1), ("exp", 1, 3, 1), ("x2_norm", 0, 0, 0), ("PV", 1, 0, 1)],
    34: [("P_T", 1, 2, 1), ("qkv", 0, 1, 2), ("logits", 0, 0, 0)],
    35: [("P_T", 1, 3, 1), ("gates", 0, 0, 1), ("gate_T", 0, 1, 1)],
    36: [("PV", 1, 1, 1), ("gates", 1, 0, 1), ("gather", 1, 0, 1), ("choose", 0, 0, 0)],
    38: [("rest", 0, 0, 2), ("hi", 0, 0, 2)],
    39: [("mid", 0, 0, 2)],
    41: [("lo", 0, 0, 2), ("x1_sum", 0, 0, 1)],
    42: [("x1_norm", 0, 0, 1)],
    43: [("qk_T", 0, 0, 2)],
    45: [("qk_T", 0, 1, 2), ("x1_T", 0, 0, 1)],
    47: [("mask", 0, 0, 2), ("qk_T", 0, 2, 2), ("scores", 0, 0, 2)],
    48: [("qk_T", 0, 3, 2)],
    49: [("exp", 0, 0, 2), ("mask", 0, 1, 2)],
    50: [("scores", 0, 1, 2)],
    51: [("exp", 0, 1, 2)],
}
AHEAD = {_key[:3]: _key[3] for _keys in TIMETABLE.values() for _key in _keys}
for _name, _n in LARGE:
    AHEAD[_name, 0, _n] = -1 if _name in ("ffn", "ffn_out") else 0
TIMETABLE = {_pos: [_key[:3] for _key in _keys] for _pos, _keys in TIMETABLE.items()}
assert max(TIMETABLE) < POSITIONS

SMALL_USERS = ("x_T", "qkv", "qk_T", "P_T", "PV", "gate_T", "x1_T", "xm_T", "oh_T")
SMALL_ORDER = [k for _p in sorted(TIMETABLE) for k in TIMETABLE[_p] if k[0] in SMALL_USERS]
USE = {k: u for u, k in enumerate(SMALL_ORDER)}
HID_ORDER = [("hidden", 0, n) for n in range(HIDDEN)] + [("ffn", 0, n) for n in range(C2 // 2)]
OUT_ORDER = [("output", 0, n) for n in range(OUTPUTS)] + [("ffn_out", 0, n) for n in range(TILES)]
assert all(len(o) % 2 == 0 for o in (SMALL_ORDER, HID_ORDER, OUT_ORDER))

WCHUNK = 1024
WNAMES = ["pin", "pout", "w1", "wo"]
WPARTS = {"pin": 8, "pout": 8, "w1": 8, "wo": 2}
WCHUNKS = [c for _g in range(4) for c in (("pin", _g), ("pin", 4 + _g), ("pout", 2 * _g), ("pout", 2 * _g + 1))]
WCHUNKS += [("w1", _n) for _n in range(8)] + [("wo", _n) for _n in range(2)]
PLACE = {c: m for m, c in enumerate(WCHUNKS)}
TOP_COLUMN = {c: m for m, c in enumerate((_w, _n) for _w in WNAMES for _n in range(WPARTS[_w]))}
LOADS = 8


MAXIMA_AT = {(-2, 32 + 2 * _m): _m for _m in range(10)}
MAXIMA_AT.update({(-1, 2 * _m): 10 + _m for _m in range(16)})
SCALES_AT = (-1, 33)
B1_AT = {(-1, 41 + 3 * _n): _n for _n in range(3)}
PAIRS_AT = {(-1, 34 + _m): _m for _m in range(18)}
PAIRS_AT.update({(0, 3 + 5 * _m): 18 + _m for _m in range(8)})


def at(table, it, pos):
    return [table[it, pos]] if isinstance(it, int) and (it, pos) in table else []


def wait(eng, sem, value):
    if not (isinstance(value, int) and value <= 0):
        eng.wait_ge(sem, value)


def decoder_layer(nc, x, ctx, itok, w_qkv, b_qkv, p_in, p_out, w_router, w_1, b_1, w_o, b_o,
                  gamma, beta, out):
    STEPS = x.shape[0] // TILES

    def step_of(it, key):
        return it + AHEAD[key]

    def active(it, key):
        return not isinstance(it, int) or 0 <= step_of(it, key) < STEPS

    def pieces(it, pos):
        return [(*key, step_of(it, key)) for key in TIMETABLE.get(pos, []) if active(it, key)]

    def run_pipeline(eng, iteration):
        for it in (-2, -1, 0, 1):
            iteration(it)
        with eng.Fori(2, STEPS - 2) as it:
            iteration(it)
        for it in (STEPS - 2, STEPS - 1, STEPS, STEPS + 1):
            iteration(it)

    es = ExitStack()
    with es:
        def sb(name, shape, dt=F32):
            return es.enter_context(nc.sbuf_tensor(name, shape, dt))

        def ps(name, shape, dt=F32):
            return es.enter_context(nc.psum_tensor(name, shape, dt))

        def sem(name):
            return es.enter_context(nc.semaphore(name))

        qkv_dram = nc.dram_tensor("qkv_scratch", [TILES, P, QKV], F32, kind="Internal").ap()
        attn_dram = nc.dram_tensor("attn_scratch", [TILES, P, D], F32, kind="Internal").ap()

        weights = sb("weights", [P, len(WCHUNKS), 2, WCHUNK], F16)
        wqkv = [sb(f"wqkv{k}", [P, DK, QKV], F16) for k in "hl"]
        b1p = sb("b1p", [P, I2], BF16)
        bqkv = sb("bqkv", [P, QKV])
        bo_r = sb("bo_r", [P, D])
        gamma_r = sb("gamma_r", [P, D])
        beta_r = sb("beta_r", [P, D])
        router_r = sb("router_r", [P, E2, D])
        ident = sb("ident", [P, P])
        ident16 = sb("ident16", [P, P], BF16)
        mask = sb("mask", [P, P])
        minus_half = sb("minus_half", [P, TILES])
        choice = sb("choice", [P, E2])
        tops = sb("tops", [P, len(WCHUNKS) + 1])
        top5 = sb("top5", [P, 8])
        top5a = sb("top5a", [P, 8])
        pow2 = sb("pow2", [P, 8])
        inv2 = sb("inv2", [P, 8])
        up = sb("up", [P, 8])
        down = sb("down", [P, 8])

        x_sb = sb("x_sb", [P, TILES, D])
        x1 = sb("x1", [P, TILES, D])
        x1T = [sb(f"x1T{k}", [P, DK, T], F16) for k in "hl"]
        acc_x2 = sb("acc_x2", [P, 2, TILES, D])
        acc, x2 = acc_x2[:, 0, :, :], acc_x2[:, 1, :, :]
        hT = [sb(f"hT{k}", [P, 2, C1, T], F16) for k in "hl"]
        gT = [h[:, :, :, :].rearrange("p a c t -> p (a c) t") for h in hT]
        xm = [sb(f"xm{b}", [P, TILES, D]) for b in range(2)]
        xmT = [sb(f"xmT{k}", [P, E2, DK, T], F16) for k in "hl"]
        gate = sb("gate", [P, TILES, E1])
        yy = sb("yy", [P, TILES, D])
        x2b = sb("x2b", [P, TILES, D])
        attn = sb("attn", [P, TILES, D])
        oh12 = sb("oh12", [P, TILES, P], BF16)
        ohT = sb("ohT", [P, T], BF16)
        logit = sb("logit", [P, TILES, E2])
        logit_top = sb("logit_top", [P, TILES])
        is_top = sb("is_top", [P, TILES, E2])
        index = sb("index", [P, TILES, E2])
        index_min = sb("index_min", [P, TILES])
        onehot = sb("onehot", [P, TILES, E2])
        qk6 = [sb(f"qk6{b}", [P, HEADS, 15, HD], BF16) for b in range(2)]
        prob = sb("prob", [P, 2, 8, P])
        qkT = sb("qkT", [P, 2, 8, P], BF16)
        ctx_sb = qkT[:, 0, :, :].rearrange("p h t -> p (h t)").bitcast(F32)[:, 0:T].rearrange("p (j k) -> p j k", j=TILES)
        tok_sb = qkT[:, 1, :, :].rearrange("p h t -> p (h t)").bitcast(I32)[:, 0:T].rearrange("p (j k) -> p j k", j=TILES)
        tokf = qkT[:, 1, :, :].rearrange("p h t -> p (h t)").bitcast(F32)[:, 0:T].rearrange("p (j k) -> p j k", j=TILES)
        PT = [sb(f"PT{k}", [P, 2, 4, P], F16) for k in "hl"]
        qkv_tok = sb("qkv_tok", [P, QKV])
        qkv_h = sb("qkv_h", [P, HEADS, 3, HD])
        ctxT = sb("ctxT", [P, TILES, P])
        tokT = sb("tokT", [P, TILES, P])
        rest = sb("rest", [P, HEADS, 3, HD])
        xT = [sb(f"xT{k}", [P, DK, P], F16) for k in "hl"]
        x_top = sb("x_top", [P, TILES])
        x_pow = sb("x_pow", [P, TILES])
        x_inv = sb("x_inv", [P, TILES])
        x_down = sb("x_down", [P, TILES])
        wqkv_tops = sb("wqkv_tops", [P, DK])
        g32 = sb("g32", [P, 2, T])
        neg_max = sb("neg_max", [P, 2, 8])
        row_sum = sb("row_sum", [P, 2, 8])
        row_inv = sb("row_inv", [P, 2, 8])
        pv = sb("pv", [P, 8, HD])
        attn_h = sb("attn_h", [P, HEADS, HD])
        junk = sb("junk", [P, 2, D])
        gate_junk = sb("gate_junk", [P, 2, P])
        NORMS = ("n1", "n2", "n3", "n4")
        stats = {k: sb(f"stats_{k}", [P, TILES, 6]) for k in NORMS}
        mv = {k: sb(f"mv_{k}", [P, TILES, 2]) for k in NORMS}
        vare = {k: sb(f"vare_{k}", [P, TILES]) for k in NORMS}
        rstd = {k: sb(f"rstd_{k}", [P, TILES]) for k in NORMS}
        wqkv_values = [h[:, :, :, :].rearrange("p a c t -> p (a c t)").bitcast(F32)[:, 0:QKV] for h in hT]
        last_values = [h[:, :, :, :].rearrange("p a c t -> p (a c t)").bitcast(F32) for h in xmT]
        b1_sb = acc_x2[0:E2, :, :, :].rearrange("p a j d -> p (a j d)")
        b1_h = [t[0:E2, :, :].rearrange("p j d -> p (j d)").bitcast(BF16) for t in (xm[0], xm[1], yy)]

        hid = [ps(f"hid{b}", [P, BANK]) for b in range(2)]
        outp = [ps(f"outp{b}", [P, BANK]) for b in range(2)]
        score = ps("score", [P, 8, P])
        small = [ps(f"small{b}", [P, BANK]) for b in range(2)]

        const_pool = sem("const_pool")
        consts_loaded = sem("consts_loaded")
        chunk_loaded = [sem(f"chunk_loaded{b}") for b in range(LOADS)]
        tops_found = sem("tops_found")
        chunk_hi = sem("chunk_hi")
        chunk_lo = sem("chunk_lo")
        top_reduced = sem("top_reduced")
        wqkv_loaded = sem("wqkv_loaded")
        wqkv_scale = sem("wqkv_scale")
        wqkv_hi = sem("wqkv_hi")
        wqkv_lo = sem("wqkv_lo")
        scales = sem("scales")
        b1_steps = sem("b1_steps")
        b1_placed = sem("b1_placed")
        settled = sem("settled")
        x_loaded = sem("x_loaded")
        gates_loaded = sem("gates_loaded")
        turned = {k: sem(f"{k}_done") for k in SMALL_USERS}
        x_scale_steps = sem("x_scale_steps")
        x_scaled = sem("x_scaled")
        xT_hi = sem("xT_hi")
        xT_lo = sem("xT_lo")
        qkv_biased = sem("qkv_biased")
        qkv_stored = sem("qkv_stored")
        qkv_reloaded = sem("qkv_reloaded")
        hi_written = sem("hi_written")
        rest_found = sem("rest_found")
        mid_written = sem("mid_written")
        lo_written = sem("lo_written")
        qkT_copied = sem("qkT_copied")
        scores_done = sem("scores_done")
        scores_masked = sem("scores_masked")
        max_found = sem("max_found")
        exps_done = sem("exps_done")
        sums_inverted = sem("sums_inverted")
        PT_hi = sem("PT_hi")
        PT_lo = sem("PT_lo")
        pv_summed = sem("pv_summed")
        attn_scaled = sem("attn_scaled")
        attn_stored = sem("attn_stored")
        attn_loaded = sem("attn_loaded")
        tok_cast = sem("tok_cast")
        gatesT = sem("gatesT")
        gate_summed = sem("gate_summed")
        gate_scaled = sem("gate_scaled")
        residual_loaded = sem("residual_loaded")
        x1_sum = sem("x1_sum")
        x1_ready = sem("x1_ready")
        x1T_hi = sem("x1T_hi")
        x1T_lo = sem("x1T_lo")
        n_stats = {k: sem(f"n_stats_{k}") for k in NORMS}
        n_aggr = {k: sem(f"n_aggr_{k}") for k in NORMS}
        n_eps = {k: sem(f"n_eps_{k}") for k in NORMS}
        n_rstd = {k: sem(f"n_rstd_{k}") for k in NORMS}
        hidden_done = sem("hidden_done")
        output_done = sem("output_done")
        ffn_done = sem("ffn_done")
        ffn_out_done = sem("ffn_out_done")
        h_hi = sem("h_hi")
        h_lo = sem("h_lo")
        o_summed = sem("o_summed")
        x2_sum = sem("x2_sum")
        x2_ready = sem("x2_ready")
        x2_biased = sem("x2_biased")
        logit_done = sem("logit_done")
        choice_steps = sem("choice_steps")
        masked = sem("masked")
        xm_hi = sem("xm_hi")
        xm_lo = sem("xm_lo")
        ohT_copied = sem("ohT_copied")
        gelu_done = sem("gelu_done")
        g_hi = sem("g_hi")
        g_lo = sem("g_lo")
        y_summed = sem("y_summed")
        z_ready = sem("z_ready")
        z_gamma = sem("z_gamma")
        z_beta = sem("z_beta")
        z_done = sem("z_done")
        out_stored = sem("out_stored")

        def chunk_dram(name, n):
            if name == "pin":
                return p_in.rearrange("(k p) n -> p k n", p=P)[:, n // 4, (n % 4) * WCHUNK:(n % 4 + 1) * WCHUNK]
            if name == "w1":
                return w_1.rearrange("(c p) n -> p c n", p=P)[:, n, :]
            return (p_out if name == "pout" else w_o).rearrange("(c p) n -> p c n", p=P)[:, 4 * n:4 * n + 4, :]

        def chunk_pair(m, part):
            return weights[:, m, part, :]

        def chunk_values(m):
            if m + 2 < len(WCHUNKS):
                return weights[:, m + 2, :, :].rearrange("p a n -> p (a n)").bitcast(F32)
            return last_values[m + 2 - len(WCHUNKS)]

        def pin(part, k, c0):
            c0 = k * E1 * I1 + c0
            return weights[:, PLACE["pin", c0 // WCHUNK], part, c0 % WCHUNK:c0 % WCHUNK + P]

        def w1(part, chunk, c0):
            return weights[:, PLACE["w1", chunk], part, c0:c0 + P]

        def second(name, part, c):
            return weights[:, PLACE[name, c // 4], part, (c % 4) * D:(c % 4 + 1) * D]

        def turned_value(s, key):
            name, j, n = key
            per = {"x_T": 1, "qkv": 2, "qk_T": 4, "P_T": 4, "PV": 2}
            if name in per:
                return s * TILES * per[name] + j * per[name] + n + 1
            return s * {"gate_T": 2, "x1_T": 1, "xm_T": E2, "oh_T": 1}[name] + n + 1

        def wait_turned(eng, s, key):
            wait(eng, turned[key[0]], turned_value(s, key))

        def read_of(s, key):
            name, j, n = key
            if name in turned:
                reader = {"x_T": xT_lo, "qkv": qkv_biased, "qk_T": qkT_copied, "P_T": PT_lo, "PV": pv_summed,
                          "gate_T": gatesT, "x1_T": x1T_lo, "xm_T": xm_lo, "oh_T": ohT_copied}[name]
                return reader, turned_value(s, key)
            return {"hidden": (h_lo, s * HIDDEN + n + 1), "ffn": (gelu_done, s * (C2 // 2) + n + 1),
                    "output": (o_summed, s * OUTPUTS + n + 1), "ffn_out": (y_summed, s * TILES + n + 1)}[name]

        def wait_bank(pe, it, order, key):
            u, back = order.index(key) - 2, 0
            while back < 3:
                if u < 0:
                    u, back = u + len(order), back + 1
                before = order[u]
                if active(it - back, before):
                    wait(pe, *read_of(step_of(it - back, before), before))
                    return
                u -= 2

        def small_of(key):
            return small[USE[key] % 2]

        def rows_of(t, s):
            return t.rearrange("(i j) s d -> i s j d", j=TILES)[s]

        def it_is(it, n):
            return isinstance(it, int) and it == n

        block = es.enter_context(nc.Block())

        @block.sync
        def _(sp):
            loads = [
                     (bqkv[:, :], b_qkv[0, :].partition_broadcast(P)),
                     (b1_sb, b_1),
                     (router_r[:, :, :], w_router.partition_broadcast(P)),
                     (bo_r[:, :], b_o.partition_broadcast(P)),
                     (gamma_r[:, :], gamma.partition_broadcast(P)),
                     (beta_r[:, :], beta.partition_broadcast(P))]

            def load_weights(m):
                if m >= LOADS:
                    sp.wait_ge(tops_found, m - LOADS + 1)
                src = chunk_dram(*WCHUNKS[m])
                to = chunk_values(m)
                to = to if len(src.shape) == 2 else to.rearrange("p (c n) -> p c n", n=src.shape[-1])
                sp.dma_start(to, src).then_inc(chunk_loaded[m % LOADS], 16)

            def load_x(s):
                wait(sp, turned["x_T"], s * TILES)
                sp.dma_start(x_sb[:, :, :], rows_of(x, s)).then_inc(x_loaded, 16)

            def place_b1():
                for part in range(3):
                    sp.wait_ge(b1_steps, 2 + 2 * part)
                    sp.dma_start(b1p[E2 * part:E2 * part + E2, :], b1_h[part]).then_inc(b1_placed, 16)

            def iteration(it):
                for pos in range(POSITIONS):
                    if it_is(it, -2) and pos == 0:
                        load_x(0)
                        for k in range(DK):
                            sp.dma_start(wqkv_values[k], w_qkv.rearrange("(k p) n -> p k n", p=P)[:, k, :]).then_inc(wqkv_loaded, 16)
                        for to, of in loads:
                            sp.dma_start(to, of).then_inc(consts_loaded, 16)
                        for m in range(LOADS):
                            load_weights(m)
                    for m in at(MAXIMA_AT, it, pos):
                        if m + LOADS < len(WCHUNKS):
                            load_weights(m + LOADS)
                    if it_is(it, 0) and pos == 30:
                        place_b1()
                    for name, j, n, s in pieces(it, pos):
                        if name == "x_load" and not it_is(s, 0):
                            load_x(s)
                        if name == "residual":
                            wait(sp, x2_sum, s * TILES)
                            sp.dma_start(x1[:, :, :], rows_of(x, s)).then_inc(residual_loaded, 16)
                        if name == "shuffle_out":
                            wait(sp, qkv_biased, s * 2 * TILES + 2 * j + 2)
                            sp.dma_start(qkv_dram[j], qkv_tok[:, :]).then_inc(qkv_stored, 16)
                        if name == "shuffle_in":
                            wait(sp, rest_found, s * TILES + j)
                            sp.sem_inc(settled, 1)
                            wait(sp, qkv_stored, (s * TILES + j + 1) * 16)
                            sp.dma_start(qkv_h[:, :, :, :].rearrange("p h s e -> p h (s e)"),
                                         qkv_dram[j].rearrange("s (c f) -> (s c) f", c=HEADS)
                                         .rearrange("(h p) f -> p h f", h=HEADS)).then_inc(qkv_reloaded, 16)
                        if name == "gather":
                            wait(sp, attn_scaled, s * 2 * TILES + 2 * j + 2)
                            sp.dma_start(attn_dram[j].rearrange("s (c f) -> (s c) f", c=HEADS)
                                         .rearrange("(h p) f -> p h f", h=HEADS),
                                         attn_h[:, :, :]).then_inc(attn_stored, 16)
                            wait(sp, x1_sum, s * TILES)
                            sp.sem_inc(settled, 1)
                            wait(sp, attn_stored, (s * TILES + j + 1) * 16)
                            sp.dma_start(attn[:, j, :], attn_dram[j]).then_inc(attn_loaded, 16)
                        if name == "gate_load":
                            wait(sp, scores_done, (s + 1) * 2 * TILES)
                            sp.dma_start(ctx_sb, rows_of(ctx, s)).then_inc(gates_loaded, 16)
                            sp.dma_start(tok_sb, rows_of(itok, s)).then_inc(gates_loaded, 16)
                        if name == "store":
                            wait(sp, z_done, (s + 1) * TILES)
                            sp.dma_start(rows_of(out, s), yy[:, :, :]).then_inc(out_stored, 16)

            run_pipeline(sp, iteration)
            sp.wait_ge(out_stored, 16 * STEPS)

        @block.gpsimd
        def _(pool):
            pool.memset(ident[:, :], 0.0).then_inc(const_pool, 1)
            pool.memset(ident16[:, :], 0.0).then_inc(const_pool, 1)
            pool.memset(mask[:, :], 0.0).then_inc(const_pool, 1)
            pool.memset(minus_half[:, :], -0.5).then_inc(const_pool, 1)
            pool.memset(oh12[:, :, :], 0.0).then_inc(const_pool, 1)
            pool.memset(b1p[:, :], 0.0).then_inc(const_pool, 1)
            for e in range(E2):
                pool.memset(choice[:, e:e + 1], float(E2 + e)).then_inc(const_pool, 1)
            pool.memset(tops[:, :], 0.0).then_inc(const_pool, 1)
            pool.wait_ge(const_pool, 11)
            for m in (ident, ident16):
                pool.affine_select(out=m[:, :], in_=m[:, :], compare_op=ALU.not_equal, fill=1.0, base=0,
                                   pattern=[[-1, P]], channel_multiplier=1).then_inc(const_pool, 1)
            pool.affine_select(out=mask[:, :], in_=mask[:, :], compare_op=ALU.is_ge, fill=MASKED, base=0,
                               pattern=[[-1, P]], channel_multiplier=1).then_inc(const_pool, 1)
            pool.wait_ge(wqkv_scale, 3)
            pool.partition_all_reduce(top5a[:, 6:7], top5[:, 6:7], P, bass.bass_isa.ReduceOp.max).then_inc(wqkv_scale, 1)

            def weights_maxima():
                pool.wait_ge(top_reduced, 1)
                pool.partition_all_reduce(top5a[:, 0:5], top5[:, 0:5], P, bass.bass_isa.ReduceOp.max).then_inc(scales, 1)

            pool.wait_ge(consts_loaded, 16 * 6)

            def rsqrt(k, s):
                wait(pool, n_eps[k], s + 1)
                pool.tensor_tensor(rstd[k][:, :], vare[k][:, :], minus_half[:, :], ALU.pow).then_inc(n_rstd[k], 1)

            def iteration(it):
                for pos in range(POSITIONS):
                    if it_is(it, SCALES_AT[0]) and pos == SCALES_AT[1]:
                        weights_maxima()
                    for name, j, n, s in pieces(it, pos):
                        if name == "x_scale":
                            wait(pool, x_scale_steps, s * 5 + 4)
                            pool.tensor_tensor(x_sb[:, :, :], x_sb[:, :, :],
                                               x_inv[:, :, None].to_broadcast([P, TILES, D]), ALU.mult).then_inc(x_scaled, 1)
                        if name == "gate_T" and n == 0:
                            wait(pool, gates_loaded, (s + 1) * 32)
                            pool.sem_inc(settled, 1)
                            pool.tensor_copy(tokf, tok_sb).then_inc(tok_cast, 1)
                        if name == "x1_norm":
                            rsqrt("n1", s)
                        if name == "x2_norm":
                            rsqrt("n2", s)
                        if name == "xm":
                            if n == 0:
                                wait(pool, choice_steps, (s + 1) * 6 - 1)
                            if n == 0 and it_is(it, 1):
                                pool.wait_ge(b1_placed, 48)
                            wait(pool, turned["xm_T"], s * E2 + n - 1)
                            pool.tensor_tensor(xm[n % 2][:, :, :], x2, onehot[:, :, n:n + 1].to_broadcast([P, TILES, D]),
                                               ALU.mult).then_inc(masked, 1)
                        if name == "x2_bias":
                            wait(pool, x2_ready, (s + 1) * TILES)
                            wait(pool, z_beta, s)
                            pool.tensor_tensor(x2b[:, :, :], x2, beta_r[:, None, :].to_broadcast([P, TILES, D]),
                                               ALU.add).then_inc(x2_biased, 1)
                            wait(pool, out_stored, s * 16)
                            if it_is(it, 1):
                                pool.wait_ge(b1_placed, 48)
                            pool.tensor_tensor(yy[:, :, :], x2, bo_r[:, None, :].to_broadcast([P, TILES, D]),
                                               ALU.add).then_inc(x2_biased, 1)
                        if name == "z_norm":
                            rsqrt("n3", s)
                            wait(pool, z_ready, (s + 1) * TILES)
                            pool.tensor_tensor(yy[:, :, :], yy[:, :, :], gamma_r[:, None, :].to_broadcast([P, TILES, D]),
                                               ALU.mult).then_inc(z_gamma, 1)
                            wait(pool, z_gamma, s + 1)
                            pool.tensor_tensor(yy[:, :, :], yy[:, :, :], x2b[:, :, :], ALU.add).then_inc(z_beta, 1)
                        if name == "z_out_norm":
                            rsqrt("n4", s)

            run_pipeline(pool, iteration)

        @block.scalar
        def _(act):
            def weight_hi(m):
                name = WCHUNKS[m][0]
                if m == 0:
                    act.wait_ge(scales, 6)
                wait(act, chunk_lo, m - 1)
                act.activation(chunk_pair(m, 0), chunk_values(m), ACT.Copy,
                               scale=up[:, WNAMES.index(name):WNAMES.index(name) + 1]).then_inc(chunk_hi, 1)

            act.wait_ge(wqkv_scale, 8)
            for k in range(DK):
                act.activation(wqkv[0][:, k, :], wqkv_values[k], ACT.Copy, scale=up[:, 6:7]).then_inc(wqkv_hi, 1)

            def piece(name, j, n, s):
                key = (name, j, n)
                b = j % 2
                if name == "x_T":
                    wait_turned(act, s, key)
                    wait(act, turned["qkv"], s * 2 * TILES + 2 * j)
                    act.activation(xT[0][:, :, :].rearrange("p k s -> p (k s)"), small_of(key)[:, 0:D],
                                   ACT.Copy, scale=X_SCALE).then_inc(xT_hi, 1)
                if name == "hi":
                    wait(act, qkv_reloaded, (s * TILES + j + 1) * 16)
                    wait(act, turned["PV"], (s - 1) * 2 * TILES + 2 * j + 2)
                    q, k, v = (qkv_h[:, :, m, :] for m in range(3))
                    act.activation(qk6[b][:, :, 3:6, :], q[:, :, None, :].to_broadcast([P, HEADS, 3, HD]),
                                   ACT.Copy).then_inc(hi_written, 1)
                    act.activation(qk6[b][:, :, 6:11:2, :], k[:, :, None, :].to_broadcast([P, HEADS, 3, HD]),
                                   ACT.Copy).then_inc(hi_written, 1)
                    act.activation(qk6[b][:, :, 12, :], v, ACT.Copy).then_inc(hi_written, 1)
                if name == "mid":
                    wait(act, rest_found, s * TILES + j + 1)
                    q, k, v = (rest[:, :, m, :] for m in range(3))
                    act.activation(qk6[b][:, :, 0:2, :], q[:, :, None, :].to_broadcast([P, HEADS, 2, HD]),
                                   ACT.Copy).then_inc(mid_written, 1)
                    act.activation(qk6[b][:, :, 7:10:2, :], k[:, :, None, :].to_broadcast([P, HEADS, 2, HD]),
                                   ACT.Copy).then_inc(mid_written, 1)
                    act.activation(qk6[b][:, :, 14, :], v, ACT.Copy).then_inc(mid_written, 1)
                if name == "qk_T":
                    wait_turned(act, s, key)
                    wait(act, scores_done, s * 2 * TILES + 2 * j + n // 2)
                    if j == 0 and n < 2:
                        wait(act, turned["gate_T"], 2 * s)
                    act.activation(qkT[0:96, n % 2, :, :].rearrange("p h t -> p (h t)"),
                                   small_of(key)[0:96, :].bitcast(BF16), ACT.Copy).then_inc(qkT_copied, 1)
                if name == "exp":
                    h = n // 2
                    wait(act, max_found, s * 2 * TILES + 2 * j + h + 1)
                    wait(act, sums_inverted, s * 2 * TILES + 2 * (j - 1) + h + 1)
                    for g in range(4 * (n % 2), 4 * (n % 2) + 4):
                        act.activation(prob[:, h, g, :], prob[:, h, g, :], ACT.Exp, bias=neg_max[:, h, g:g + 1],
                                       scale=1.0, accum_out=row_sum[:, h, g:g + 1]).then_inc(exps_done, 1)
                if name == "P_T":
                    wait_turned(act, s, key)
                    act.activation(PT[0][:, n % 2, :, :].rearrange("p h t -> p (h t)"), small_of(key)[:, :],
                                   ACT.Copy).then_inc(PT_hi, 1)
                if name == "gate_T":
                    wait_turned(act, s, key)
                    wait(act, gate_summed, s * TILES * E1)
                    act.activation((ctxT, tokT)[n][:, :, :].rearrange("p j k -> p (j k)"), small_of(key)[:, 0:T],
                                   ACT.Copy).then_inc(gatesT, 1)
                if name == "x1_T":
                    wait_turned(act, s, key)
                    wait(act, hidden_done, s * HIDDEN)
                    act.activation(x1T[0][:, :, :].rearrange("p k t -> p (k t)"), small_of(key)[:, :],
                                   ACT.Copy).then_inc(x1T_hi, 1)
                if name == "xm_T":
                    wait_turned(act, s, key)
                    if it_is(s, 0) and n == 0:
                        act.wait_ge(chunk_lo, len(WCHUNKS))
                    wait(act, ffn_done, s * (C2 // 2))
                    act.activation(xmT[0][:, n, :, :].rearrange("p k t -> p (k t)"), small_of(key)[:, :],
                                   ACT.Copy).then_inc(xm_hi, 1)
                if name == "oh_T":
                    wait_turned(act, s, key)
                    act.activation(ohT[:, :], small_of(key)[:, 0:T // 2].bitcast(BF16), ACT.Copy).then_inc(ohT_copied, 1)

            def large(name, n, s):
                if name == "hidden":
                    e, half = n // 2, n % 2
                    wait(act, hidden_done, s * HIDDEN + n + 1)
                    if e >= 2:
                        wait(act, output_done, s * OUTPUTS + (e - 1) * TILES)
                    else:
                        wait(act, ffn_out_done, (s - 1) * TILES)
                    act.activation(hT[0][:, e % 2, 2 * half:2 * half + 2, :].rearrange("p c t -> p (c t)"),
                                   hid[n % 2][:, :], ACT.Relu).then_inc(h_hi, 1)
                if name == "ffn" and n % 4 == 3:
                    q = n // 4
                    wait(act, ffn_done, s * (C2 // 2) + q + 1)
                    wait(act, g_lo, s * (C2 // 2) + q)
                    act.activation(g32[:, :, :].rearrange("p c t -> p (c t)"), hid[q % 2][:, :], ACT.Gelu,
                                   scale=down[:, 2:3]).then_inc(gelu_done, 1)
                    wait(act, gelu_done, s * (C2 // 2) + q + 1)
                    act.activation(gT[0][:, 2 * q:2 * q + 2, :], g32[:, :, :], ACT.Copy, scale=up[:, 4:5]).then_inc(g_hi, 1)

            def iteration(it):
                for pos in range(POSITIONS):
                    for m in at(PAIRS_AT, it, pos):
                        weight_hi(m)
                    name, n = LARGE[pos]
                    if active(it, (name, 0, n)):
                        large(name, n, step_of(it, (name, 0, n)))
                    for p in pieces(it, pos):
                        piece(*p)

            run_pipeline(act, iteration)

        @block.tensor
        def _(pe):
            pe.wait_ge(const_pool, 14)

            def piece(it, name, j, n, s):
                key = (name, j, n)
                b = j % 2
                if name == "scores":
                    wait(pe, qkT_copied, s * 4 * TILES + 4 * j + 2 * n + 2)
                    wait(pe, scores_masked, s * 2 * TILES + 2 * j + n)
                    for g in range(8):
                        mm = pe.matmul(score[:, g, :], qkT[0:96, g // 4, 2 * (g % 4), :], qkT[0:96, g // 4, 2 * (g % 4) + 1, :],
                                       start=True, stop=True)
                    mm.then_inc(scores_done, 1)
                if key not in USE:
                    return
                bank = small_of(key)
                if name == "x_T":
                    wait(pe, x_scaled, s + 1)
                if name == "qkv":
                    if it_is(s, 0) and j == 0 and n == 0:
                        pe.wait_ge(wqkv_lo, DK)
                    wait(pe, xT_lo, s * TILES + j + 1)
                if name == "qk_T":
                    wait(pe, lo_written, s * 2 * TILES + 2 * j + 2)
                if name == "P_T":
                    wait(pe, exps_done, s * 16 * TILES + 16 * j + 4 * n + 4)
                if name == "PV":
                    wait(pe, PT_lo, s * 4 * TILES + 4 * j + 2 * n + 2)
                if name == "gate_T":
                    wait(pe, *((gates_loaded, (s + 1) * 32), (tok_cast, s + 1))[n])
                if name == "x1_T":
                    wait(pe, x1_ready, (s + 1) * TILES)
                if name == "xm_T":
                    wait(pe, masked, s * E2 + n + 1)
                if name == "oh_T":
                    wait(pe, choice_steps, (s + 1) * 6)
                wait_bank(pe, it, SMALL_ORDER, key)
                if name == "x_T":
                    for k in range(DK):
                        mm = pe.transpose(bank[:, k * P:(k + 1) * P], x_sb[:, j, k * P:(k + 1) * P], ident[:, :])
                if name == "qkv":
                    c0, c1 = (0, BANK) if n == 0 else (BANK, QKV)
                    terms = [(k, w, v) for k in range(DK) for w, v in PAIRS]
                    for m, (k, w, v) in enumerate(terms):
                        mm = pe.matmul(bank[:, 0:c1 - c0], xT[v][:, k, :], wqkv[w][:, k, c0:c1],
                                       start=(m == 0), stop=(m == len(terms) - 1))
                if name == "qk_T":
                    for g in range(4):
                        flat = qk6[b][:, 4 * n + g, :, :].rearrange("p s e -> p (s e)")
                        for half in range(2):
                            m = 2 * g + half
                            mm = pe.transpose(bank[:, :].bitcast(BF16)[0:96, m * P:(m + 1) * P],
                                              flat[:, 96 * half:96 * half + 96], ident16[:, :])
                if name == "P_T":
                    for g in range(4):
                        mm = pe.transpose(bank[:, g * P:(g + 1) * P], prob[:, n // 2, 4 * (n % 2) + g, :], ident[:, :])
                if name == "PV":
                    for g in range(8):
                        v3 = qk6[b][:, 8 * n + g, 12:15, :].rearrange("p s e -> p (s e)")
                        for part in range(2):
                            mm = pe.matmul(bank[:, 48 * g:48 * g + 48], PT[part][:, g // 4, g % 4, :], v3,
                                           start=(part == 0), stop=(part == 1))
                if name == "gate_T":
                    for t in range(TILES):
                        mm = pe.transpose(bank[:, t * P:(t + 1) * P], (ctx_sb, tokf)[n][:, t, :], ident[:, :])
                if name == "x1_T" or name == "xm_T":
                    src = x1 if name == "x1_T" else xm[n % 2]
                    for k in range(DK):
                        for t in range(TILES):
                            c = k * T + t * P
                            mm = pe.transpose(bank[:, c:c + P], src[:, t, k * P:(k + 1) * P], ident[:, :])
                if name == "oh_T":
                    for t in range(TILES):
                        mm = pe.transpose(bank[:, 0:T // 2].bitcast(BF16)[:, t * P:(t + 1) * P], oh12[:, t, :], ident16[:, :])
                mm.then_inc(turned[name], 1)

            def hidden(it, n, s):
                e, half = n // 2, n % 2
                if n == 0:
                    wait(pe, x1T_lo, s + 1)
                if n % 4 == 0 and it_is(it, 0):
                    pe.wait_ge(chunk_lo, PLACE["pin", 4 + n // 4] + 1)
                wait_bank(pe, it, HID_ORDER, ("hidden", 0, n))
                terms = [(k, w, v) for k in range(DK) for w, v in PAIRS]
                for c in range(2):
                    first = e * I1 + (2 * half + c) * P
                    for m, (k, w, v) in enumerate(terms):
                        mm = pe.matmul(hid[n % 2][:, c * T:(c + 1) * T], pin(w, k, first), x1T[v][:, k, :],
                                       start=(m == 0), stop=(m == len(terms) - 1))
                mm.then_inc(hidden_done, 1)

            def output(it, n, s):
                e, j = n // TILES, n % TILES
                if j == 0 and it_is(it, 0):
                    pe.wait_ge(chunk_lo, PLACE["pout", e] + 1)
                if j == 0:
                    wait(pe, h_lo, s * HIDDEN + 2 * (e + 1))
                wait_bank(pe, it, OUT_ORDER, ("output", 0, n))
                terms = [(c, v, w) for c in range(C1) for w, v in PAIRS]
                for m, (c, v, w) in enumerate(terms):
                    mm = pe.matmul(outp[n % 2][:, 0:D], hT[w][:, e % 2, c, j * P:(j + 1) * P], second("pout", v, e * C1 + c),
                                   start=(m == 0), stop=(m == len(terms) - 1))
                mm.then_inc(output_done, 1)

            def ffn(it, n, s):
                c, second = n // 2, n % 2
                if n == 0:
                    if it_is(it, 1):
                        pe.wait_ge(chunk_lo, len(WCHUNKS))
                        pe.wait_ge(b1_placed, 48)
                    wait(pe, ohT_copied, s + 1)
                    wait(pe, xm_lo, (s + 1) * E2)
                if n % 4 == 0:
                    wait_bank(pe, it, HID_ORDER, ("ffn", 0, n // 4))
                to = hid[(c // 2) % 2][:, (c % 2) * T:(c % 2 + 1) * T]
                if not second:
                    pe.matmul(to, b1p[:, c * P:(c + 1) * P], ohT[:, :], start=True, stop=False)
                terms = [(e, k, w, v) for e in (range(2, E2) if second else range(2)) for k in range(DK) for w, v in PAIRS]
                for m, (e, k, w, v) in enumerate(terms):
                    mm = pe.matmul(to, w1(w, e * DK + k, c * P), xmT[v][:, e, k, :],
                                   start=False, stop=(second == 1 and m == len(terms) - 1))
                if n % 4 == 3:
                    mm.then_inc(ffn_done, 1)

            def ffn_out(it, n, s):
                j, half = n // 2, n % 2
                if half == 0:
                    wait_bank(pe, it, OUT_ORDER, ("ffn_out", 0, j))
                for c in range(half * C2 // 2, (half + 1) * C2 // 2):
                    if j == 0 and c % 2 == 0:
                        wait(pe, g_lo, s * (C2 // 2) + c // 2 + 1)
                    for p, (w, v) in enumerate(PAIRS):
                        mm = pe.matmul(outp[j % 2][:, 0:D], gT[w][:, c, j * P:(j + 1) * P], second("wo", v, c),
                                       start=(c == 0 and p == 0), stop=(c == C2 - 1 and p == 2))
                if half == 1:
                    mm.then_inc(ffn_out_done, 1)

            def iteration(it):
                for pos in range(POSITIONS):
                    name, n = LARGE[pos]
                    if active(it, (name, 0, n)):
                        {"hidden": hidden, "output": output, "ffn": ffn, "ffn_out": ffn_out}[name](
                            it, n, step_of(it, (name, 0, n)))
                    for p in pieces(it, pos):
                        piece(it, *p)

            run_pipeline(pe, iteration)

        @block.vector
        def _(dve):
            dve.wait_ge(const_pool, 14)

            dve.wait_ge(wqkv_loaded, 16 * DK)
            for k in range(DK):
                dve.tensor_reduce(wqkv_tops[:, k:k + 1], wqkv_values[k], AX.X, ALU.max,
                                  apply_absolute_value=True).then_inc(wqkv_scale, 1)
            dve.wait_ge(wqkv_scale, 2)
            dve.tensor_reduce(top5[:, 6:7], wqkv_tops[:, :], AX.X, ALU.max).then_inc(wqkv_scale, 1)
            dve.wait_ge(wqkv_scale, 4)
            dve.tensor_scalar(pow2[:, 6:7], top5a[:, 6:7], 2.0 ** -40, None, ALU.max).then_inc(wqkv_scale, 1)
            dve.wait_ge(wqkv_scale, 5)
            wqkv_bits = pow2[:, 6:7].bitcast(I32)
            dve.tensor_scalar(wqkv_bits, wqkv_bits, 0x7F800000, None, ALU.bitwise_and).then_inc(wqkv_scale, 1)
            dve.wait_ge(wqkv_scale, 6)
            dve.reciprocal(inv2[:, 6:7], pow2[:, 6:7]).then_inc(wqkv_scale, 1)
            dve.wait_ge(wqkv_scale, 7)
            dve.tensor_scalar(down[:, 6:7], pow2[:, 6:7], 2.0 ** -6 / X_SCALE, None, ALU.mult)
            dve.tensor_scalar(up[:, 6:7], inv2[:, 6:7], 2.0 ** 6, None, ALU.mult).then_inc(wqkv_scale, 1)
            dve.wait_ge(wqkv_scale, 8)
            for k in range(DK):
                dve.wait_ge(wqkv_hi, k + 1)
                dve.scalar_tensor_tensor(out=wqkv[1][:, k, :], in0=wqkv_values[k], scalar=up[:, 6:7],
                                         in1=wqkv[0][:, k, :], op0=ALU.mult, op1=ALU.subtract).then_inc(wqkv_lo, 1)

            dve.wait_ge(consts_loaded, 16 * 6)

            def weight_top(m):
                dve.wait_ge(chunk_loaded[m % LOADS], 16 * (m // LOADS + 1))
                to = TOP_COLUMN[WCHUNKS[m]]
                dve.tensor_reduce(tops[:, to:to + 1], chunk_values(m), AX.X, ALU.max,
                                  apply_absolute_value=True).then_inc(tops_found, 1)

            def weight_lo(m):
                name = WCHUNKS[m][0]
                dve.wait_ge(chunk_hi, m + 1)
                dve.scalar_tensor_tensor(out=chunk_pair(m, 1), in0=chunk_values(m),
                                         scalar=up[:, WNAMES.index(name):WNAMES.index(name) + 1],
                                         in1=chunk_pair(m, 0), op0=ALU.mult, op1=ALU.subtract).then_inc(chunk_lo, 1)

            def find_scales():
                K = len(WCHUNKS)
                dve.tensor_reduce(tops[0:E2, K:K + 1], b1_sb, AX.X, ALU.max, apply_absolute_value=True).then_inc(tops_found, 1)
                dve.wait_ge(tops_found, K + 1)
                dve.tensor_reduce(top5[:, 0:3], tops[:, 0:24].rearrange("p (w n) -> p w n", n=8), AX.X, ALU.max)
                dve.tensor_reduce(top5[:, 3:4], tops[:, 24:26], AX.X, ALU.max)
                dve.tensor_copy(top5[:, 4:5], tops[:, K:K + 1]).then_inc(top_reduced, 1)
                dve.wait_ge(scales, 1)
                dve.scalar_tensor_tensor(out=top5a[:, 4:5], in0=top5a[:, 2:3], scalar=float(D), in1=top5a[:, 4:5],
                                         op0=ALU.mult, op1=ALU.add).then_inc(scales, 1)
                dve.wait_ge(scales, 2)
                dve.tensor_scalar(pow2[:, 0:5], top5a[:, 0:5], 2.0 ** -40, None, ALU.max).then_inc(scales, 1)
                dve.wait_ge(scales, 3)
                bits = pow2[:, 0:5].bitcast(I32)
                dve.tensor_scalar(bits, bits, 0x7F800000, None, ALU.bitwise_and).then_inc(scales, 1)
                dve.wait_ge(scales, 4)
                dve.reciprocal(inv2[:, 0:5], pow2[:, 0:5]).then_inc(scales, 1)
                dve.wait_ge(scales, 5)
                for c0, c1, f in ((0, 4, 2.0 ** 6), (4, 5, 2.0 ** 14)):
                    dve.tensor_scalar(down[:, c0:c1], pow2[:, c0:c1], 1.0 / f, None, ALU.mult)
                    last = dve.tensor_scalar(up[:, c0:c1], inv2[:, c0:c1], f, None, ALU.mult)
                last.then_inc(scales, 1)
                dve.wait_ge(scales, 6)
                dve.tensor_tensor(down[:, 5:6], down[:, 3:4], down[:, 4:5], ALU.mult)
                dve.tensor_scalar(b1_sb, b1_sb, up[0:E2, 2:3], None, ALU.mult).then_inc(b1_steps, 1)

            def b1_part(part):
                dve.wait_ge(b1_steps, 1 + 2 * part)
                dve.tensor_copy(b1_h[part], b1_sb).then_inc(b1_steps, 1)
                if part < 2:
                    dve.wait_ge(b1_steps, 2 + 2 * part)
                    dve.tensor_tensor(b1_sb, b1_sb, b1_h[part], ALU.subtract).then_inc(b1_steps, 1)
                else:
                    dve.wait_ge(b1_steps, 6)

            def norm_stats(k, s, src):
                for j in range(TILES):
                    dve.bn_stats(stats[k][:, j, :], src[:, j, :]).then_inc(n_stats[k], 1)

            def norm_aggregate(k, s, eps):
                wait(dve, n_stats[k], (s + 1) * TILES)
                dve.sem_inc(settled, 1)
                for j in range(TILES):
                    last = dve.bn_aggr(mv[k][:, j, :], stats[k][:, j, :])
                last.then_inc(n_aggr[k], 1)
                wait(dve, n_aggr[k], s + 1)
                dve.tensor_scalar(vare[k][:, :], mv[k][:, :, 1], eps, None, ALU.add).then_inc(n_eps[k], 1)

            def norm_apply(k, s, to, of, done):
                wait(dve, n_rstd[k], s + 1)
                for j in range(TILES):
                    dve.tensor_scalar(to[:, j, :], of[:, j, :], mv[k][:, j, 0:1], rstd[k][:, j:j + 1],
                                      ALU.subtract, ALU.mult).then_inc(done, 1)

            def piece(name, j, n, s):
                key = (name, j, n)
                b = j % 2
                if name == "x_scale":
                    wait(dve, x_loaded, (s + 1) * 16)
                    wait(dve, qkv_biased, s * 2 * TILES)
                    dve.sem_inc(settled, 1)
                    wait(dve, x_scale_steps, s * 5)
                    dve.tensor_reduce(x_top[:, :], x_sb[:, :, :], AX.X, ALU.max,
                                      apply_absolute_value=True).then_inc(x_scale_steps, 1)
                    wait(dve, x_scale_steps, s * 5 + 1)
                    dve.tensor_scalar(x_pow[:, :], x_top[:, :], 2.0 ** -40, None, ALU.max).then_inc(x_scale_steps, 1)
                    wait(dve, x_scale_steps, s * 5 + 2)
                    bits = x_pow[:, :].bitcast(I32)
                    dve.tensor_scalar(bits, bits, 0x7F800000, None, ALU.bitwise_and).then_inc(x_scale_steps, 1)
                    wait(dve, x_scale_steps, s * 5 + 3)
                    dve.reciprocal(x_inv[:, :], x_pow[:, :]).then_inc(x_scale_steps, 1)
                    dve.tensor_scalar(x_down[:, :], x_pow[:, :], down[:, 6:7], None, ALU.mult).then_inc(x_scale_steps, 1)
                if name == "x_T":
                    wait(dve, xT_hi, s * TILES + j + 1)
                    dve.scalar_tensor_tensor(out=xT[1][:, :, :].rearrange("p k s -> p (k s)"), in0=small_of(key)[:, 0:D],
                                             scalar=X_SCALE, in1=xT[0][:, :, :].rearrange("p k s -> p (k s)"),
                                             op0=ALU.mult, op1=ALU.subtract).then_inc(xT_lo, 1)
                if name == "qkv":
                    if n == 0:
                        wait(dve, x_scale_steps, (s + 1) * 5)
                        dve.sem_inc(settled, 1)
                    wait_turned(dve, s, key)
                    wait(dve, qkv_stored, (s * TILES + j) * 16)
                    c0, c1 = (0, BANK) if n == 0 else (BANK, QKV)
                    dve.scalar_tensor_tensor(out=qkv_tok[:, c0:c1], in0=small_of(key)[:, 0:c1 - c0],
                                             scalar=x_down[:, j:j + 1], in1=bqkv[:, c0:c1],
                                             op0=ALU.mult, op1=ALU.add).then_inc(qkv_biased, 1)
                if name == "rest":
                    wait(dve, hi_written, s * 3 * TILES + 3 * j + 3)
                    wait(dve, mid_written, s * 3 * TILES + 3 * j)
                    wait(dve, lo_written, s * 2 * TILES + 2 * j)
                    dve.tensor_tensor(rest[:, :, :, :], qkv_h[:, :, :, :], qk6[b][:, :, 4:13:4, :],
                                      ALU.subtract).then_inc(rest_found, 1)
                if name == "lo":
                    wait(dve, mid_written, s * 3 * TILES + 3 * j + 3)
                    dve.tensor_tensor(qk6[b][:, :, 2:12:9, :], rest[:, :, 0:2, :], qk6[b][:, :, 0:8:7, :],
                                      ALU.subtract).then_inc(lo_written, 1)
                    dve.tensor_tensor(qk6[b][:, :, 13, :], rest[:, :, 2, :], qk6[b][:, :, 14, :],
                                      ALU.subtract).then_inc(lo_written, 1)
                if name == "mask":
                    wait(dve, scores_done, s * 2 * TILES + 2 * j + n + 1)
                    wait(dve, turned["P_T"], s * 4 * TILES + 4 * (j - 1) + 2 * n + 2)
                    dve.scalar_tensor_tensor(out=prob[:, n, :, :], in0=score[:, :, :], scalar=SCORE_SCALE,
                                             in1=mask[:, None, :].to_broadcast([P, 8, P]),
                                             op0=ALU.mult, op1=ALU.add).then_inc(scores_masked, 1)
                    wait(dve, scores_masked, s * 2 * TILES + 2 * j + n + 1)
                    wait(dve, exps_done, s * 16 * TILES + 16 * (j - 1) + 8 * n + 8)
                    dve.tensor_reduce(neg_max[:, n, :], prob[:, n, :, :], AX.X, ALU.max,
                                      negate=True).then_inc(max_found, 1)
                if name == "P_T":
                    wait(dve, PT_hi, s * 4 * TILES + 4 * j + n + 1)
                    dve.tensor_tensor(PT[1][:, n % 2, :, :].rearrange("p h t -> p (h t)"), small_of(key)[:, :],
                                      PT[0][:, n % 2, :, :].rearrange("p h t -> p (h t)"),
                                      ALU.subtract).then_inc(PT_lo, 1)
                if name == "PV":
                    wait(dve, exps_done, s * 16 * TILES + 16 * j + 8 * n + 8)
                    dve.reciprocal(row_inv[:, n, :], row_sum[:, n, :]).then_inc(sums_inverted, 1)
                    wait_turned(dve, s, key)
                    wait(dve, attn_scaled, s * 2 * TILES + 2 * j + n)
                    dve.tensor_reduce(pv[:, :, :], small_of(key)[:, 0:384].rearrange("p (h c e) -> p h e c", h=8, c=3),
                                      AX.X, ALU.add).then_inc(pv_summed, 1)
                    wait(dve, pv_summed, s * 2 * TILES + 2 * j + n + 1)
                    wait(dve, attn_stored, (s * TILES + j) * 16)
                    dve.tensor_tensor(attn_h[:, 8 * n:8 * n + 8, :], pv[:, :, :],
                                      row_inv[:, n, :, None].to_broadcast([P, 8, HD]),
                                      ALU.mult).then_inc(attn_scaled, 1)
                if name == "gates":
                    wait(dve, gatesT, (s + 1) * 2)
                    wait(dve, o_summed, s * OUTPUTS)
                    wait(dve, gate_scaled, s * TILES + j)
                    for e in range(E1):
                        wait(dve, gate_summed, s * TILES * E1 + j * E1 + e - 1)
                        dve.scalar_tensor_tensor(out=gate_junk[:, e % 2, :], in0=tokT[:, j, :], scalar=float(e),
                                                 in1=ctxT[:, j, :], op0=ALU.is_equal, op1=ALU.mult,
                                                 accum_out=gate[:, j, e:e + 1]).then_inc(gate_summed, 1)
                    wait(dve, gate_summed, s * TILES * E1 + (j + 1) * E1)
                    dve.tensor_scalar(gate[:, j, :], gate[:, j, :], down[:, 0:1], None, ALU.mult).then_inc(gate_scaled, 1)
                if name == "x1_sum":
                    wait(dve, attn_loaded, (s + 1) * TILES * 16)
                    wait(dve, residual_loaded, (s + 1) * 16)
                    for t in range(TILES):
                        dve.tensor_tensor(x1[:, t, :], x1[:, t, :], attn[:, t, :], ALU.add).then_inc(x1_sum, 1)
                    wait(dve, x1_sum, (s + 1) * TILES)
                    norm_stats("n1", s, x1)
                if name == "x1_norm":
                    norm_aggregate("n1", s, 1e-5)
                    norm_apply("n1", s, x1, x1, x1_ready)
                if name == "x1_T":
                    wait(dve, x1T_hi, s + 1)
                    dve.tensor_tensor(x1T[1][:, :, :].rearrange("p k t -> p (k t)"), small_of(key)[:, :],
                                      x1T[0][:, :, :].rearrange("p k t -> p (k t)"), ALU.subtract).then_inc(x1T_lo, 1)
                if name == "x2_sum":
                    wait(dve, o_summed, (s + 1) * OUTPUTS)
                    for t in range(TILES):
                        dve.scalar_tensor_tensor(out=acc[:, t, :], in0=acc[:, t, :], scalar=down[:, 1:2], in1=x1[:, t, :],
                                                 op0=ALU.mult, op1=ALU.add).then_inc(x2_sum, 1)
                    wait(dve, x2_sum, (s + 1) * TILES)
                    norm_stats("n2", s, acc)
                if name == "x2_norm":
                    norm_aggregate("n2", s, 1e-5)
                    wait(dve, x2_biased, 2 * s)
                    wait(dve, masked, s * E2)
                    norm_apply("n2", s, x2, acc, x2_ready)
                if name == "logits":
                    wait(dve, x2_ready, (s + 1) * TILES)
                    for t in range(TILES):
                        for e in range(E2):
                            wait(dve, logit_done, s * TILES * E2 + t * E2 + e - 1)
                            dve.tensor_tensor_reduce(junk[:, e % 2, :], x2[:, t, :], router_r[:, e, :], 1.0, 0.0,
                                                     ALU.mult, ALU.add, logit[:, t, e:e + 1]).then_inc(logit_done, 1)
                if name == "choose":
                    choose(s)
                if name == "xm_T":
                    wait(dve, xm_hi, s * E2 + n + 1)
                    dve.tensor_tensor(xmT[1][:, n, :, :].rearrange("p k t -> p (k t)"), small_of(key)[:, :],
                                      xmT[0][:, n, :, :].rearrange("p k t -> p (k t)"), ALU.subtract).then_inc(xm_lo, 1)
                if name == "z_stats":
                    wait(dve, y_summed, (s + 1) * TILES)
                    norm_stats("n3", s, yy)
                    norm_aggregate("n3", s, 1e-12)
                if name == "z_norm":
                    norm_apply("n3", s, yy, yy, z_ready)
                if name == "z_out_stats":
                    wait(dve, z_beta, s + 1)
                    norm_stats("n4", s, yy)
                    norm_aggregate("n4", s, 1e-5)
                if name == "z_out_norm":
                    norm_apply("n4", s, yy, yy, z_done)

            def choose(s):
                wait(dve, logit_done, (s + 1) * TILES * E2)
                dve.tensor_reduce(logit_top[:, :], logit[:, :, :], AX.X, ALU.max).then_inc(choice_steps, 1)
                wait(dve, choice_steps, s * 6 + 1)
                dve.tensor_tensor(is_top[:, :, :], logit[:, :, :], logit_top[:, :, None].to_broadcast([P, TILES, E2]),
                                  ALU.is_ge).then_inc(choice_steps, 1)
                wait(dve, choice_steps, s * 6 + 2)
                dve.scalar_tensor_tensor(out=index[:, :, :], in0=is_top[:, :, :], scalar=-float(E2),
                                         in1=choice[:, None, :].to_broadcast([P, TILES, E2]),
                                         op0=ALU.mult, op1=ALU.add).then_inc(choice_steps, 1)
                wait(dve, choice_steps, s * 6 + 3)
                dve.tensor_reduce(index_min[:, :], index[:, :, :], AX.X, ALU.min).then_inc(choice_steps, 1)
                wait(dve, choice_steps, s * 6 + 4)
                dve.tensor_tensor(onehot[:, :, :], index[:, :, :], index_min[:, :, None].to_broadcast([P, TILES, E2]),
                                  ALU.is_equal).then_inc(choice_steps, 1)
                wait(dve, choice_steps, s * 6 + 5)
                wait(dve, turned["oh_T"], s)
                dve.tensor_copy(oh12[:, :, 0:3 * E2].rearrange("p j (c e) -> p j c e", c=3),
                                onehot[:, :, None, :].to_broadcast([P, TILES, 3, E2])).then_inc(choice_steps, 1)

            def large(name, n, s):
                if name == "hidden":
                    e, half = n // 2, n % 2
                    wait(dve, h_hi, s * HIDDEN + n + 1)
                    chunk = (slice(None), e % 2, slice(2 * half, 2 * half + 2), slice(None))
                    dve.scalar_tensor_tensor(out=hT[1][chunk].rearrange("p c t -> p (c t)"), in0=hid[n % 2][:, :], scalar=0.0,
                                             in1=hT[0][chunk].rearrange("p c t -> p (c t)"),
                                             op0=ALU.max, op1=ALU.subtract).then_inc(h_lo, 1)
                if name == "output":
                    e, j = n // TILES, n % TILES
                    if n == 0:
                        wait(dve, gate_scaled, (s + 1) * TILES)
                        wait(dve, x2_ready, s * TILES)
                    wait(dve, output_done, s * OUTPUTS + n + 1)
                    if e == 0:
                        dve.tensor_scalar(acc[:, j, :], outp[n % 2][:, 0:D], gate[:, j, e:e + 1], None,
                                          ALU.mult).then_inc(o_summed, 1)
                    else:
                        wait(dve, o_summed, s * OUTPUTS + n - TILES + 1)
                        dve.scalar_tensor_tensor(out=acc[:, j, :], in0=outp[n % 2][:, 0:D], scalar=gate[:, j, e:e + 1],
                                                 in1=acc[:, j, :], op0=ALU.mult, op1=ALU.add).then_inc(o_summed, 1)
                if name == "ffn" and n % 4 == 3:
                    q = n // 4
                    wait(dve, g_hi, s * (C2 // 2) + q + 1)
                    dve.scalar_tensor_tensor(out=gT[1][:, 2 * q:2 * q + 2, :], in0=g32[:, :, :], scalar=up[:, 4:5],
                                             in1=gT[0][:, 2 * q:2 * q + 2, :], op0=ALU.mult, op1=ALU.subtract).then_inc(g_lo, 1)
                if name == "ffn_out" and n % 2:
                    j = n // 2
                    if j == 0:
                        wait(dve, x2_biased, 2 * s + 2)
                    wait(dve, ffn_out_done, s * TILES + j + 1)
                    dve.scalar_tensor_tensor(out=yy[:, j, :], in0=outp[j % 2][:, 0:D], scalar=down[:, 5:6],
                                             in1=yy[:, j, :], op0=ALU.mult, op1=ALU.add).then_inc(y_summed, 1)

            def iteration(it):
                for pos in range(POSITIONS):
                    for m in at(MAXIMA_AT, it, pos):
                        weight_top(m)
                    for m in at(PAIRS_AT, it, pos):
                        weight_lo(m)
                    if it_is(it, SCALES_AT[0]) and pos == SCALES_AT[1]:
                        find_scales()
                    for part in at(B1_AT, it, pos):
                        b1_part(part)
                    name, n = LARGE[pos]
                    if active(it, (name, 0, n)):
                        large(name, n, step_of(it, (name, 0, n)))
                    for p in pieces(it, pos):
                        piece(*p)

            run_pipeline(dve, iteration)


def kernel(x, ctx_512, itok_BxS2xS_0_7, L0_attn_qkv_kernel, L0_attn_qkv_bias, L0_xattn_proj_in, L0_xattn_proj_out,
           L0_ffn_W_router, L0_ffn_W1, L0_ffn_b1, L0_ffn_Wo, L0_ffn_bo, L0_ffn_ln_gamma, L0_ffn_ln_beta):
    import numpy as np
    import concourse.bacc as bacc
    from concourse.bass_utils import run_bass_kernel_spmd

    ins = {
        "x": x, "ctx": ctx_512, "itok": itok_BxS2xS_0_7, "w_qkv": L0_attn_qkv_kernel, "b_qkv": L0_attn_qkv_bias,
        "p_in": np.transpose(np.asarray(L0_xattn_proj_in), (2, 0, 1)).reshape(D, E1 * I1),
        "p_out": np.transpose(np.asarray(L0_xattn_proj_out), (0, 2, 1)).reshape(E1 * I1, D),
        "w_router": np.transpose(np.asarray(L0_ffn_W_router)),
        "w_1": np.asarray(L0_ffn_W1).reshape(E2 * D, I2), "b_1": L0_ffn_b1, "w_o": L0_ffn_Wo, "b_o": L0_ffn_bo,
        "gamma": L0_ffn_ln_gamma, "beta": L0_ffn_ln_beta,
    }
    nc = bacc.Bacc("TRN2", target_bir_lowering=False, num_devices=1, dynamic_dma_scratch_size=1024)
    arrays, args = {}, {}
    for name, a in ins.items():
        a = np.ascontiguousarray(a)
        arrays[f"in_{name}"] = a
        args[name] = nc.dram_tensor(f"in_{name}", a.shape, mybir.dt.from_np(a.dtype), kind="ExternalInput").ap()
    out = nc.dram_tensor("out", tuple(np.shape(x)), F32, kind="ExternalOutput").ap()
    decoder_layer(nc, *[args[n] for n in ins], out)
    r = run_bass_kernel_spmd(nc, [arrays], core_ids=[0])
    return r.results[0]["out"]
```
